# Optimizing a Trainium2 kernel written in Bass

```python
import numpy as np
import jax
import jax.numpy as jnp

def _softmax(x, axis=-1):
    return jax.nn.softmax(x, axis=axis)

def _gelu(x):
    return jax.nn.gelu(x, approximate=True)

def _silu(x):
    return jax.nn.silu(x)

def _sigmoid(x):
    return jax.nn.sigmoid(x)

def _layernorm(x, axis=-1, eps=1e-05):
    m = jnp.mean(x, axis=axis, keepdims=True)
    v = jnp.var(x, axis=axis, keepdims=True)
    return (x - m) / jnp.sqrt(v + eps)

def _scatter_add(tgt, idx, src, axis=0):
    return tgt.at[idx].add(src)

def _segment_sum(src, seg, n):
    return jax.ops.segment_sum(src, seg, n)
kernel_name = 'mk_seq_postln_d2_jaxref_r8_38eb13'

def setup_inputs(seed: int=0):
    np.random.seed(seed)
    _w = jnp.asarray

    def _L0_attn_setup():
        import jax, jax.numpy as jnp
        import numpy as np
        H = 32
        HKV = 8
        D = 512
        HD = D // H
        S = 128
        MASK_OUT = 0.9
        MIN_REMAIN = 128
        THETA = 10000.0

        def rope_tables(seq_len, hd):
            inv_freq = 1.0 / THETA ** (jnp.arange(0, hd, 2, dtype=jnp.float32) / hd)
            t = jnp.arange(seq_len, dtype=jnp.float32)
            freqs = jnp.outer(t, inv_freq)
            emb = jnp.concatenate([freqs, freqs], axis=-1)
            return (jnp.cos(emb), jnp.sin(emb))

        def rotate_half(x):
            x1, x2 = jnp.split(x, 2, axis=-1)
            return jnp.concatenate([-x2, x1], axis=-1)

        def apply_rope(x, cos, sin):
            return x * cos + rotate_half(x) * sin
        key = jax.random.key(seed)
        k0, k1, k2, k3, k4 = jax.random.split(key, 5)
        hidden_states = jax.random.normal(k0, (1, S, D), jnp.float32)
        Wq = jax.random.normal(k1, (D, D), jnp.float32) * 0.02
        Wk = jax.random.normal(k2, (HKV * HD, D), jnp.float32) * 0.02
        Wv = jax.random.normal(k3, (HKV * HD, D), jnp.float32) * 0.02
        Wo = jax.random.normal(k4, (D, D), jnp.float32) * 0.02
        return {'hidden_states': hidden_states, 'Wq': Wq, 'Wk': Wk, 'Wv': Wv, 'Wo': Wo}
    _L0_attn_in = _L0_attn_setup()

    def _L0_ffn_setup():
        import jax, jax.numpy as jnp
        import numpy as np
        HIDDEN = 512
        INTER = 1376
        GROUP = 128
        B, S = (4, 256)
        NIB = jnp.uint32(15)

        def _pack_rows(nib):
            r = nib.reshape(-1, 8, nib.shape[-1])
            shifts = (jnp.arange(8, dtype=jnp.uint32) * 4)[None, :, None]
            return jnp.sum(r << shifts, axis=1, dtype=jnp.uint32)

        def _pack_cols(nib):
            r = nib.reshape(nib.shape[0], -1, 8)
            shifts = (jnp.arange(8, dtype=jnp.uint32) * 4)[None, None, :]
            return jnp.sum(r << shifts, axis=2, dtype=jnp.uint32)

        def _dequant(qw, qz, sc, g_idx):
            shifts = jnp.arange(8, dtype=jnp.uint32) * 4
            wq = qw[:, None, :] >> shifts[None, :, None] & NIB
            wq = wq.reshape(-1, qw.shape[1]).astype(jnp.float32)
            zq = qz[:, :, None] >> shifts[None, None, :] & NIB
            zq = zq.reshape(qz.shape[0], -1).astype(jnp.float32) + 1.0
            return sc[g_idx] * (wq - zq[g_idx])
        key = jax.random.key(seed)
        ks = jax.random.split(key, 7)
        n_groups = HIDDEN // GROUP
        n_groups_d = INTER // GROUP
        x = jax.random.normal(ks[0], (B, S, HIDDEN), jnp.float32)
        nib_w_gu = jax.random.randint(ks[1], (HIDDEN, 2 * INTER), 0, 16).astype(jnp.uint32)
        nib_z_gu = jax.random.randint(ks[2], (n_groups, 2 * INTER), 0, 15).astype(jnp.uint32)
        qweight_gu = _pack_rows(nib_w_gu)
        qzeros_gu = _pack_cols(nib_z_gu)
        scales_gu = jax.random.uniform(ks[3], (n_groups, 2 * INTER), jnp.float32, 0.005, 0.02)
        g_idx_gu = jnp.arange(HIDDEN, dtype=jnp.int32) // GROUP
        nib_w_d = jax.random.randint(ks[4], (INTER, HIDDEN), 0, 16).astype(jnp.uint32)
        nib_z_d = jax.random.randint(ks[5], (n_groups_d, HIDDEN), 0, 15).astype(jnp.uint32)
        qweight_down = _pack_rows(nib_w_d)
        qzeros_down = _pack_cols(nib_z_d)
        scales_down = jax.random.uniform(ks[6], (n_groups_d, HIDDEN), jnp.float32, 0.005, 0.02)
        g_idx_down = jnp.arange(INTER, dtype=jnp.int32) // GROUP
        return {'x': x, 'qweight_gu': qweight_gu, 'qzeros_gu': qzeros_gu, 'scales_gu': scales_gu, 'g_idx_gu': g_idx_gu, 'qweight_down': qweight_down, 'qzeros_down': qzeros_down, 'scales_down': scales_down, 'g_idx_down': g_idx_down}
    _L0_ffn_in = _L0_ffn_setup()

    def _L1_attn_setup():
        import jax, jax.numpy as jnp
        import numpy as np
        D_MODEL = 512
        N_Q = 32
        N_KV = 8
        HD = 128
        SLIDE = 64

        def _gqa_swa_attention(q, k, v, slide):
            B, Hq, N, D = q.shape
            Hkv = k.shape[1]
            G = Hq // Hkv
            qg = q.reshape(B, Hkv, G, N, D)
            scale = 1.0 / jnp.sqrt(jnp.asarray(D, q.dtype))
            s = jnp.einsum('bhgnd,bhmd->bhgnm', qg, k) * scale
            i = jnp.arange(N)[:, None]
            j = jnp.arange(N)[None, :]
            mask = j <= i
            if slide > 0:
                mask = mask & (i - j < slide)
            s = jnp.where(mask[None, None, None], s, jnp.asarray(-jnp.inf, s.dtype))
            p = jax.nn.softmax(s, axis=-1)
            o = jnp.einsum('bhgnm,bhmd->bhgnd', p, v)
            return o.reshape(B, Hq, N, D)
        key = jax.random.key(seed)
        ks = jax.random.split(key, 5)
        std = 0.01
        x = jax.random.normal(ks[0], (2, 256, D_MODEL), dtype=jnp.float32)
        wq = jax.random.normal(ks[1], (N_Q * HD, D_MODEL), dtype=jnp.float32) * std
        wk = jax.random.normal(ks[2], (N_KV * HD, D_MODEL), dtype=jnp.float32) * std
        wv = jax.random.normal(ks[3], (N_KV * HD, D_MODEL), dtype=jnp.float32) * std
        wo = jax.random.normal(ks[4], (D_MODEL, N_Q * HD), dtype=jnp.float32) * std
        return {'x': x, 'wq': wq, 'wk': wk, 'wv': wv, 'wo': wo}
    _L1_attn_in = _L1_attn_setup()

    def _L1_ffn_setup():
        import jax, jax.numpy as jnp
        import numpy as np
        NUM_EXPERTS = 4
        HIDDEN = 512
        RANK = 8
        ALPHA = 8.0
        SCALE = ALPHA / RANK
        key = jax.random.key(seed)
        ks = jax.random.split(key, 6)
        B, T, H, E, R = (4, 512, HIDDEN, NUM_EXPERTS, RANK)
        x = jax.random.normal(ks[0], (B, T, H), dtype=jnp.float32)
        W_up = jax.random.normal(ks[1], (H, H), dtype=jnp.float32) / np.sqrt(H)
        gate_w = jax.random.normal(ks[2], (E, H), dtype=jnp.float32) / np.sqrt(H)
        expert_bias = jnp.zeros((E,), dtype=jnp.float32)
        lora_A = jax.random.normal(ks[3], (E, R, H), dtype=jnp.float32) / np.sqrt(H)
        lora_B = jax.random.normal(ks[4], (E, H, R), dtype=jnp.float32) * 0.01
        return {'x': x, 'W_up': W_up, 'gate_w': gate_w, 'expert_bias': expert_bias, 'lora_A': lora_A, 'lora_B': lora_B}
    _L1_ffn_in = _L1_ffn_setup()
    _d = {'L0_attn_hidden_states': _L0_attn_in['hidden_states'], 'L0_attn_Wq': _L0_attn_in['Wq'], 'L0_attn_Wk': _L0_attn_in['Wk'], 'L0_attn_Wv': _L0_attn_in['Wv'], 'L0_attn_Wo': _L0_attn_in['Wo'], 'L0_ffn_qweight_gu': _L0_ffn_in['qweight_gu'], 'L0_ffn_qzeros_gu': _L0_ffn_in['qzeros_gu'], 'L0_ffn_scales_gu': _L0_ffn_in['scales_gu'], 'L0_ffn_g_idx_gu': _L0_ffn_in['g_idx_gu'], 'L0_ffn_qweight_down': _L0_ffn_in['qweight_down'], 'L0_ffn_qzeros_down': _L0_ffn_in['qzeros_down'], 'L0_ffn_scales_down': _L0_ffn_in['scales_down'], 'L0_ffn_g_idx_down': _L0_ffn_in['g_idx_down'], 'L1_attn_wq': _L1_attn_in['wq'], 'L1_attn_wk': _L1_attn_in['wk'], 'L1_attn_wv': _L1_attn_in['wv'], 'L1_attn_wo': _L1_attn_in['wo'], 'L1_ffn_W_up': _L1_ffn_in['W_up'], 'L1_ffn_gate_w': _L1_ffn_in['gate_w'], 'L1_ffn_expert_bias': _L1_ffn_in['expert_bias'], 'L1_ffn_lora_A': _L1_ffn_in['lora_A'], 'L1_ffn_lora_B': _L1_ffn_in['lora_B']}
    _x0 = _d['L0_attn_hidden_states']
    _d['L0_attn_hidden_states'] = jax.random.normal(jax.random.fold_in(jax.random.key(seed), 1), (4, 512, 512), dtype=_x0.dtype)
    del _x0
    return _d

def reference(L0_attn_hidden_states, L0_attn_Wq, L0_attn_Wk, L0_attn_Wv, L0_attn_Wo, L0_ffn_qweight_gu, L0_ffn_qzeros_gu, L0_ffn_scales_gu, L0_ffn_g_idx_gu, L0_ffn_qweight_down, L0_ffn_qzeros_down, L0_ffn_scales_down, L0_ffn_g_idx_down, L1_attn_wq, L1_attn_wk, L1_attn_wv, L1_attn_wo, L1_ffn_W_up, L1_ffn_gate_w, L1_ffn_expert_bias, L1_ffn_lora_A, L1_ffn_lora_B):

    def _L0_attn_ref(hidden_states, Wq, Wk, Wv, Wo):
        import jax, jax.numpy as jnp
        import numpy as np
        H = 32
        HKV = 8
        D = 512
        HD = D // H
        S = 128
        MASK_OUT = 0.9
        MIN_REMAIN = 128
        THETA = 10000.0

        def rope_tables(seq_len, hd):
            inv_freq = 1.0 / THETA ** (jnp.arange(0, hd, 2, dtype=jnp.float32) / hd)
            t = jnp.arange(seq_len, dtype=jnp.float32)
            freqs = jnp.outer(t, inv_freq)
            emb = jnp.concatenate([freqs, freqs], axis=-1)
            return (jnp.cos(emb), jnp.sin(emb))

        def rotate_half(x):
            x1, x2 = jnp.split(x, 2, axis=-1)
            return jnp.concatenate([-x2, x1], axis=-1)

        def apply_rope(x, cos, sin):
            return x * cos + rotate_half(x) * sin
        B, Sq, Dm = hidden_states.shape
        dtype = hidden_states.dtype
        neg = jnp.finfo(dtype).min
        q = (hidden_states @ Wq.T).reshape(B, Sq, H, HD).transpose(0, 2, 1, 3)
        k = (hidden_states @ Wk.T).reshape(B, Sq, HKV, HD).transpose(0, 2, 1, 3)
        v = (hidden_states @ Wv.T).reshape(B, Sq, HKV, HD).transpose(0, 2, 1, 3)
        rep = H // HKV
        k = jnp.repeat(k, rep, axis=1)
        v = jnp.repeat(v, rep, axis=1)
        cos, sin = rope_tables(Sq, HD)
        qr = apply_rope(q, cos, sin)
        kr = apply_rope(k, cos, sin)
        draft = jnp.einsum('bhqd,bhkd->bhqk', qr, kr)
        qi = jnp.arange(Sq)
        ki = jnp.arange(Sq)
        causal_future = qi[:, None] < ki[None, :]
        draft = draft + jnp.where(causal_future, neg, jnp.asarray(0.0, dtype))
        num_remain = max(min(Sq, MIN_REMAIN), Sq - int(Sq * MASK_OUT))
        _, draft_indices = jax.lax.top_k(draft, num_remain)
        mask = jnp.full((B, H, Sq, Sq), neg, dtype)
        b_idx = jnp.arange(B)[:, None, None, None]
        h_idx = jnp.arange(H)[None, :, None, None]
        s_idx = jnp.arange(Sq)[None, None, :, None]
        mask = mask.at[b_idx, h_idx, s_idx, draft_indices].set(0.0)
        mask = jnp.where(causal_future[None, None, :, :], neg, mask)
        scores = jnp.einsum('bhqd,bhkd->bhqk', qr, kr) / np.sqrt(HD).astype(np.float32) + mask
        attn = jax.nn.softmax(scores, axis=-1)
        out = jnp.einsum('bhqk,bhkd->bhqd', attn, v)
        out = out.transpose(0, 2, 1, 3).reshape(B, Sq, Dm)
        return out @ Wo.T

    def _L0_ffn_ref(x, qweight_gu, qzeros_gu, scales_gu, g_idx_gu, qweight_down, qzeros_down, scales_down, g_idx_down):
        import jax, jax.numpy as jnp
        import numpy as np
        HIDDEN = 512
        INTER = 1376
        GROUP = 128
        B, S = (4, 256)
        NIB = jnp.uint32(15)

        def _pack_rows(nib):
            r = nib.reshape(-1, 8, nib.shape[-1])
            shifts = (jnp.arange(8, dtype=jnp.uint32) * 4)[None, :, None]
            return jnp.sum(r << shifts, axis=1, dtype=jnp.uint32)

        def _pack_cols(nib):
            r = nib.reshape(nib.shape[0], -1, 8)
            shifts = (jnp.arange(8, dtype=jnp.uint32) * 4)[None, None, :]
            return jnp.sum(r << shifts, axis=2, dtype=jnp.uint32)

        def _dequant(qw, qz, sc, g_idx):
            shifts = jnp.arange(8, dtype=jnp.uint32) * 4
            wq = qw[:, None, :] >> shifts[None, :, None] & NIB
            wq = wq.reshape(-1, qw.shape[1]).astype(jnp.float32)
            zq = qz[:, :, None] >> shifts[None, None, :] & NIB
            zq = zq.reshape(qz.shape[0], -1).astype(jnp.float32) + 1.0
            return sc[g_idx] * (wq - zq[g_idx])
        w_gu = _dequant(qweight_gu, qzeros_gu, scales_gu, g_idx_gu)
        inter = jnp.einsum('bsh,hf->bsf', x, w_gu)
        gate, up = (inter[..., :INTER], inter[..., INTER:])
        h = jax.nn.silu(gate) * up
        w_d = _dequant(qweight_down, qzeros_down, scales_down, g_idx_down)
        return jnp.einsum('bsf,fh->bsh', h, w_d)

    def _L1_attn_ref(x, wq, wk, wv, wo):
        import jax, jax.numpy as jnp
        import numpy as np
        D_MODEL = 512
        N_Q = 32
        N_KV = 8
        HD = 128
        SLIDE = 64

        def _gqa_swa_attention(q, k, v, slide):
            B, Hq, N, D = q.shape
            Hkv = k.shape[1]
            G = Hq // Hkv
            qg = q.reshape(B, Hkv, G, N, D)
            scale = 1.0 / jnp.sqrt(jnp.asarray(D, q.dtype))
            s = jnp.einsum('bhgnd,bhmd->bhgnm', qg, k) * scale
            i = jnp.arange(N)[:, None]
            j = jnp.arange(N)[None, :]
            mask = j <= i
            if slide > 0:
                mask = mask & (i - j < slide)
            s = jnp.where(mask[None, None, None], s, jnp.asarray(-jnp.inf, s.dtype))
            p = jax.nn.softmax(s, axis=-1)
            o = jnp.einsum('bhgnm,bhmd->bhgnd', p, v)
            return o.reshape(B, Hq, N, D)
        B, N, _ = x.shape
        q = (x @ wq.T).reshape(B, N, N_Q, HD).transpose(0, 2, 1, 3)
        k = (x @ wk.T).reshape(B, N, N_KV, HD).transpose(0, 2, 1, 3)
        v = (x @ wv.T).reshape(B, N, N_KV, HD).transpose(0, 2, 1, 3)
        o = _gqa_swa_attention(q, k, v, SLIDE)
        o = o.transpose(0, 2, 1, 3).reshape(B, N, N_Q * HD)
        return o @ wo.T

    def _L1_ffn_ref(x, W_up, gate_w, expert_bias, lora_A, lora_B):
        import jax, jax.numpy as jnp
        import numpy as np
        NUM_EXPERTS = 4
        HIDDEN = 512
        RANK = 8
        ALPHA = 8.0
        SCALE = ALPHA / RANK
        B, T, H = x.shape
        E = gate_w.shape[0]
        x_flat = x.reshape(-1, H)
        logits = x_flat @ gate_w.T + expert_bias
        top1 = jnp.argmax(logits, axis=-1)
        one_hot = jax.nn.one_hot(top1, E, dtype=x_flat.dtype)
        base_out = jnp.einsum('bth,oh->bto', x, W_up)
        z = jnp.einsum('nh,erh->ner', x_flat, lora_A)
        d = jnp.einsum('ner,ehr->neh', z, lora_B) * SCALE
        delta = jnp.einsum('neh,ne->nh', d, one_hot)
        return base_out + delta.reshape(B, T, H)
    x = L0_attn_hidden_states
    x = _layernorm(x + _L0_attn_ref(x, L0_attn_Wq, L0_attn_Wk, L0_attn_Wv, L0_attn_Wo), axis=-1)
    x = _layernorm(x + _L0_ffn_ref(x, L0_ffn_qweight_gu, L0_ffn_qzeros_gu, L0_ffn_scales_gu, L0_ffn_g_idx_gu, L0_ffn_qweight_down, L0_ffn_qzeros_down, L0_ffn_scales_down, L0_ffn_g_idx_down), axis=-1)
    x = _layernorm(x + _L1_attn_ref(x, L1_attn_wq, L1_attn_wk, L1_attn_wv, L1_attn_wo), axis=-1)
    x = _layernorm(x + _L1_ffn_ref(x, L1_ffn_W_up, L1_ffn_gate_w, L1_ffn_expert_bias, L1_ffn_lora_A, L1_ffn_lora_B), axis=-1)
    return x

_drawn_inputs = setup_inputs


def setup_inputs(seed=0):
    import zlib

    import numpy as np

    out = dict(_drawn_inputs(seed))
    spreads = {'L1_ffn_expert_bias': (0.0, 0.8)}
    factors = {'L0_attn_Wq': 2.857,
     'L0_attn_Wk': 2.815,
     'L1_attn_wq': 8.0,
     'L1_attn_wk': 8.0,
     'L1_ffn_gate_w': 3.235,
     'L1_ffn_lora_A': 2.814,
     'L1_ffn_lora_B': 2.784}
    for name, (base, spread) in spreads.items():
        noise = np.random.default_rng([zlib.crc32(name.encode()), seed]).standard_normal(out[name].shape)
        drawn = base * np.exp(spread * noise) if base else spread * noise
        out[name] = jnp.asarray(drawn.astype(out[name].dtype))
    for name, factor in factors.items():
        out[name] = (out[name] * factor).astype(out[name].dtype)
    return out
```

```python
from contextlib import ExitStack

import concourse.bass as bass
from concourse import mybir

ALU = mybir.AluOpType
ACT = mybir.ActivationFunctionType
AX = mybir.AxisListType
F32 = mybir.dt.float32
BF16 = mybir.dt.bfloat16
U32 = mybir.dt.uint32
I32 = mybir.dt.int32

P = 128
D = 512
KC = D // P
NB = 4
S = 512
TT = S // P
EPS = 1e-5

H0 = 32
G0 = 8
HD0 = D // H0
R0 = H0 // G0
KV0 = G0 * HD0
KEEP = 128
TOP = 8
NEG = -3.0e38

INTER = 1376
FT = (INTER + P - 1) // P
GU_GROUPS = 4
DN_GROUPS = 10
PACK = 8

H1 = 32
G1 = 8
R1 = H1 // G1
HD1 = 128
WIN = 64
NW = S // WIN
W1 = (R1 + 2) * HD1

E1 = 4
RK = 8


def rows_of(f):
    return min(P, INTER - f * P)


def after(k, unit=1):
    return unit * k + 1


class Place:

    def __init__(self, nc, ctx, prefix):
        self.nc, self.ctx, self.prefix = nc, ctx, prefix
        self.owned = []
        ctx.callback(self.release)

    def release(self):
        if self.owned:
            self.nc.clear_and_free_semaphores(self.owned)
            self.nc.all_engine_barrier()

    def sbuf(self, name, shape, dtype=F32):
        return self.ctx.enter_context(self.nc.sbuf_tensor(self.prefix + name, shape, dtype))

    def psum(self, name, shape, dtype=F32):
        return self.ctx.enter_context(self.nc.psum_tensor(self.prefix + name, shape, dtype))

    def sem(self, name):
        s = self.nc.alloc_semaphore(self.prefix + name)
        self.owned.append(s)
        return s

    def sems(self, name, n=2):
        return [self.sem(f"{name}{i}") for i in range(n)]


def bcast(ap, axis, n):
    v = ap.unsqueeze(axis)
    shape = list(v.shape)
    shape[axis] = n
    return v.broadcast_to(shape)


def wait_apart(eng, sem, value, passed):
    eng.wait_ge(sem, value)
    eng.sem_inc(passed, 1)


def start_at_one(eng, *groups):
    for g in groups:
        for s in (g if isinstance(g, list) else [g]):
            eng.sem_inc(s, 1)




def dequantise(nc, a, w_gu, w_dn, space):
    CH = 512
    with ExitStack() as ctx:
        m = Place(nc, ctx, "dq_")
        words = space.bitcast(U32)[:, 0:4 * INTER].rearrange("p (s n) -> p s n", s=2)
        shift = m.sbuf("shift", [P, 1], U32)
        iota = m.sbuf("iota", [16, 1])
        gidx_i = m.sbuf("gidx_i", [16, D + INTER], I32)
        gidx = m.sbuf("gidx", [16, D + INTER])
        wrap = m.sbuf("wrap", [16, D + INTER])
        onehot = m.sbuf("onehot", [16, D + INTER])
        scale_gu = m.sbuf("scale_gu", [GU_GROUPS, 2 * INTER])
        scale_dn = m.sbuf("scale_dn", [DN_GROUPS, D])
        zw_gu = m.sbuf("zw_gu", [GU_GROUPS, 2 * INTER // PACK], U32)
        zw_dn = m.sbuf("zw_dn", [DN_GROUPS, D // PACK], U32)
        zi_gu = m.sbuf("zi_gu", [GU_GROUPS, 2 * INTER], U32)
        zi_dn = m.sbuf("zi_dn", [DN_GROUPS, D], U32)
        zero_gu = m.sbuf("zero_gu", [GU_GROUPS, 2 * INTER])
        zero_dn = m.sbuf("zero_dn", [DN_GROUPS, D])
        centred = m.sbuf("centred", [P, 2, CH])
        ps_scale = m.psum("ps_scale", [P, 2, CH])
        ps_zero = m.psum("ps_zero", [P, 2, CH])
        small_in = m.sem("small_in")
        words_in = m.sems("words_in")
        unpacked = m.sem("unpacked")
        prepared = m.sem("prepared")
        spread = m.sem("spread")
        centre_done = m.sem("centre_done")
        piece_done = m.sem("piece_done")

        chunks = [("gu", k, P) for k in range(KC)] + [("dn", f, rows_of(f)) for f in range(FT)]
        pieces = []
        for c, (kind, k, rows) in enumerate(chunks):
            width = 2 * INTER if kind == "gu" else D
            pieces += [(c, j, min(CH, width - j)) for j in range(0, width, CH)]

        block = ctx.enter_context(nc.Block())

        @block.sync
        def _(sp):
            sp.dma_start(gidx_i[0:GU_GROUPS, 0:D], a["g_idx_gu"].partition_broadcast(GU_GROUPS)).then_inc(small_in, 16)
            sp.dma_start(gidx_i[0:DN_GROUPS, D:], a["g_idx_dn"].partition_broadcast(DN_GROUPS)).then_inc(small_in, 16)
            for dst, src in ((shift, "shift"), (iota, "iota"), (scale_gu, "scales_gu"), (scale_dn, "scales_dn"),
                             (zw_gu, "qzeros_gu"), (zw_dn, "qzeros_dn")):
                sp.dma_start(dst[:], a[src]).then_inc(small_in, 16)
            for c, (kind, k, rows) in enumerate(chunks):
                if c >= 2:
                    sp.wait_ge(piece_done, max(n + 1 for n, p in enumerate(pieces) if p[0] == c - 2))
                width = 2 * INTER if kind == "gu" else D
                src = a["qw_gu"] if kind == "gu" else a["qw_dn"]
                sp.dma_start(words[0:rows, c % 2, 0:width], src[k * P:k * P + rows, :]).then_inc(words_in[c % 2], 16)

        @block.vector
        def _(dve):
            steps = [0]

            def step(ins):
                steps[0] += 1
                ins.then_inc(prepared, 1)

            def settle():
                dve.wait_ge(prepared, steps[0])

            dve.wait_ge(small_in, 16 * 8)
            for rows, cols, n in ((GU_GROUPS, slice(0, D), GU_GROUPS), (DN_GROUPS, slice(D, D + INTER), DN_GROUPS)):
                g, h, w = gidx[0:rows, cols], onehot[0:rows, cols], wrap[0:rows, cols]
                step(nc.vector.tensor_copy(g, gidx_i[0:rows, cols]))
                settle()
                step(nc.vector.tensor_scalar(w, g, 0.0, float(n), ALU.is_lt, ALU.mult))
                settle()
                step(nc.vector.tensor_tensor(g, g, w, ALU.add))
                settle()
                step(nc.vector.tensor_scalar(g, g, 0.0, float(n - 1), ALU.max, ALU.min))
                settle()
                step(nc.vector.tensor_scalar(h, g, iota[0:rows, 0:1], None, ALU.is_equal))
            for zw, zi, zero in ((zw_gu, zi_gu, zero_gu), (zw_dn, zi_dn, zero_dn)):
                v = zi[:].rearrange("p (c s) -> p c s", s=PACK)
                for s in range(PACK):
                    step(nc.vector.tensor_scalar(v[:, :, s], zw[:], 4 * s, 15,
                                                 ALU.logical_shift_right, ALU.bitwise_and))
                settle()
                step(nc.vector.tensor_scalar(zero[:], zi[:], 1.0, None, ALU.add))

            n = 0
            for c, (kind, k, rows) in enumerate(chunks):
                width = 2 * INTER if kind == "gu" else D
                dve.wait_ge(words_in[c % 2], 16 * (c // 2 + 1))
                u = words[0:rows, c % 2, 0:width]
                nc.vector.tensor_scalar(u, u, shift[0:rows, 0:1], 15, ALU.logical_shift_right,
                                        ALU.bitwise_and).then_inc(unpacked, 1)
                dve.wait_ge(unpacked, c + 1)
                while n < len(pieces) and pieces[n][0] == c:
                    _, j, w = pieces[n]
                    dst = w_gu[0:rows, k, j:j + w] if kind == "gu" else w_dn[0:rows, k, j:j + w]
                    dve.wait_ge(spread, n + 1)
                    nc.vector.tensor_tensor(centred[0:rows, n % 2, 0:w], words[0:rows, c % 2, j:j + w],
                                            ps_zero[0:rows, n % 2, 0:w], ALU.subtract).then_inc(centre_done, 1)
                    dve.wait_ge(centre_done, n + 1)
                    nc.vector.tensor_tensor(dst, centred[0:rows, n % 2, 0:w], ps_scale[0:rows, n % 2, 0:w],
                                            ALU.mult).then_inc(piece_done, 1)
                    n += 1

        @block.tensor
        def _(pe):
            pe.wait_ge(prepared, 2 * 5 + 2 * (PACK + 1))
            for n, (c, j, w) in enumerate(pieces):
                kind, k, rows = chunks[c]
                if n >= 2:
                    pe.wait_ge(piece_done, n - 1)
                if kind == "gu":
                    hot, sc, ze = onehot[0:GU_GROUPS, k * P:k * P + rows], scale_gu, zero_gu
                else:
                    hot, sc, ze = onehot[0:DN_GROUPS, D + k * P:D + k * P + rows], scale_dn, zero_dn
                nc.tensor.matmul(ps_scale[0:rows, n % 2, 0:w], hot, sc[:, j:j + w], start=True, stop=True)
                nc.tensor.matmul(ps_zero[0:rows, n % 2, 0:w], hot, ze[:, j:j + w], start=True,
                                 stop=True).then_inc(spread, 1)




def project_layer0(nc, a, ident, v_all, qT_dram, kT_dram):
    W = D + 2 * KV0
    with ExitStack() as ctx:
        m = Place(nc, ctx, "p0_")
        w = m.sbuf("w", [P, KC, W])
        rope = m.sbuf("rope", [P, TT, 4, HD0])
        xT = m.sbuf("xT", [P, 2, KC, P])
        cosed = m.sbuf("cosed", [P, 2, D + KV0])
        sined = m.sbuf("sined", [P, 2, D + KV0])
        roped = m.sbuf("roped", [P, 2, D + KV0])
        turned = m.sbuf("turned", [P, 2, KC + 1, P])
        ps_q = m.psum("ps_q", [P, 2, D])
        ps_kv = m.psum("ps_kv", [P, 2, 512])
        ps_t = m.psum("ps_t", [P, 2, 1024])
        weights_in = m.sem("weights_in")
        x_in = m.sems("x_in")
        projected = m.sems("projected")
        rotated = m.sems("rotated")
        summed = m.sems("summed")
        transposed = m.sems("transposed")
        evacuated = m.sems("evacuated")
        stored = m.sems("stored")

        block = ctx.enter_context(nc.Block())

        @block.sync
        def _(sp):
            for k in range(KC):
                sp.dma_start(w[:, k, :], a["wqkvT"][k * P:(k + 1) * P, :]).then_inc(weights_in, 16)
            sp.dma_start(rope[:], a["rope"]).then_inc(weights_in, 16)
            src = a["xT"].rearrange("(k p) (b t c) -> p k b t c", p=P, b=NB, t=TT)
            with sp.Fori(0, NB) as b:
                for t in range(TT):
                    sp.wait_ge(projected[t % 2], after(b * 2 + t // 2))
                    sp.dma_start(xT[:, t % 2, :, :], src[:, :, b, t, :]).then_inc(x_in[t % 2], 16)

        @block.tensor
        def _(pe):
            start_at_one(pe, projected, transposed)
            pe.wait_ge(weights_in, 16 * (KC + 1))

            def project(b, t):
                s, k2 = t % 2, b * 2 + t // 2
                pe.wait_ge(x_in[s], 16 * (k2 + 1))
                pe.wait_ge(rotated[s], after(k2))
                for k in range(KC):
                    nc.tensor.matmul(ps_q[:, s, :], xT[:, s, k, :], w[:, k, 0:D], start=(k == 0), stop=(k == KC - 1))
                for k in range(KC):
                    last = nc.tensor.matmul(ps_kv[:, s, 0:2 * KV0], xT[:, s, k, :], w[:, k, D:W],
                                            start=(k == 0), stop=(k == KC - 1))
                last.then_inc(projected[s], 1)

            def transpose(b, t):
                s, k2 = t % 2, b * 2 + t // 2
                pe.wait_ge(summed[s], after(k2 + 1))
                pe.wait_ge(evacuated[s], after(k2))
                for c in range(KC + 1):
                    last = nc.tensor.transpose(ps_t[:, s, c * P:(c + 1) * P], roped[:, s, c * P:(c + 1) * P], ident[:])
                last.then_inc(transposed[s], 1)

            with pe.Fori(0, NB) as b:
                for t in range(TT + 1):
                    if t < TT:
                        project(b, t)
                    if t >= 1:
                        transpose(b, t - 1)

        @block.vector
        def _(dve):
            start_at_one(dve, rotated)
            dve.wait_ge(weights_in, 16 * (KC + 1))
            half = HD0 // 2
            with dve.Fori(0, NB) as b:
                for t in range(TT):
                    s, k2 = t % 2, b * 2 + t // 2
                    dve.wait_ge(projected[s], after(k2 + 1))
                    dve.wait_ge(summed[s], after(k2))
                    for src, lo, heads, cos in ((ps_q[:, s, :], 0, H0, 0), (ps_kv[:, s, 0:KV0], D, G0, 2)):
                        width = heads * HD0
                        x = src.rearrange("p (h d) -> p h d", d=HD0)
                        c_out = cosed[:, s, lo:lo + width].rearrange("p (h d) -> p h d", d=HD0)
                        s_out = sined[:, s, lo:lo + width].rearrange("p (h d) -> p h d", d=HD0)
                        nc.vector.tensor_tensor(c_out, x, bcast(rope[:, t, cos, :], 1, heads), ALU.mult)
                        nc.vector.tensor_tensor(s_out[:, :, 0:half], x[:, :, half:],
                                                bcast(rope[:, t, cos + 1, 0:half], 1, heads), ALU.mult)
                        last = nc.vector.tensor_tensor(s_out[:, :, half:], x[:, :, 0:half],
                                                       bcast(rope[:, t, cos + 1, half:], 1, heads), ALU.mult)
                    last = nc.vector.tensor_copy(v_all[:, b, :, t, :], ps_kv[:, s, KV0:2 * KV0]
                                                 .rearrange("p (g d) -> p g d", d=HD0))
                    last.then_inc(rotated[s], 1)

        @block.gpsimd
        def _(pool):
            start_at_one(pool, summed)
            with pool.Fori(0, NB) as b:
                for t in range(TT):
                    s, k2 = t % 2, b * 2 + t // 2
                    pool.wait_ge(rotated[s], after(k2 + 1))
                    pool.wait_ge(transposed[s], after(k2))
                    nc.gpsimd.tensor_tensor(roped[:, s, :], cosed[:, s, :], sined[:, s, :], ALU.add)\
                        .then_inc(summed[s], 1)

        @block.scalar
        def _(act):
            start_at_one(act, evacuated, stored)

            def evacuate(b, t):
                s, k2 = t % 2, b * 2 + t // 2
                act.wait_ge(transposed[s], after(k2 + 1))
                act.wait_ge(stored[s], after(k2, 32))
                nc.scalar.activation(turned[:, s, :, :], ps_t[:, s, 0:(KC + 1) * P]
                                     .rearrange("p (k c) -> p k c", c=P), ACT.Copy).then_inc(evacuated[s], 1)
                act.wait_ge(evacuated[s], after(k2 + 1))
                dst = qT_dram.rearrange("(b k p) (t c) -> b t p k c", b=NB, k=KC, t=TT)
                act.dma_start(dst[b, t], turned[:, s, 0:KC, :]).then_inc(stored[s], 16)
                dst = kT_dram.rearrange("(b p) (t c) -> b t p c", b=NB, t=TT)
                act.dma_start(dst[b, t], turned[:, s, KC, :]).then_inc(stored[s], 16)

            with act.Fori(0, NB) as b:
                for t in range(TT):
                    evacuate(b, t)
            for s in range(2):
                act.wait_ge(stored[s], after(NB * 2, 32))




def attend_layer0(nc, a, ident, ident16, v_all, qT_dram, kT_dram, o_all, work):
    PAIRS = NB * G0
    UNITS = 2 * TT
    TURNS = PAIRS // 2
    CHUNKS = TT * (TT + 1) // 2
    ROUNDS = KEEP // TOP
    with ExitStack() as ctx:
        m = Place(nc, ctx, "a0_")
        qT = m.sbuf("qT", [P, 2, S])
        kT = m.sbuf("kT", [P, 2, S])
        mask32 = m.sbuf("mask32", [P, P])
        mask = m.sbuf("mask", [P, P], BF16)
        exps = work[:, 0]
        rest = work[:, 1]
        top = m.sbuf("top", [P, R0, TOP])
        nmax = m.sbuf("nmax", [P, 2, R0])
        rsum = m.sbuf("rsum", [P, 2, R0])
        rinv = m.sbuf("rinv", [P, 2, R0])
        pT = m.sbuf("pT", [P, 2, R0 * P])
        ps_s = m.psum("ps_s", [P, R0, S])
        ps_t = m.psum("ps_t", [P, 2, R0 * P])
        ps_o = m.psum("ps_o", [P, 2, 512])
        mask_in = m.sem("mask_in")
        mask_ready = m.sem("mask_ready")
        heads_in = m.sems("heads_in")
        scored = m.sem("scored")
        maxed = m.sem("maxed")
        exped = m.sem("exped")
        step_done = m.sem("step_done")
        passed = m.sem("passed")
        kept = m.sem("kept")
        inverted = m.sem("inverted")
        turned = m.sems("turned")
        pT_out = m.sems("pT_out")
        attended = m.sems("attended")
        scaled = m.sems("scaled")

        block = ctx.enter_context(nc.Block())

        def chunk(ii, u, kb):
            local = (u // TT) * CHUNKS + (u % TT) * (u % TT + 1) // 2 + kb
            return local % 2, ii * CHUNKS + local // 2

        @block.sync
        def _(sp):
            sp.dma_start(mask32[:], a["causal"]).then_inc(mask_in, 16)

            def load(i, s):
                for j in range(R0):
                    sp.dma_start(qT[32 * j:32 * j + HD0, s, :],
                                 qT_dram[bass.ds(i * (R0 * HD0) + j * HD0, HD0), :]).then_inc(heads_in[s], 16)
                    sp.dma_start(kT[32 * j:32 * j + HD0, s, :],
                                 kT_dram[bass.ds(i * HD0, HD0), :]).then_inc(heads_in[s], 16)

            load(0, 0)
            load(1, 1)
            with sp.Fori(1, TURNS) as ii:
                for s in range(2):
                    sp.wait_ge(scored, (ii - 1) * UNITS + (s + 1) * TT)
                    load(ii * 2 + s, s)

        @block.gpsimd
        def _(pool):
            pool.wait_ge(mask_in, 16)
            nc.gpsimd.tensor_copy(mask[:], mask32[:]).then_inc(mask_ready, 1)

        def turns(eng, prologue, body):
            prologue()
            with eng.Fori(0, TURNS - 1) as ii:
                for u in range(UNITS):
                    body(ii, u, True)
            for u in range(UNITS):
                body(TURNS - 1, u, u < UNITS - 1)

        @block.tensor
        def _(pe):
            start_at_one(pe, attended)
            pe.wait_ge(mask_ready, 1)

            def scores(ii, u):
                s, qt = (u // TT) % 2, u % TT
                n = ii * UNITS + u
                L = (qt + 1) * P
                if qt == 0:
                    pe.wait_ge(heads_in[s], 16 * 2 * R0 * (ii + u // UNITS + 1))
                pe.wait_ge(exped, after(n))
                for j in range(R0):
                    nc.tensor.matmul(ps_s[:, j, 0:L], qT[32 * j:32 * j + HD0, s, qt * P:(qt + 1) * P],
                                     kT[32 * j:32 * j + HD0, s, 0:L], start=True, stop=False)
                for j in range(R0):
                    last = nc.tensor.matmul(ps_s[:, j, L - P:L], ident16[:], mask[:], start=False, stop=True)
                last.then_inc(scored, 1)

            def body(ii, u, more):
                if more:
                    scores(ii, u + 1)
                s, qt, i = u % 2, u % TT, ii * 2 + u // TT
                k2 = ii * (UNITS // 2) + u // 2
                probs = exps if qt == 0 else rest
                pe.wait_ge(kept, ii * UNITS + u + 1)
                pe.wait_ge(scaled[s], after(k2))

                def attend(kb):
                    bank, c = chunk(ii, u, kb)
                    pe.wait_ge(pT_out[bank], after(c + 1))
                    for j in range(R0):
                        last = nc.tensor.matmul(ps_o[:, s, j * HD0:(j + 1) * HD0], pT[:, bank, j * P:(j + 1) * P],
                                                v_all[:, i, kb, :], start=(kb == 0 and j == 0),
                                                stop=(kb == qt), skip_group_check=True)
                    last.then_inc(attended[bank], 1)

                for kb in range(qt + 1):
                    bank, c = chunk(ii, u, kb)
                    pe.wait_ge(pT_out[bank], after(c))
                    for j in range(R0):
                        last = nc.tensor.transpose(ps_t[:, bank, j * P:(j + 1) * P],
                                                   probs[:, s, j, kb * P:(kb + 1) * P], ident[:])
                    last.then_inc(turned[bank], 1)
                    if kb >= 1:
                        attend(kb - 1)
                attend(qt)

            turns(pe, lambda: scores(0, 0), body)

        @block.vector
        def _(dve):
            def maxes(ii, u):
                qt = u % TT
                n = ii * UNITS + u
                k2 = ii * (UNITS // 2) + u // 2
                dve.wait_ge(scored, n + 1)
                dve.wait_ge(scaled[u % 2], after(k2))
                nc.vector.tensor_reduce(nmax[:, u % 2, :], ps_s[:, :, 0:(qt + 1) * P], AX.X, ALU.max, negate=True)\
                    .then_inc(maxed, 1)

            def body(ii, u, more):
                if more:
                    maxes(ii, u + 1)
                s, qt = u % 2, u % TT
                n = ii * UNITS + u
                L = (qt + 1) * P
                if qt >= 1:
                    dve.sem_clear(step_done)
                    done = 0
                wait_apart(dve, exped, after(n + 1), passed)
                if qt >= 1:
                    for r in range(ROUNDS):
                        if r >= 1:
                            dve.wait_ge(step_done, done)
                        src = exps if r == 0 else rest
                        for j in range(R0):
                            last = nc.vector.max(top[:, j, :], src[:, s, j, 0:L])
                        last.then_inc(step_done, 1)
                        dve.wait_ge(step_done, done + 1)
                        for j in range(R0):
                            last = nc.vector.match_replace(rest[:, s, j, 0:L], top[:, j, :], src[:, s, j, 0:L], 0.0)
                        last.then_inc(step_done, 1)
                        done += 2
                    dve.wait_ge(step_done, done)
                    for j in range(R0):
                        last = nc.vector.scalar_tensor_tensor(
                            out=rest[:, s, j, 0:L], in0=exps[:, s, j, 0:L], scalar=1.0, in1=rest[:, s, j, 0:L],
                            op0=ALU.mult, op1=ALU.subtract, accum_out=rsum[:, s, j:j + 1])
                    last.then_inc(step_done, 1)
                    dve.wait_ge(step_done, done + 1)
                nc.vector.reciprocal(rinv[:, s, :], rsum[:, s, :]).then_inc(kept, 1)

            turns(dve, lambda: maxes(0, 0), body)

        @block.scalar
        def _(act):
            start_at_one(act, exped, pT_out, scaled)

            def exponentials(ii, u):
                s, qt = u % 2, u % TT
                n = ii * UNITS + u
                k2 = ii * (UNITS // 2) + u // 2
                act.wait_ge(maxed, n + 1)
                act.wait_ge(scaled[s], after(k2))
                for j in range(R0):
                    sums = {"accum_out": rsum[:, s, j:j + 1]} if qt == 0 else {}
                    last = nc.scalar.activation(exps[:, s, j, 0:(qt + 1) * P], ps_s[:, j, 0:(qt + 1) * P], ACT.Exp,
                                                bias=nmax[:, s, j:j + 1], **sums)
                last.then_inc(exped, 1)

            def body(ii, u, more):
                if more:
                    exponentials(ii, u + 1)
                s, qt, i = u % 2, u % TT, ii * 2 + u // TT
                for kb in range(qt + 1):
                    bank, c = chunk(ii, u, kb)
                    act.wait_ge(turned[bank], c + 1)
                    act.wait_ge(attended[bank], after(c))
                    nc.scalar.activation(pT[:, bank, :], ps_t[:, bank, :], ACT.Copy).then_inc(pT_out[bank], 1)
                bank, c = chunk(ii, u, qt)
                act.wait_ge(attended[bank], after(c + 1))
                act.wait_ge(kept, ii * UNITS + u + 1)
                for j in range(R0):
                    last = nc.scalar.activation(o_all[:, i, qt, j * HD0:(j + 1) * HD0],
                                                ps_o[:, s, j * HD0:(j + 1) * HD0], ACT.Copy,
                                                scale=rinv[:, s, j:j + 1])
                last.then_inc(scaled[s], 1)

            turns(act, lambda: exponentials(0, 0), body)




class Norm:

    def __init__(self, m):
        self.res = m.sbuf("res", [P, 2, D])
        self.xn = m.sbuf("xn", [P, 2, D])
        self.stats = m.sbuf("stats", [P, 2, 6])
        self.mv = m.sbuf("mv", [P, 2, 2])
        self.sd = m.sbuf("sd", [P, 2, 1])
        self.rstd = m.sbuf("rstd", [P, 2, 1])
        self.summed = m.sems("n_summed")
        self.stated = m.sems("n_stated")
        self.meaned = m.sems("n_meaned")
        self.rooted = m.sems("n_rooted")
        self.inverted = m.sems("n_inverted")
        self.normed = m.sems("n_normed")
        self.passed = m.sem("n_passed")
        self.pool_passed = m.sem("n_pool_passed")

    def on_dve(self, nc, dve, s, k2, out=None):
        out = self.xn[:, s, :] if out is None else out
        dve.wait_ge(self.summed[s], after(k2 + 1))
        nc.vector.bn_stats(self.stats[:, s, :], self.res[:, s, :]).then_inc(self.stated[s], 1)
        wait_apart(dve, self.stated[s], k2 + 1, self.passed)
        nc.vector.bn_aggr(self.mv[:, s, :], self.stats[:, s, :]).then_inc(self.meaned[s], 1)
        dve.wait_ge(self.rooted[s], k2 + 1)
        nc.vector.reciprocal(self.rstd[:, s, :], self.sd[:, s, :]).then_inc(self.inverted[s], 1)
        dve.wait_ge(self.inverted[s], k2 + 1)
        nc.vector.tensor_scalar(out, self.res[:, s, :], self.mv[:, s, 0:1], self.rstd[:, s, :],
                                ALU.subtract, ALU.mult).then_inc(self.normed[s], 1)

    def on_act(self, nc, act, s, k2, eps):
        act.wait_ge(self.meaned[s], k2 + 1)
        nc.scalar.activation(self.sd[:, s, :], self.mv[:, s, 1:2], ACT.Sqrt, bias=eps[:, 0:1])\
            .then_inc(self.rooted[s], 1)




def project_out0(nc, a, ident, eps, x_all, xT_all):
    with ExitStack() as ctx:
        m = Place(nc, ctx, "o0_")
        w = m.sbuf("w", [P, KC, D])
        rows = m.sbuf("rows", [P, TT, D])
        rowsT = m.sbuf("rowsT", [P, 2, D])
        x = m.sbuf("x", [P, 2, D])
        norm = Norm(m)
        ps_t = m.psum("ps_t", [P, 2, D])
        ps_y = m.psum("ps_y", [P, 2, D])
        ps_n = m.psum("ps_n", [P, 2, D])
        w_in = m.sem("w_in")
        x_in = m.sems("x_in")
        gathered = m.sem("gathered")
        batch_turned = m.sem("batch_turned")
        turned = m.sems("turned")
        rowsT_out = m.sems("rowsT_out")
        projected = m.sems("projected")
        copied = m.sems("copied")
        xn_turned = m.sems("xn_turned")
        xT_out = m.sems("xT_out")

        block = ctx.enter_context(nc.Block())
        o_view = x_all[:].rearrange("p b (g t c) -> p b t g c", g=G0, t=TT)
        x_view = x_all[:].rearrange("p b (t c) -> p b t c", t=TT)

        @block.sync
        def _(sp):
            sp.dma_start(w[:], a["wo0T"].rearrange("(k p) n -> p k n", p=P)).then_inc(w_in, 16)
            src = a["x"].rearrange("(b t p) n -> b t p n", b=NB, t=TT)
            with sp.Fori(0, NB) as b:
                for t in range(TT):
                    s, k2 = t % 2, b * 2 + t // 2
                    sp.wait_ge(norm.summed[s], after(k2))
                    sp.dma_start(x[:, s, :], src[b, t]).then_inc(x_in[s], 16)

        @block.gpsimd
        def _(pool):
            start_at_one(pool, copied)
            with pool.Fori(0, NB) as b:
                wait_apart(pool, batch_turned, after(b), norm.pool_passed)
                for t in range(TT):
                    nc.gpsimd.tensor_copy(rows[:, t, :].rearrange("p (g c) -> p g c", g=G0),
                                          o_view[:, b, t, :, :]).then_inc(gathered, 1)
                pool.wait_ge(gathered, b * TT + TT)
                for t in range(TT):
                    s, k2 = t % 2, b * 2 + t // 2
                    wait_apart(pool, norm.normed[s], after(k2 + 1), norm.pool_passed)
                    nc.gpsimd.tensor_copy(x_view[:, b, t, :], norm.xn[:, s, :]).then_inc(copied[s], 1)

        @block.tensor
        def _(pe):
            start_at_one(pe, batch_turned, turned, projected, xn_turned)
            pe.wait_ge(w_in, 16)
            with pe.Fori(0, NB) as b:
                for t in range(TT + 1):
                    if t < TT:
                        s, k2 = t % 2, b * 2 + t // 2
                        pe.wait_ge(gathered, b * TT + t + 1)
                        pe.wait_ge(rowsT_out[s], after(k2))
                        for k in range(KC):
                            last = nc.tensor.transpose(ps_t[:, s, k * P:(k + 1) * P], rows[:, t, k * P:(k + 1) * P],
                                                       ident[:])
                        last.then_inc(turned[s], 1)
                        pe.wait_ge(rowsT_out[s], after(k2 + 1))
                        pe.wait_ge(norm.summed[s], after(k2))
                        for k in range(KC):
                            last = nc.tensor.matmul(ps_y[:, s, :], rowsT[:, s, k * P:(k + 1) * P], w[:, k, :],
                                                    start=(k == 0), stop=(k == KC - 1))
                        last.then_inc(projected[s], 1)
                    if t == TT - 1:
                        pe.wait_ge(turned[1], after(b * 2 + 2))
                        pe.sem_inc(batch_turned, 1)
                    if t >= 1:
                        transpose_rows(nc, pe, ident, norm, (t - 1) % 2, b * 2 + (t - 1) // 2, ps_n, xn_turned, xT_out)

        @block.scalar
        def _(act):
            start_at_one(act, rowsT_out, xT_out)
            with act.Fori(0, NB) as b:
                for t in range(TT + 1):
                    if t < TT:
                        s, k2 = t % 2, b * 2 + t // 2
                        act.wait_ge(turned[s], after(k2 + 1))
                        act.wait_ge(projected[s], after(k2))
                        nc.scalar.activation(rowsT[:, s, :], ps_t[:, s, :], ACT.Copy).then_inc(rowsT_out[s], 1)
                    if t >= 1:
                        s, k2 = (t - 1) % 2, b * 2 + (t - 1) // 2
                        norm.on_act(nc, act, s, k2, eps)
                        act.wait_ge(xn_turned[s], after(k2 + 1))
                        nc.scalar.activation(xT_all[:, :, b, (t - 1) * P:t * P],
                                             ps_n[:, s, :].rearrange("p (k c) -> p k c", k=KC), ACT.Copy)\
                            .then_inc(xT_out[s], 1)

        @block.vector
        def _(dve):
            start_at_one(dve, norm.summed, norm.normed)
            with dve.Fori(0, NB) as b:
                for t in range(TT):
                    s, k2 = t % 2, b * 2 + t // 2
                    dve.wait_ge(projected[s], after(k2 + 1))
                    dve.wait_ge(x_in[s], 16 * (k2 + 1))
                    nc.vector.tensor_tensor(norm.res[:, s, :], ps_y[:, s, :], x[:, s, :], ALU.add)\
                        .then_inc(norm.summed[s], 1)
                    dve.wait_ge(copied[s], after(k2))
                    dve.wait_ge(xn_turned[s], after(k2))
                    norm.on_dve(nc, dve, s, k2)


def transpose_rows(nc, pe, ident, norm, s, k2, ps, turned, out):
    pe.wait_ge(norm.normed[s], after(k2 + 1))
    pe.wait_ge(out[s], after(k2))
    for k in range(KC):
        last = nc.tensor.transpose(ps[:, s, k * P:(k + 1) * P], norm.xn[:, s, k * P:(k + 1) * P], ident[:])
    last.then_inc(turned[s], 1)




def feed_forward0(nc, a, ident, eps, x_all, xT_all, w_gu, w_dn):
    USES = [(FT + 1 - f) // 2 for f in range(2)]
    with ExitStack() as ctx:
        m = Place(nc, ctx, "f0_")
        hT = m.sbuf("hT", [P, FT, S])
        silu = m.sbuf("silu", [P, 2, S])
        norm = Norm(m)
        ps_g = m.psum("ps_g", [P, 2, S])
        ps_u = m.psum("ps_u", [P, 2, S])
        ps_y = m.psum("ps_y", [P, 2, D])
        ps_n = m.psum("ps_n", [P, 2, D])
        up_done = m.sems("up_done")
        silu_done = m.sems("silu_done")
        gated = m.sems("gated")
        projected = m.sems("projected")
        copied = m.sems("copied")
        xn_turned = m.sems("xn_turned")
        xT_out = m.sems("xT_out")

        block = ctx.enter_context(nc.Block())
        x_view = x_all[:].rearrange("p b (t c) -> p b t c", t=TT)

        @block.tensor
        def _(pe):
            start_at_one(pe, projected, xn_turned)
            with pe.Fori(0, NB) as b:
                for f in range(FT):
                    s, c, r = f % 2, b * USES[f % 2] + f // 2, rows_of(f)
                    pe.wait_ge(gated[s], after(c))
                    for ps, col in ((ps_g, f * P), (ps_u, INTER + f * P)):
                        for k in range(KC):
                            last = nc.tensor.matmul(ps[0:r, s, :], w_gu[:, k, col:col + r], xT_all[:, k, b, :],
                                                    start=(k == 0), stop=(k == KC - 1))
                    last.then_inc(up_done[s], 1)
                for s in range(2):
                    pe.wait_ge(gated[s], after((b + 1) * USES[s]))
                for t in range(TT + 1):
                    if t < TT:
                        s, k2 = t % 2, b * 2 + t // 2
                        pe.wait_ge(norm.summed[s], after(k2))
                        for f in range(FT):
                            last = nc.tensor.matmul(ps_y[:, s, :], hT[0:rows_of(f), f, t * P:(t + 1) * P],
                                                    w_dn[0:rows_of(f), f, :], start=(f == 0), stop=(f == FT - 1))
                        last.then_inc(projected[s], 1)
                    if t >= 1:
                        transpose_rows(nc, pe, ident, norm, (t - 1) % 2, b * 2 + (t - 1) // 2, ps_n, xn_turned, xT_out)

        @block.scalar
        def _(act):
            start_at_one(act, xT_out)
            with act.Fori(0, NB) as b:
                for f in range(FT):
                    s, c, r = f % 2, b * USES[f % 2] + f // 2, rows_of(f)
                    act.wait_ge(up_done[s], c + 1)
                    act.wait_ge(gated[s], after(c))
                    nc.scalar.activation(silu[0:r, s, :], ps_g[0:r, s, :], ACT.Silu).then_inc(silu_done[s], 1)
                for t in range(TT):
                    s, k2 = t % 2, b * 2 + t // 2
                    norm.on_act(nc, act, s, k2, eps)
                    act.wait_ge(xn_turned[s], after(k2 + 1))
                    nc.scalar.activation(xT_all[:, :, b, t * P:(t + 1) * P],
                                         ps_n[:, s, :].rearrange("p (k c) -> p k c", k=KC), ACT.Copy)\
                        .then_inc(xT_out[s], 1)

        @block.vector
        def _(dve):
            start_at_one(dve, gated, norm.summed, norm.normed)
            with dve.Fori(0, NB) as b:
                for f in range(FT):
                    s, c, r = f % 2, b * USES[f % 2] + f // 2, rows_of(f)
                    dve.wait_ge(silu_done[s], c + 1)
                    nc.vector.tensor_tensor(hT[0:r, f, :], ps_u[0:r, s, :], silu[0:r, s, :], ALU.mult)\
                        .then_inc(gated[s], 1)
                for t in range(TT):
                    s, k2 = t % 2, b * 2 + t // 2
                    dve.wait_ge(projected[s], after(k2 + 1))
                    nc.vector.tensor_tensor(norm.res[:, s, :], ps_y[:, s, :], x_view[:, b, t, :], ALU.add)\
                        .then_inc(norm.summed[s], 1)
                    dve.wait_ge(copied[s], after(k2))
                    dve.wait_ge(xn_turned[s], after(k2))
                    norm.on_dve(nc, dve, s, k2)

        @block.gpsimd
        def _(pool):
            start_at_one(pool, copied)
            with pool.Fori(0, NB) as b:
                for t in range(TT):
                    s, k2 = t % 2, b * 2 + t // 2
                    wait_apart(pool, norm.normed[s], after(k2 + 1), norm.pool_passed)
                    nc.gpsimd.tensor_copy(x_view[:, b, t, :], norm.xn[:, s, :]).then_inc(copied[s], 1)




def attend_layer1(nc, a, ident, ident16, x_all, xT_all):
    HP = R1 // 2
    PADS = S + WIN
    with ExitStack() as ctx:
        m = Place(nc, ctx, "a1_")
        w = m.sbuf("w", [P, 2, KC, W1])
        wo = m.sbuf("wo", [P, 2, R1, D])
        mask = m.sbuf("mask", [P, NW, P], BF16)
        qT = m.sbuf("qT", [P, HP, NW, 2 * WIN])
        kT = m.sbuf("kT", [P, PADS])
        vT = m.sbuf("vT", [P, PADS])
        vw = m.sbuf("vw", [P, NW, HD1])
        probs = m.sbuf("probs", [P, HP, NW, P])
        pT = m.sbuf("pT", [P, HP, NW, P])
        oT = m.sbuf("oT", [P, R1, S])
        mx = m.sbuf("mx", [P, HP, NW])
        rsum = m.sbuf("rsum", [P, HP, NW])
        rinv = m.sbuf("rinv", [P, HP, NW])
        ps = m.psum("ps", [P, 4, 512])
        ps_y = m.psum("ps_y", [P, TT, D])
        mask_in = m.sem("mask_in")
        w_in = m.sems("w_in")
        padded = m.sem("padded")
        kv_done = m.sem("kv_done")
        q_done = m.sem("q_done")
        kv_out = m.sem("kv_out")
        q_out = m.sem("q_out")
        scored = m.sem("scored")
        maxed = m.sem("maxed")
        shifted = m.sem("shifted")
        exped = m.sem("exped")
        rsummed = m.sem("rsummed")
        inverted = m.sem("inverted")
        normed = m.sem("normed")
        v_turned = m.sem("v_turned")
        vw_out = m.sem("vw_out")
        p_turned = m.sem("p_turned")
        pT_out = m.sem("pT_out")
        attended = m.sem("attended")
        oT_out = m.sem("oT_out")
        projected = m.sem("projected")
        added = m.sem("added")

        block = ctx.enter_context(nc.Block())
        scale = float(HD1) ** -0.5
        x_view = x_all[:].rearrange("p b (t c) -> p b t c", t=TT)
        banks = [ps[:, 0:2, :].rearrange("p b (w c) -> p (b w) c", c=P),
                 ps[:, 2:4, :].rearrange("p b (w c) -> p (b w) c", c=P)]

        def items(eng, body):
            with eng.Fori(0, G1 // 2) as gg:
                for s in range(2):
                    with eng.Fori(0, NB) as b:
                        body(gg, s, b, (gg * 2 + s) * NB + b)

        @block.sync
        def _(sp):
            sp.dma_start(probs[:, 0, :, :], a["window"]).then_inc(mask_in, 16)

            def load(g, s):
                sp.dma_start(w[:, s, :, :], a["w1T"][g]).then_inc(w_in[s], 16)
                sp.dma_start(wo[:, s, :, :], a["wo1T"][g]).then_inc(w_in[s], 16)

            load(0, 0)
            load(1, 1)
            with sp.Fori(1, G1 // 2) as gg:
                for s in range(2):
                    sp.wait_ge(projected, ((gg - 1) * 2 + s + 1) * NB * TT)
                    load(gg * 2 + s, s)

        @block.tensor
        def _(pe):
            pe.wait_ge(padded, 3)

            def body(gg, g, b, i):
                pe.wait_ge(w_in[g], 32 * (gg + 1))

                def project(bank, col, sem):
                    for k in range(KC):
                        last = nc.tensor.matmul(ps[:, bank, :], w[:, g, k, col:col + HD1], xT_all[:, k, b, :],
                                                start=(k == 0), stop=(k == KC - 1))
                    last.then_inc(sem, 1)

                def scores(hp):
                    for half in range(2):
                        for q in range(4):
                            wi = 4 * half + q
                            nc.tensor.matmul(banks[hp][:, wi, :], qT[:, hp, wi, :], kT[:, wi * WIN:wi * WIN + P],
                                             start=(q == 0), stop=False, skip_group_check=True)
                        last = nc.tensor.matmul(ps[:, 2 * hp + half, :], ident16[:],
                                                mask[:, 4 * half:4 * half + 4, :].rearrange("p w c -> p (w c)"),
                                                start=False, stop=True, skip_group_check=True)
                    last.then_inc(scored, 1)

                def turn_probs(hp):
                    pe.wait_ge(normed, 2 * i + hp + 1)
                    for wi in range(NW):
                        last = nc.tensor.transpose(banks[hp][:, wi, :], probs[:, hp, wi, :], ident[:])
                    last.then_inc(p_turned, 1)

                def attend(hp):
                    pe.wait_ge(pT_out, 2 * i + hp + 1)
                    for wi in range(NW):
                        last = nc.tensor.matmul(banks[hp][:, wi, :], vw[:, wi, :], pT[:, hp, wi, :],
                                                start=(wi % 4 == 0), stop=True, skip_group_check=True)
                    last.then_inc(attended, 1)

                def project_out(hp):
                    pe.wait_ge(oT_out, 2 * i + hp + 1)
                    for t in range(TT):
                        for j in range(2 * hp, 2 * hp + 2):
                            last = nc.tensor.matmul(ps_y[:, t, :], oT[:, j, t * P:(t + 1) * P], wo[:, g, j, :],
                                                    start=(j == 0), stop=(j == R1 - 1))
                        if hp == HP - 1:
                            last.then_inc(projected, 1)

                project(0, R1 * HD1, kv_done)
                project(1, (R1 + 1) * HD1, kv_done)
                project(2, 0, q_done)
                project(3, HD1, q_done)
                pe.wait_ge(kv_out, 2 * i + 2)
                pe.wait_ge(q_out, 4 * i + 2)
                scores(0)
                project(2, 2 * HD1, q_done)
                project(3, 3 * HD1, q_done)
                pe.wait_ge(shifted, 2 * i + 1)
                for wi in range(NW):
                    last = nc.tensor.transpose(banks[0][:, wi, :], vT[:, wi * WIN:wi * WIN + P], ident[:])
                last.then_inc(v_turned, 1)
                pe.wait_ge(q_out, 4 * i + 4)
                scores(1)
                pe.wait_ge(vw_out, i + 1)
                turn_probs(0)
                attend(0)
                pe.wait_ge(added, after(4 * i))
                project_out(0)
                turn_probs(1)
                attend(1)
                project_out(1)

            items(pe, body)

        @block.scalar
        def _(act):
            def body(gg, g, b, i):
                def query(j):
                    act.wait_ge(q_done, 4 * i + j + 1)
                    dst = qT[:, j // 2, :, (j % 2) * WIN:(j % 2 + 1) * WIN]
                    nc.scalar.activation(dst, ps[:, 2 + j % 2, :].rearrange("p (w c) -> p w c", c=WIN), ACT.Copy)\
                        .then_inc(q_out, 1)

                for n, dst in enumerate((kT, vT)):
                    act.wait_ge(kv_done, 2 * i + n + 1)
                    nc.scalar.activation(dst[:, WIN:PADS], ps[:, n, :], ACT.Copy).then_inc(kv_out, 1)
                for j in range(R1):
                    query(j)

                def exponential(hp):
                    act.wait_ge(shifted, 2 * i + hp + 1)
                    nc.scalar.activation(probs[:, hp, :, :], probs[:, hp, :, :], ACT.Exp, scale=scale)\
                        .then_inc(exped, 1)

                def turned(hp):
                    act.wait_ge(p_turned, 2 * i + hp + 1)
                    nc.scalar.activation(pT[:, hp, :, :], banks[hp], ACT.Copy).then_inc(pT_out, 1)

                exponential(0)
                exponential(1)
                turned(0)
                turned(1)

            act.wait_ge(padded, 3)
            items(act, body)

        @block.gpsimd
        def _(pool):
            nc.gpsimd.memset(kT[:, 0:WIN], 0.0).then_inc(padded, 1)
            nc.gpsimd.memset(vT[:, 0:WIN], 0.0).then_inc(padded, 1)
            pool.wait_ge(mask_in, 16)
            nc.gpsimd.tensor_copy(mask[:], probs[:, 0, :, :]).then_inc(padded, 1)

            def body(gg, g, b, i):
                for hp in range(HP):
                    pool.wait_ge(inverted, 2 * i + hp + 1)
                    nc.gpsimd.tensor_tensor(probs[:, hp, :, :], probs[:, hp, :, :],
                                            bcast(rinv[:, hp, :], 2, P), ALU.mult).then_inc(normed, 1)

            items(pool, body)

        @block.vector
        def _(dve):
            start_at_one(dve, added)

            def body(gg, g, b, i):
                def shift(hp):
                    dve.wait_ge(scored, 2 * i + hp + 1)
                    nc.vector.tensor_reduce(mx[:, hp, :], banks[hp], AX.X, ALU.max).then_inc(maxed, 1)
                    dve.wait_ge(maxed, 2 * i + hp + 1)
                    nc.vector.tensor_tensor(probs[:, hp, :, :], banks[hp], bcast(mx[:, hp, :], 2, P),
                                            ALU.subtract).then_inc(shifted, 1)

                def invert(hp):
                    dve.wait_ge(exped, 2 * i + hp + 1)
                    nc.vector.tensor_reduce(rsum[:, hp, :], probs[:, hp, :, :], AX.X, ALU.add).then_inc(rsummed, 1)
                    dve.wait_ge(rsummed, 2 * i + hp + 1)
                    nc.vector.reciprocal(rinv[:, hp, :], rsum[:, hp, :]).then_inc(inverted, 1)

                def output(hp):
                    dve.wait_ge(attended, 2 * i + hp + 1)
                    for h in range(2):
                        last = nc.vector.tensor_copy(
                            oT[:, 2 * hp + h, :].rearrange("p (w c) -> p w c", c=WIN),
                            banks[hp][:, :, h * WIN:(h + 1) * WIN])
                    last.then_inc(oT_out, 1)

                shift(0)
                invert(0)
                dve.wait_ge(v_turned, i + 1)
                nc.vector.tensor_copy(vw[:], banks[0]).then_inc(vw_out, 1)
                shift(1)
                invert(1)
                output(0)
                output(1)
                for t in range(TT):
                    dve.wait_ge(projected, 4 * i + t + 1)
                    nc.vector.tensor_tensor(x_view[:, b, t, :], ps_y[:, t, :], x_view[:, b, t, :], ALU.add)\
                        .then_inc(added, 1)

            items(dve, body)




def feed_forward1(nc, a, ident, eps, x_all, out):
    NZ = E1 + E1 * RK
    with ExitStack() as ctx:
        m = Place(nc, ctx, "f1_")
        w = m.sbuf("w", [P, KC, D])
        wz = m.sbuf("wz", [P, KC, NZ])
        wb = m.sbuf("wb", [E1 * RK, D])
        bias = m.sbuf("bias", [P, E1])
        xT = m.sbuf("xT", [P, 2, D])
        logit = m.sbuf("logit", [P, 2, E1])
        best = m.sbuf("best", [P, 2, 1])
        is_best = m.sbuf("is_best", [P, 2, E1])
        left = m.sbuf("left", [P, 2, E1 + 1])
        chosen = m.sbuf("chosen", [P, 2, E1])
        z = m.sbuf("z", [P, 2, E1, RK])
        zT = m.sbuf("zT", [E1 * RK, 2, P])
        out_rows = m.sbuf("out_rows", [P, 2, D])
        first = Norm(Place(nc, ctx, "f1a_"))
        second = Norm(Place(nc, ctx, "f1b_"))
        ps_n = m.psum("ps_n", [P, 2, D])
        ps_y = m.psum("ps_y", [P, 2, D])
        ps_z = m.psum("ps_z", [P, 2, 512])
        ps_zT = m.psum("ps_zT", [P, 2, 512])
        w_in = m.sem("w_in")
        xn_turned = m.sems("xn_turned")
        xT_out = m.sems("xT_out")
        z_done = m.sems("z_done")
        picked = m.sem("picked")
        z_out = m.sems("z_out")
        z_turned = m.sems("z_turned")
        zT_out = m.sems("zT_out")
        y_done = m.sems("y_done")
        stored = m.sems("stored")
        PICKS = 4 + 2 * (E1 - 1)

        block = ctx.enter_context(nc.Block())
        x_view = x_all[:].rearrange("p b (t c) -> p b t c", t=TT)
        out_view = out.rearrange("(b t p) n -> b t p n", b=NB, t=TT)

        @block.sync
        def _(sp):
            start_at_one(sp, stored)
            sp.dma_start(w[:], a["w_upT"].rearrange("(k p) n -> p k n", p=P)).then_inc(w_in, 16)
            sp.dma_start(wz[:], a["wzT"].rearrange("(k p) n -> p k n", p=P)).then_inc(w_in, 16)
            sp.dma_start(wb[:], a["lora_BT"]).then_inc(w_in, 16)
            sp.dma_start(bias[:], a["bias"].partition_broadcast(P)).then_inc(w_in, 16)
            with sp.Fori(0, NB) as b:
                for t in range(TT):
                    s, k2 = t % 2, b * 2 + t // 2
                    sp.wait_ge(second.normed[s], after(k2 + 1))
                    sp.dma_start(out_view[b, t], out_rows[:, s, :]).then_inc(stored[s], 16)
            for s in range(2):
                sp.wait_ge(stored[s], after(NB * 2, 16))

        @block.tensor
        def _(pe):
            start_at_one(pe, xn_turned, z_turned, y_done)
            pe.wait_ge(w_in, 64)

            def base(b, t):
                s, k2 = t % 2, b * 2 + t // 2
                transpose_rows(nc, pe, ident, first, s, k2, ps_n, xn_turned, xT_out)
                pe.wait_ge(xT_out[s], after(k2 + 1))
                pe.wait_ge(z_out[s], after(k2))
                for k in range(KC):
                    last = nc.tensor.matmul(ps_z[:, s, 0:NZ], xT[:, s, k * P:(k + 1) * P], wz[:, k, :],
                                            start=(k == 0), stop=(k == KC - 1))
                last.then_inc(z_done[s], 1)
                pe.wait_ge(second.summed[s], after(k2))
                for k in range(KC):
                    nc.tensor.matmul(ps_y[:, s, :], xT[:, s, k * P:(k + 1) * P], w[:, k, :],
                                     start=(k == 0), stop=False)

            def expert(b, t):
                s, k2 = t % 2, b * 2 + t // 2
                pe.wait_ge(z_out[s], after(k2 + 1))
                pe.wait_ge(zT_out[s], after(k2))
                nc.tensor.transpose(ps_zT[0:E1 * RK, s, 0:P], z[:, s, :, :].rearrange("p e r -> p (e r)"), ident[:])\
                    .then_inc(z_turned[s], 1)
                pe.wait_ge(zT_out[s], after(k2 + 1))
                nc.tensor.matmul(ps_y[:, s, :], zT[:, s, :], wb[:], start=False, stop=True).then_inc(y_done[s], 1)

            with pe.Fori(0, NB) as b:
                for t in range(TT + 1):
                    if t < TT:
                        base(b, t)
                    if t >= 1:
                        expert(b, t - 1)

        @block.scalar
        def _(act):
            start_at_one(act, xT_out, zT_out)

            def head(b, t):
                s, k2 = t % 2, b * 2 + t // 2
                first.on_act(nc, act, s, k2, eps)
                act.wait_ge(xn_turned[s], after(k2 + 1))
                act.wait_ge(y_done[s], after(k2))
                nc.scalar.activation(xT[:, s, :], ps_n[:, s, :], ACT.Copy).then_inc(xT_out[s], 1)

            def tail(b, t):
                s, k2 = t % 2, b * 2 + t // 2
                act.wait_ge(z_turned[s], after(k2 + 1))
                nc.scalar.activation(zT[:, s, :], ps_zT[0:E1 * RK, s, 0:P], ACT.Copy).then_inc(zT_out[s], 1)
                second.on_act(nc, act, s, k2, eps)

            with act.Fori(0, NB) as b:
                for t in range(TT + 1):
                    if t < TT:
                        head(b, t)
                    if t >= 1:
                        tail(b, t - 1)

        @block.vector
        def _(dve):
            start_at_one(dve, first.summed, first.normed, second.summed, second.normed, z_out)

            def head(b, t):
                s, k2 = t % 2, b * 2 + t // 2
                nc.vector.tensor_copy(first.res[:, s, :], x_view[:, b, t, :]).then_inc(first.summed[s], 1)
                dve.wait_ge(xn_turned[s], after(k2))
                dve.wait_ge(second.summed[s], after(k2))
                first.on_dve(nc, dve, s, k2)

            def choose(b, t):
                s, k2 = t % 2, b * 2 + t // 2
                done = [0]

                def step(ins):
                    done[0] += 1
                    ins.then_inc(picked, 1)
                    dve.wait_ge(picked, (b * TT + t) * PICKS + done[0])

                dve.wait_ge(z_done[s], k2 + 1)
                step(nc.vector.tensor_tensor(logit[:, s, :], ps_z[:, s, 0:E1], bias[:], ALU.add))
                step(nc.vector.tensor_reduce(best[:, s, :], logit[:, s, :], AX.X, ALU.max))
                step(nc.vector.tensor_scalar(is_best[:, s, :], logit[:, s, :], best[:, s, :], None, ALU.is_ge))
                step(nc.vector.tensor_copy(chosen[:, s, 0:1], is_best[:, s, 0:1]))
                for e in range(1, E1):
                    step(nc.vector.tensor_reduce(left[:, s, e:e + 1], chosen[:, s, 0:e], AX.X, ALU.add))
                    step(nc.vector.tensor_tensor(chosen[:, s, e:e + 1], is_best[:, s, e:e + 1], left[:, s, e:e + 1],
                                                 ALU.is_gt))
                dve.wait_ge(z_turned[s], after(k2))
                nc.vector.tensor_tensor(z[:, s, :, :], ps_z[:, s, E1:NZ].rearrange("p (e r) -> p e r", r=RK),
                                        bcast(chosen[:, s, :], 2, RK), ALU.mult).then_inc(z_out[s], 1)

            def tail(b, t):
                s, k2 = t % 2, b * 2 + t // 2
                dve.wait_ge(y_done[s], after(k2 + 1))
                nc.vector.tensor_tensor(second.res[:, s, :], ps_y[:, s, :], first.xn[:, s, :], ALU.add)\
                    .then_inc(second.summed[s], 1)
                dve.wait_ge(stored[s], after(k2, 16))
                second.on_dve(nc, dve, s, k2, out_rows[:, s, :])

            with dve.Fori(0, NB) as b:
                for t in range(TT + 1):
                    if t < TT:
                        head(b, t)
                        choose(b, t)
                    if t >= 1:
                        tail(b, t - 1)


def load_constants(nc, a, ident, ident16, eps):
    with ExitStack() as ctx:
        m = Place(nc, ctx, "c_")
        ident_in = m.sem("ident_in")
        eps_set = m.sem("eps_set")
        block = ctx.enter_context(nc.Block())

        @block.sync
        def _(sp):
            sp.dma_start(ident[:], a["ident"]).then_inc(ident_in, 16)

        @block.vector
        def _(dve):
            nc.vector.memset(eps[:], EPS).then_inc(eps_set, 1)
            dve.wait_ge(ident_in, 16)
            nc.vector.tensor_copy(ident16[:], ident[:]).then_inc(eps_set, 1)
            dve.wait_ge(eps_set, 2)


def program(nc, a, out, debug=None):
    qT_dram = nc.dram_tensor("qT_scratch", [NB * D, S], F32).ap()
    kT_dram = nc.dram_tensor("kT_scratch", [NB * KV0, S], F32).ap()
    with ExitStack() as ctx:
        m = Place(nc, ctx, "")
        ident = m.sbuf("ident_sb", [P, P])
        ident16 = m.sbuf("ident16_sb", [P, P], BF16)
        eps = m.sbuf("eps_sb", [P, 1])
        x_all = m.sbuf("x_all", [P, NB, TT * D])
        xT_all = m.sbuf("xT_all", [P, KC, NB, S])
        load_constants(nc, a, ident, ident16, eps)
        with ExitStack() as ffn:
            mf = Place(nc, ffn, "")
            w_gu = mf.sbuf("w_gu", [P, KC, 2 * INTER])
            w_dn = mf.sbuf("w_dn", [P, FT, D])
            dequantise(nc, a, w_gu, w_dn, x_all[:].rearrange("p b n -> p (b n)"))
            with ExitStack() as att:
                v_all = Place(nc, att, "").sbuf("v_all", [P, NB, G0, TT, HD0])
                project_layer0(nc, a, ident, v_all, qT_dram, kT_dram)
                v_pairs = v_all[:].rearrange("p b g t d -> p (b g) t d")
                o_pairs = x_all[:].rearrange("p b (g t c) -> p (b g) t c", g=G0, t=TT)
                work = xT_all[:].rearrange("p (a s) h n -> p a s h n", a=2)
                attend_layer0(nc, a, ident, ident16, v_pairs, qT_dram, kT_dram, o_pairs, work)
            project_out0(nc, a, ident, eps, x_all, xT_all)
            if debug is not None:
                dump(nc, x_all, debug, 0)
            feed_forward0(nc, a, ident, eps, x_all, xT_all, w_gu, w_dn)
        if debug is not None:
            dump(nc, x_all, debug, 1)
        attend_layer1(nc, a, ident, ident16, x_all, xT_all)
        if debug is not None:
            dump(nc, x_all, debug, 2)
        feed_forward1(nc, a, ident, eps, x_all, out)


def dump(nc, x_all, debug, n):
    with ExitStack() as ctx:
        m = Place(nc, ctx, f"d{n}_")
        dumped = m.sem("dumped")
        block = ctx.enter_context(nc.Block())

        @block.sync
        def _(sp):
            dst = debug.rearrange("n (b t p) c -> n b p t c", b=NB, p=P)
            for b in range(NB):
                sp.dma_start(dst[n, b], x_all[:, b, :].rearrange("p (t c) -> p t c", t=TT)).then_inc(dumped, 16)
            sp.wait_ge(dumped, 16 * NB)


def constants():
    import numpy as np

    inv_freq = (1.0 / np.float32(10000.0) ** (np.arange(0, HD0, 2, dtype=np.float32) / np.float32(HD0)))
    freqs = np.outer(np.arange(S, dtype=np.float32), inv_freq.astype(np.float32)).astype(np.float32)
    emb = np.concatenate([freqs, freqs], axis=-1)
    cos, sin = np.cos(emb).astype(np.float32), np.sin(emb).astype(np.float32)
    sin[:, :HD0 // 2] *= -1
    scale = np.float32(HD0 ** -0.5)
    rope = np.stack([cos * scale, sin * scale, cos, sin], axis=1)
    rope = rope.reshape(TT, P, 4, HD0).transpose(1, 0, 2, 3)
    q, c = np.arange(P)[:, None], np.arange(P)[None, :]
    causal = np.where(c > q, NEG, 0.0).astype(np.float32)
    seen = (c > q % WIN) & (c <= q % WIN + WIN)
    window = np.broadcast_to(np.where(seen, 0.0, NEG)[:, None, :], (P, NW, P)).copy()
    window[:, 0, :WIN] = NEG
    return {
        "rope": np.ascontiguousarray(rope),
        "causal": causal,
        "window": window.astype(np.float32),
        "ident": np.eye(P, dtype=np.float32),
        "shift": (4 * (np.arange(P, dtype=np.uint32) % PACK)).reshape(P, 1),
        "iota": np.arange(16, dtype=np.float32).reshape(16, 1),
    }


def layout(i):
    import numpy as np

    x = i["L0_attn_hidden_states"].reshape(NB * S, D)
    w1 = [i["L1_attn_wq"].reshape(G1, R1 * HD1, KC, P), i["L1_attn_wk"].reshape(G1, HD1, KC, P),
          i["L1_attn_wv"].reshape(G1, HD1, KC, P)]
    return {
        "x": x,
        "xT": x.T,
        "wqkvT": np.concatenate([i["L0_attn_Wq"], i["L0_attn_Wk"], i["L0_attn_Wv"]]).T,
        "wo0T": i["L0_attn_Wo"].T,
        "qw_gu": np.repeat(i["L0_ffn_qweight_gu"], PACK, axis=0),
        "qw_dn": np.repeat(i["L0_ffn_qweight_down"], PACK, axis=0),
        "qzeros_gu": i["L0_ffn_qzeros_gu"],
        "qzeros_dn": i["L0_ffn_qzeros_down"],
        "scales_gu": i["L0_ffn_scales_gu"],
        "scales_dn": i["L0_ffn_scales_down"],
        "g_idx_gu": i["L0_ffn_g_idx_gu"],
        "g_idx_dn": i["L0_ffn_g_idx_down"],
        "w1T": np.concatenate(w1, axis=1).transpose(0, 3, 2, 1),
        "wo1T": i["L1_attn_wo"].T.reshape(G1, R1, HD1, D).transpose(0, 2, 1, 3),
        "w_upT": i["L1_ffn_W_up"].T,
        "wzT": np.concatenate([i["L1_ffn_gate_w"], i["L1_ffn_lora_A"].reshape(E1 * RK, D)]).T,
        "lora_BT": i["L1_ffn_lora_B"].transpose(0, 2, 1).reshape(E1 * RK, D),
        "bias": i["L1_ffn_expert_bias"],
    }


def kernel(**inputs):
    import numpy as np
    import concourse.bacc as bacc
    from concourse.bass_utils import run_bass_kernel_spmd

    nc = bacc.Bacc("TRN2", target_bir_lowering=False, num_devices=1)
    arrays, aps = {}, {}
    host = layout({k: np.asarray(v) for k, v in inputs.items()})
    for name, v in {**host, **constants()}.items():
        v = np.ascontiguousarray(v)
        arrays[f"in_{name}"] = v
        aps[name] = nc.dram_tensor(f"in_{name}", v.shape, mybir.dt.from_np(v.dtype), kind="ExternalInput").ap()
    out = nc.dram_tensor("out", [NB * S, D], F32, kind="ExternalOutput").ap()
    debug = nc.dram_tensor("debug", [3, NB * S, D], F32, kind="ExternalOutput").ap() if DEBUG else None
    program(nc, aps, out, debug)
    r = run_bass_kernel_spmd(nc, [arrays], core_ids=[0])
    return r.results[0]["out"].reshape(NB, S, D)


DEBUG = False
```

```python
import math
from contextlib import ExitStack

import concourse.bass as bass
from concourse import mybir

ALU = mybir.AluOpType
ACT = mybir.ActivationFunctionType
AX = mybir.AxisListType
F32 = mybir.dt.float32
BF16 = mybir.dt.bfloat16
U32 = mybir.dt.uint32
I32 = mybir.dt.int32

P = 128
D = 512
KC = D // P
NB = 4
S = 512
TT = S // P
EPS = 1e-5

H0 = 32
G0 = 8
HD0 = D // H0
R0 = H0 // G0
KV0 = G0 * HD0
KEEP = 128
TOP = 8
NEG = -3.0e38

INTER = 1376
FT = (INTER + P - 1) // P
GU_GROUPS = 4
DN_GROUPS = 10
TARGET = 124.0
WITHIN = 3.5
PACK = 8

H1 = 32
G1 = 8
R1 = H1 // G1
HD1 = 128
WIN = 64
NW = S // WIN
W1 = (R1 + 2) * HD1

E1 = 4
RK = 8


START = 4


def rows_of(f):
    return min(P, INTER - f * P)


def after(k, unit=1):
    return unit * k + START


class Place:

    def __init__(self, nc, ctx, prefix):
        self.nc, self.ctx, self.prefix = nc, ctx, prefix
        self.owned = []
        ctx.callback(self.release)

    def release(self):
        if self.owned:
            self.nc.clear_and_free_semaphores(self.owned)
            self.nc.all_engine_barrier()

    def sbuf(self, name, shape, dtype=F32):
        return self.ctx.enter_context(self.nc.sbuf_tensor(self.prefix + name, shape, dtype))

    def psum(self, name, shape, dtype=F32):
        return self.ctx.enter_context(self.nc.psum_tensor(self.prefix + name, shape, dtype))

    def sem(self, name):
        s = self.nc.alloc_semaphore(self.prefix + name)
        self.owned.append(s)
        return s

    def sems(self, name, n=2):
        return [self.sem(f"{name}{i}") for i in range(n)]


def bcast(ap, axis, n):
    v = ap.unsqueeze(axis)
    shape = list(v.shape)
    shape[axis] = n
    return v.broadcast_to(shape)


def wait_apart(eng, sem, value, passed):
    eng.wait_ge(sem, value)
    eng.sem_inc(passed, 1)


def start_ahead(eng, *groups):
    for g in groups:
        for s in (g if isinstance(g, list) else [g]):
            eng.sem_inc(s, START)




def dequantise(nc, a, w_gu, w_dn, space):
    CH = 512
    with ExitStack() as ctx:
        m = Place(nc, ctx, "dq_")
        words = space.bitcast(U32)[:, 0:4 * INTER].rearrange("p (s n) -> p s n", s=2)
        shift = m.sbuf("shift", [P, 1], U32)
        iota = m.sbuf("iota", [16, 1])
        gidx_i = m.sbuf("gidx_i", [16, D + INTER], I32)
        gidx = m.sbuf("gidx", [16, D + INTER])
        wrap = m.sbuf("wrap", [16, D + INTER])
        onehot = m.sbuf("onehot", [16, D + INTER])
        scale_gu = m.sbuf("scale_gu", [GU_GROUPS, 2 * INTER])
        scale_dn = m.sbuf("scale_dn", [DN_GROUPS, D])
        zw_gu = m.sbuf("zw_gu", [GU_GROUPS, 2 * INTER // PACK], U32)
        zw_dn = m.sbuf("zw_dn", [DN_GROUPS, D // PACK], U32)
        zi_gu = m.sbuf("zi_gu", [GU_GROUPS, 2 * INTER], U32)
        zi_dn = m.sbuf("zi_dn", [DN_GROUPS, D], U32)
        zero_gu = m.sbuf("zero_gu", [GU_GROUPS, 2 * INTER])
        zero_dn = m.sbuf("zero_dn", [DN_GROUPS, D])
        centred = m.sbuf("centred", [P, 2, CH])
        ps_scale = m.psum("ps_scale", [P, 2, CH])
        ps_zero = m.psum("ps_zero", [P, 2, CH])
        small_in = m.sem("small_in")
        words_in = m.sems("words_in")
        unpacked = m.sem("unpacked")
        prepared = m.sem("prepared")
        spread = m.sem("spread")
        centre_done = m.sem("centre_done")
        piece_done = m.sem("piece_done")

        chunks = [("gu", k, P) for k in range(KC)] + [("dn", f, rows_of(f)) for f in range(FT)]
        pieces = []
        for c, (kind, k, rows) in enumerate(chunks):
            width = 2 * INTER if kind == "gu" else D
            pieces += [(c, j, min(CH, width - j)) for j in range(0, width, CH)]

        block = ctx.enter_context(nc.Block())

        @block.sync
        def _(sp):
            sp.dma_start(gidx_i[0:GU_GROUPS, 0:D], a["g_idx_gu"].partition_broadcast(GU_GROUPS)).then_inc(small_in, 16)
            sp.dma_start(gidx_i[0:DN_GROUPS, D:], a["g_idx_dn"].partition_broadcast(DN_GROUPS)).then_inc(small_in, 16)
            for dst, src in ((shift, "shift"), (iota, "iota"), (scale_gu, "scales_gu"), (scale_dn, "scales_dn"),
                             (zw_gu, "qzeros_gu"), (zw_dn, "qzeros_dn")):
                sp.dma_start(dst[:], a[src]).then_inc(small_in, 16)
            for c, (kind, k, rows) in enumerate(chunks):
                if c >= 2:
                    sp.wait_ge(piece_done, max(n + 1 for n, p in enumerate(pieces) if p[0] == c - 2))
                width = 2 * INTER if kind == "gu" else D
                src = a["qw_gu"] if kind == "gu" else a["qw_dn"]
                sp.dma_start(words[0:rows, c % 2, 0:width], src[k * P:k * P + rows, :]).then_inc(words_in[c % 2], 16)

        @block.vector
        def _(dve):
            steps = [0]

            def step(ins):
                steps[0] += 1
                ins.then_inc(prepared, 1)

            def settle():
                dve.wait_ge(prepared, steps[0])

            dve.wait_ge(small_in, 16 * 8)
            for rows, cols, n in ((GU_GROUPS, slice(0, D), GU_GROUPS), (DN_GROUPS, slice(D, D + INTER), DN_GROUPS)):
                g, h, w = gidx[0:rows, cols], onehot[0:rows, cols], wrap[0:rows, cols]
                step(nc.vector.tensor_copy(g, gidx_i[0:rows, cols]))
                settle()
                step(nc.vector.tensor_scalar(w, g, 0.0, float(n), ALU.is_lt, ALU.mult))
                settle()
                step(nc.vector.tensor_tensor(g, g, w, ALU.add))
                settle()
                step(nc.vector.tensor_scalar(g, g, 0.0, float(n - 1), ALU.max, ALU.min))
                settle()
                step(nc.vector.tensor_scalar(h, g, iota[0:rows, 0:1], None, ALU.is_equal))
            for zw, zi, zero in ((zw_gu, zi_gu, zero_gu), (zw_dn, zi_dn, zero_dn)):
                v = zi[:].rearrange("p (c s) -> p c s", s=PACK)
                for s in range(PACK):
                    step(nc.vector.tensor_scalar(v[:, :, s], zw[:], 4 * s, 15,
                                                 ALU.logical_shift_right, ALU.bitwise_and))
                settle()
                step(nc.vector.tensor_scalar(zero[:], zi[:], 1.0, None, ALU.add))

            n = 0
            for c, (kind, k, rows) in enumerate(chunks):
                width = 2 * INTER if kind == "gu" else D
                dve.wait_ge(words_in[c % 2], 16 * (c // 2 + 1))
                u = words[0:rows, c % 2, 0:width]
                nc.vector.tensor_scalar(u, u, shift[0:rows, 0:1], 15, ALU.logical_shift_right,
                                        ALU.bitwise_and).then_inc(unpacked, 1)
                dve.wait_ge(unpacked, c + 1)
                while n < len(pieces) and pieces[n][0] == c:
                    _, j, w = pieces[n]
                    dst = w_gu[0:rows, k, j:j + w] if kind == "gu" else w_dn[0:rows, k, j:j + w]
                    dve.wait_ge(spread, n + 1)
                    nc.vector.tensor_tensor(centred[0:rows, n % 2, 0:w], words[0:rows, c % 2, j:j + w],
                                            ps_zero[0:rows, n % 2, 0:w], ALU.subtract).then_inc(centre_done, 1)
                    dve.wait_ge(centre_done, n + 1)
                    nc.vector.tensor_tensor(dst, centred[0:rows, n % 2, 0:w], ps_scale[0:rows, n % 2, 0:w],
                                            ALU.mult).then_inc(piece_done, 1)
                    n += 1

        @block.tensor
        def _(pe):
            pe.wait_ge(prepared, 2 * 5 + 2 * (PACK + 1))
            for n, (c, j, w) in enumerate(pieces):
                kind, k, rows = chunks[c]
                if n >= 2:
                    pe.wait_ge(piece_done, n - 1)
                if kind == "gu":
                    hot, sc, ze = onehot[0:GU_GROUPS, k * P:k * P + rows], scale_gu, zero_gu
                else:
                    hot, sc, ze = onehot[0:DN_GROUPS, D + k * P:D + k * P + rows], scale_dn, zero_dn
                nc.tensor.matmul(ps_scale[0:rows, n % 2, 0:w], hot, sc[:, j:j + w], start=True, stop=True)
                nc.tensor.matmul(ps_zero[0:rows, n % 2, 0:w], hot, ze[:, j:j + w], start=True,
                                 stop=True).then_inc(spread, 1)




def project_layer0(nc, a, ident, v_all, qT_dram, kT_dram):
    W = D + 2 * KV0
    with ExitStack() as ctx:
        m = Place(nc, ctx, "p0_")
        w = m.sbuf("w", [P, KC, W])
        rope = m.sbuf("rope", [P, TT, 4, HD0])
        xT = m.sbuf("xT", [P, 2, KC, P])
        cosed = m.sbuf("cosed", [P, 2, D + KV0])
        sined = m.sbuf("sined", [P, 2, D + KV0])
        roped = m.sbuf("roped", [P, 2, D + KV0])
        turned = m.sbuf("turned", [P, 2, KC + 1, P])
        ps_q = m.psum("ps_q", [P, 2, D])
        ps_kv = m.psum("ps_kv", [P, 2, 512])
        ps_t = m.psum("ps_t", [P, 2, 1024])
        weights_in = m.sem("weights_in")
        x_in = m.sems("x_in")
        projected = m.sems("projected")
        rotated = m.sems("rotated")
        summed = m.sems("summed")
        transposed = m.sems("transposed")
        evacuated = m.sems("evacuated")
        stored = m.sems("stored")

        block = ctx.enter_context(nc.Block())

        @block.sync
        def _(sp):
            for k in range(KC):
                sp.dma_start(w[:, k, :], a["wqkvT"][k * P:(k + 1) * P, :]).then_inc(weights_in, 16)
            sp.dma_start(rope[:], a["rope"]).then_inc(weights_in, 16)
            src = a["xT"].rearrange("(k p) (b t c) -> p k b t c", p=P, b=NB, t=TT)
            with sp.Fori(0, NB) as b:
                for t in range(TT):
                    sp.wait_ge(projected[t % 2], after(b * 2 + t // 2))
                    sp.dma_start(xT[:, t % 2, :, :], src[:, :, b, t, :]).then_inc(x_in[t % 2], 16)

        @block.tensor
        def _(pe):
            start_ahead(pe, projected, transposed)
            pe.wait_ge(weights_in, 16 * (KC + 1))

            def project(b, t):
                s, k2 = t % 2, b * 2 + t // 2
                pe.wait_ge(x_in[s], 16 * (k2 + 1))
                pe.wait_ge(rotated[s], after(k2))
                for k in range(KC):
                    nc.tensor.matmul(ps_q[:, s, :], xT[:, s, k, :], w[:, k, 0:D], start=(k == 0), stop=(k == KC - 1))
                for k in range(KC):
                    last = nc.tensor.matmul(ps_kv[:, s, 0:2 * KV0], xT[:, s, k, :], w[:, k, D:W],
                                            start=(k == 0), stop=(k == KC - 1))
                last.then_inc(projected[s], 1)

            def transpose(b, t):
                s, k2 = t % 2, b * 2 + t // 2
                pe.wait_ge(summed[s], after(k2 + 1))
                pe.wait_ge(evacuated[s], after(k2))
                for c in range(KC + 1):
                    last = nc.tensor.transpose(ps_t[:, s, c * P:(c + 1) * P], roped[:, s, c * P:(c + 1) * P], ident[:])
                last.then_inc(transposed[s], 1)

            with pe.Fori(0, NB) as b:
                for t in range(TT + 1):
                    if t < TT:
                        project(b, t)
                    if t >= 1:
                        transpose(b, t - 1)

        @block.vector
        def _(dve):
            start_ahead(dve, rotated)
            dve.wait_ge(weights_in, 16 * (KC + 1))
            half = HD0 // 2
            with dve.Fori(0, NB) as b:
                for t in range(TT):
                    s, k2 = t % 2, b * 2 + t // 2
                    dve.wait_ge(projected[s], after(k2 + 1))
                    dve.wait_ge(summed[s], after(k2))
                    for src, lo, heads, cos in ((ps_q[:, s, :], 0, H0, 0), (ps_kv[:, s, 0:KV0], D, G0, 2)):
                        width = heads * HD0
                        x = src.rearrange("p (h d) -> p h d", d=HD0)
                        c_out = cosed[:, s, lo:lo + width].rearrange("p (h d) -> p h d", d=HD0)
                        s_out = sined[:, s, lo:lo + width].rearrange("p (h d) -> p h d", d=HD0)
                        nc.vector.tensor_tensor(c_out, x, bcast(rope[:, t, cos, :], 1, heads), ALU.mult)
                        nc.vector.tensor_tensor(s_out[:, :, 0:half], x[:, :, half:],
                                                bcast(rope[:, t, cos + 1, 0:half], 1, heads), ALU.mult)
                        last = nc.vector.tensor_tensor(s_out[:, :, half:], x[:, :, 0:half],
                                                       bcast(rope[:, t, cos + 1, half:], 1, heads), ALU.mult)
                    last = nc.vector.tensor_copy(v_all[:, b, :, t, :], ps_kv[:, s, KV0:2 * KV0]
                                                 .rearrange("p (g d) -> p g d", d=HD0))
                    last.then_inc(rotated[s], 1)

        @block.gpsimd
        def _(pool):
            start_ahead(pool, summed)
            with pool.Fori(0, NB) as b:
                for t in range(TT):
                    s, k2 = t % 2, b * 2 + t // 2
                    pool.wait_ge(rotated[s], after(k2 + 1))
                    pool.wait_ge(transposed[s], after(k2))
                    nc.gpsimd.tensor_tensor(roped[:, s, :], cosed[:, s, :], sined[:, s, :], ALU.add)\
                        .then_inc(summed[s], 1)

        @block.scalar
        def _(act):
            start_ahead(act, evacuated, stored)

            def evacuate(b, t):
                s, k2 = t % 2, b * 2 + t // 2
                act.wait_ge(transposed[s], after(k2 + 1))
                act.wait_ge(stored[s], after(k2, 32))
                nc.scalar.activation(turned[:, s, :, :], ps_t[:, s, 0:(KC + 1) * P]
                                     .rearrange("p (k c) -> p k c", c=P), ACT.Copy).then_inc(evacuated[s], 1)
                act.wait_ge(evacuated[s], after(k2 + 1))
                dst = qT_dram.rearrange("(b k p) (t c) -> b t p k c", b=NB, k=KC, t=TT)
                act.dma_start(dst[b, t], turned[:, s, 0:KC, :]).then_inc(stored[s], 16)
                dst = kT_dram.rearrange("(b p) (t c) -> b t p c", b=NB, t=TT)
                act.dma_start(dst[b, t], turned[:, s, KC, :]).then_inc(stored[s], 16)

            with act.Fori(0, NB) as b:
                for t in range(TT):
                    evacuate(b, t)
            for s in range(2):
                act.wait_ge(stored[s], after(NB * 2, 32))




def attend_layer0(nc, a, ident, ident16, v_all, qT_dram, kT_dram, o_all, work):
    PAIRS = NB * G0
    UNITS = 2 * TT
    TURNS = PAIRS // 2
    CHUNKS = TT * (TT + 1) // 2
    ROUNDS = KEEP // TOP
    SEARCHED = 2 * (TT - 1)
    SLOTS = 4
    AHEAD = 3
    with ExitStack() as ctx:
        m = Place(nc, ctx, "a0_")
        qT = m.sbuf("qT", [P, 2, S])
        kT = m.sbuf("kT", [P, 2, S])
        mask32 = m.sbuf("mask32", [P, P])
        mask = m.sbuf("mask", [P, P], BF16)
        exps = work
        scores_sb = m.sbuf("scores", [P, SLOTS, R0, S])
        junk = m.sbuf("junk", [P, 2, R0, S], BF16)
        junk_act = m.sbuf("junk_act", [P, R0, S], BF16)
        guess = m.sbuf("guess", [P, TT, 2])
        half = m.sbuf("half", [P, R0])
        iota = m.sbuf("iota", [P, R0, TOP])
        nmax = m.sbuf("nmax", [P, SLOTS, R0])
        stats = m.sbuf("stats", [P, SLOTS, R0, 6])
        thr = m.sbuf("thr", [P, SLOTS, R0])
        slope = m.sbuf("slope", [P, SLOTS, R0])
        count = m.sbuf("count", [P, SLOTS, 5, R0])
        error = m.sbuf("error", [P, SLOTS, 2, R0])
        tmp = m.sbuf("tmp", [P, 5, 4, R0])
        missing = m.sbuf("missing", [P, R0])
        top = m.sbuf("top", [P, R0, TOP + 1])
        hot = m.sbuf("hot", [P, R0, TOP])
        picked = m.sbuf("picked", [P, R0, 2, TOP])
        bound = m.sbuf("bound", [P, R0, 2])
        unsure = m.sbuf("unsure", [P, R0])
        unsure_sum = m.sbuf("unsure_sum", [P, 1])
        unsure_all = m.sbuf("unsure_all", [P, 1])
        unsure_int = m.sbuf("unsure_int", [P, 1], I32)
        rsum = m.sbuf("rsum", [P, SLOTS, R0])
        rinv = m.sbuf("rinv", [P, SLOTS, R0])
        pT = m.sbuf("pT", [P, 2, R0 * P])
        ps_s = m.psum("ps_s", [P, R0, S])
        ps_t = m.psum("ps_t", [P, 2, R0 * P])
        ps_o = m.psum("ps_o", [P, 2, 512])
        consts_in = m.sem("consts_in")
        consts_ready = m.sem("consts_ready")
        heads_in = m.sems("heads_in")
        scored = m.sem("scored")
        stated = m.sem("stated")
        copied = m.sem("copied")
        exped = m.sem("exped")
        moved = m.sems("moved", 5)
        counted_dve = m.sem("counted_dve")
        counted_act = m.sem("counted_act")
        step_done = m.sem("step_done")
        rated = m.sem("rated")
        chained = m.sem("chained")
        reduced = m.sem("reduced")
        flagged = m.sem("flagged")
        passed = m.sem("passed")
        pool_passed = m.sem("pool_passed")
        kept = m.sem("kept")
        turned = m.sems("turned")
        pT_out = m.sems("pT_out")
        attended = m.sems("attended")
        scaled = m.sem("scaled")

        block = ctx.enter_context(nc.Block())

        def chunk(ii, u, kb):
            local = (u // TT) * CHUNKS + (u % TT) * (u % TT + 1) // 2 + kb
            return local % 2, ii * CHUNKS + local // 2

        def searched(ii, u):
            return ii * SEARCHED + (u // TT) * (TT - 1) + u % TT - 1

        def turns(eng, step):

            def run(ii, u, last):
                def has(stage, ahead):
                    v = u + ahead
                    if v < 0 or (last and v >= UNITS):
                        return
                    if v >= UNITS:
                        stage(ii + 1, v - UNITS)
                    else:
                        stage(ii, v)
                step(has)

            for u in range(-AHEAD, 0):
                run(0, u, False)
            with eng.Fori(0, TURNS - 1) as ii:
                for u in range(UNITS):
                    run(ii, u, False)
            for u in range(UNITS):
                run(TURNS - 1, u, True)

        @block.sync
        def _(sp):
            for dst, src in ((mask32, "causal"), (guess, "guess"), (iota, "iota8")):
                sp.dma_start(dst[:], a[src]).then_inc(consts_in, 16)

            def load(i, s):
                for j in range(R0):
                    sp.dma_start(qT[32 * j:32 * j + HD0, s, :],
                                 qT_dram[bass.ds(i * (R0 * HD0) + j * HD0, HD0), :]).then_inc(heads_in[s], 16)
                    sp.dma_start(kT[32 * j:32 * j + HD0, s, :],
                                 kT_dram[bass.ds(i * HD0, HD0), :]).then_inc(heads_in[s], 16)

            load(0, 0)
            load(1, 1)
            with sp.Fori(1, TURNS) as ii:
                for s in range(2):
                    sp.wait_ge(scored, (ii - 1) * UNITS + (s + 1) * TT)
                    load(ii * 2 + s, s)

        @block.tensor
        def _(pe):
            start_ahead(pe, *attended)
            pe.wait_ge(consts_ready, 4)

            def scores(ii, u):
                s, qt = u // TT, u % TT
                n = ii * UNITS + u
                L = (qt + 1) * P
                if qt == 0:
                    pe.wait_ge(heads_in[s], 16 * 2 * R0 * (ii + 1))
                pe.wait_ge(exped, after(n))
                for j in range(R0):
                    nc.tensor.matmul(ps_s[:, j, 0:L], qT[32 * j:32 * j + HD0, s, qt * P:(qt + 1) * P],
                                     kT[32 * j:32 * j + HD0, s, 0:L], start=True, stop=False)
                for j in range(R0):
                    last = nc.tensor.matmul(ps_s[:, j, L - P:L], ident16[:], mask[:], start=False, stop=True)
                last.then_inc(scored, 1)

            def values(ii, u):
                s, slot, qt, i = u % 2, u % SLOTS, u % TT, ii * 2 + u // TT
                n = ii * UNITS + u
                probs = exps if qt == 0 else scores_sb
                pe.wait_ge(kept, n + 1)
                pe.wait_ge(scaled, after(n - 1))

                def attend(kb):
                    bank, c = chunk(ii, u, kb)
                    pe.wait_ge(pT_out[bank], after(c + 1))
                    for j in range(R0):
                        last = nc.tensor.matmul(ps_o[:, s, j * HD0:(j + 1) * HD0], pT[:, bank, j * P:(j + 1) * P],
                                                v_all[:, i, kb, :], start=(kb == 0 and j == 0),
                                                stop=(kb == qt), skip_group_check=True)
                    last.then_inc(attended[bank], 1)

                for kb in range(qt + 1):
                    bank, c = chunk(ii, u, kb)
                    pe.wait_ge(pT_out[bank], after(c))
                    for j in range(R0):
                        last = nc.tensor.transpose(ps_t[:, bank, j * P:(j + 1) * P],
                                                   probs[:, slot, j, kb * P:(kb + 1) * P], ident[:])
                    last.then_inc(turned[bank], 1)
                    if kb >= 1:
                        attend(kb - 1)
                attend(qt)

            def step(has):
                has(scores, 3)
                has(values, 0)

            turns(pe, step)

        @block.vector
        def _(dve):
            def statistics(ii, u):
                slot, qt, n = u % SLOTS, u % TT, ii * UNITS + u
                dve.wait_ge(scored, n + 1)
                dve.wait_ge(scaled, after(n - 3))
                last = nc.vector.tensor_reduce(nmax[:, slot, :], ps_s[:, :, 0:(qt + 1) * P], AX.X, ALU.max, negate=True)
                for j in range(R0 if qt >= 1 else 0):
                    last = nc.vector.bn_stats(stats[:, slot, j, :], ps_s[:, j, 0:qt * P])
                last.then_inc(stated, 1)

            def count_scores(ii, u, c):
                slot, L = u % SLOTS, (u % TT + 1) * P
                for j in range(R0):
                    last = nc.vector.tensor_scalar(junk[:, c // 4, j, 0:L], scores_sb[:, slot, j, 0:L], thr[:, slot, j:j + 1], None,
                                                   ALU.is_ge, ALU.add, accum_out=count[:, slot, c, j:j + 1])
                return last

            def first_count(ii, u):
                if u % TT == 0:
                    return
                k = searched(ii, u)
                dve.wait_ge(copied, k + 1)
                dve.wait_ge(moved[0], k + 1)
                count_scores(ii, u, 0).then_inc(counted_dve, 1)

            def select(ii, u):
                slot, qt, n = u % SLOTS, u % TT, ii * UNITS + u
                L = (qt + 1) * P
                done = [0]

                def settle(last):
                    done[0] += 1
                    last.then_inc(step_done, 1)
                    dve.wait_ge(step_done, done[0])

                if qt == 0:
                    dve.wait_ge(exped, after(n + 1))
                    nc.vector.reciprocal(rinv[:, slot, :], rsum[:, slot, :]).then_inc(kept, 1)
                    return
                k = searched(ii, u)
                dve.sem_clear(step_done)
                wait_apart(dve, exped, after(n + 1), passed)
                dve.wait_ge(moved[4], k + 1)
                last = count_scores(ii, u, 4)
                settle(last)
                nc.vector.tensor_scalar(missing[:], count[:, slot, 4, :], -1.0, float(KEEP), ALU.mult, ALU.add)
                for j in range(R0):
                    row = scores_sb[:, slot, j, 0:L]
                    last = nc.vector.scalar_tensor_tensor(out=row, in0=row, scalar=thr[:, slot, j:j + 1],
                                                          in1=exps[:, slot, j, 0:L], op0=ALU.is_lt, op1=ALU.mult)
                settle(last)
                for j in range(R0):
                    nc.vector.max(top[:, j, 1:TOP + 1], scores_sb[:, slot, j, 0:L])
                last = nc.vector.tensor_tensor(hot[:], iota[:], bcast(missing[:], 2, TOP), ALU.is_equal)
                settle(last)
                for side in range(2):
                    last = nc.vector.tensor_tensor(picked[:, :, side, :], hot[:], top[:, :, side:side + TOP], ALU.mult)
                settle(last)
                settle(nc.vector.tensor_reduce(bound[:], picked[:], AX.X, ALU.add))
                nc.vector.scalar_tensor_tensor(out=unsure[:], in0=bound[:, :, 0], scalar=1.0, in1=bound[:, :, 1],
                                               op0=ALU.mult, op1=ALU.is_le,
                                               accum_out=unsure_sum[:]).then_inc(rated, 1)
                for j in range(R0):
                    row = exps[:, slot, j, 0:L]
                    last = nc.vector.scalar_tensor_tensor(out=scores_sb[:, slot, j, 0:L], in0=row,
                                                          scalar=bound[:, j, 1:2], in1=row, op0=ALU.is_gt,
                                                          op1=ALU.mult, accum_out=rsum[:, slot, j:j + 1])
                settle(last)

            def select_again(slot, L):
                rest = scores_sb
                done = 0
                dve.sem_clear(step_done)
                for r in range(ROUNDS):
                    if r >= 1:
                        dve.wait_ge(step_done, done)
                    src = exps if r == 0 else rest
                    for j in range(R0):
                        last = nc.vector.max(top[:, j, 1:TOP + 1], src[:, slot, j, 0:L])
                    last.then_inc(step_done, 1)
                    dve.wait_ge(step_done, done + 1)
                    for j in range(R0):
                        last = nc.vector.match_replace(rest[:, slot, j, 0:L], top[:, j, 1:TOP + 1],
                                                       src[:, slot, j, 0:L], 0.0)
                    last.then_inc(step_done, 1)
                    done += 2
                dve.wait_ge(step_done, done)
                for j in range(R0):
                    last = nc.vector.scalar_tensor_tensor(
                        out=rest[:, slot, j, 0:L], in0=exps[:, slot, j, 0:L], scalar=1.0, in1=rest[:, slot, j, 0:L],
                        op0=ALU.mult, op1=ALU.subtract, accum_out=rsum[:, slot, j:j + 1])
                last.then_inc(step_done, 1)
                dve.wait_ge(step_done, done + 1)

            def finish(ii, u):
                slot, qt = u % SLOTS, u % TT
                if qt == 0:
                    return
                wait_apart(dve, flagged, searched(ii, u) + 1, passed)
                rows = dve.value_load(unsure_int[0:1, 0:1])
                with dve.If(rows > 0):
                    select_again(slot, (qt + 1) * P)
                nc.vector.reciprocal(rinv[:, slot, :], rsum[:, slot, :]).then_inc(kept, 1)

            def step(has):
                has(statistics, 3)
                has(select, 1)
                has(first_count, 3)
                has(finish, 1)

            dve.wait_ge(consts_ready, 4)
            turns(dve, step)

        @block.gpsimd
        def _(pool):
            t = nc.gpsimd
            pool.wait_ge(consts_in, 48)
            t.tensor_copy(mask[:], mask32[:]).then_inc(consts_ready, 1)
            t.memset(half[:], 0.5).then_inc(consts_ready, 1)
            t.memset(top[:], 0.0).then_inc(consts_ready, 1)
            t.memset(tmp[:], 0.0).then_inc(consts_ready, 1)

            def chain():
                pool.sem_clear(chained)
                done = [0]

                def settle(last):
                    done[0] += 1
                    last.then_inc(chained, 1)
                    pool.wait_ge(chained, done[0])

                return settle

            def first_guess(ii, u):
                slot, qt = u % SLOTS, u % TT
                if qt == 0:
                    return
                wait_apart(pool, stated, ii * UNITS + u + 1, pool_passed)
                st = stats[:, slot, :, :]
                settle = chain()
                var, dev, mean, sd = (tmp[:, 0, x, :] for x in range(4))
                t.tensor_tensor(dev, st[:, :, 1], st[:, :, 4], ALU.subtract)
                t.tensor_tensor(var, st[:, :, 2], st[:, :, 5], ALU.add)
                settle(t.tensor_tensor(mean, st[:, :, 1], st[:, :, 4], ALU.add))
                t.tensor_tensor(dev, dev, dev, ALU.mult)
                t.tensor_scalar(mean, mean, 0.5, 0.0, ALU.mult, ALU.add)
                settle(t.tensor_scalar(var, var, 4.0 / (qt * P), 0.0, ALU.mult, ALU.add))
                settle(t.tensor_tensor(var, var, dev, ALU.add))
                settle(t.tensor_tensor(sd, var, half[:], ALU.pow))
                t.tensor_scalar(slope[:, slot, :], sd, guess[:, qt, 1:2], None, ALU.mult)
                settle(t.tensor_scalar(sd, sd, guess[:, qt, 0:1], None, ALU.mult))
                t.tensor_tensor(thr[:, slot, :], sd, mean, ALU.add).then_inc(moved[0], 1)

            def move(c, sem, per_item):
                def stage(ii, u):
                    slot, qt = u % SLOTS, u % TT
                    if qt == 0:
                        return
                    k = searched(ii, u)
                    L = (qt + 1) * P
                    wait_apart(pool, sem, k * per_item + (c if per_item > 1 else 1), pool_passed)
                    new, old = error[:, slot, c % 2, :], error[:, slot, (c + 1) % 2, :]
                    settle = chain()
                    by, turn, more, outside = (tmp[:, c + 1, x, :] for x in range(4))
                    rate = slope[:, slot, :]
                    if c == 0:
                        settle(t.tensor_scalar(new, count[:, slot, c, :], 1.0, -TARGET, ALU.mult, ALU.add))
                        settle(t.tensor_tensor(by, new, rate, ALU.mult))
                    else:
                        settle(t.tensor_scalar(new, count[:, slot, c, :], -0.5, L / 2 - TARGET, ALU.mult, ALU.add))
                        t.tensor_tensor(by, new, rate, ALU.mult)
                        t.tensor_tensor(outside, new, new, ALU.mult)
                        settle(t.tensor_tensor(turn, new, old, ALU.mult))
                        t.tensor_scalar(outside, outside, WITHIN * WITHIN, 1.0, ALU.is_gt, ALU.mult)
                        settle(t.tensor_scalar(turn, turn, 0.0, -0.5, ALU.is_lt, ALU.mult))
                        settle(t.tensor_tensor(by, by, outside, ALU.mult))
                        t.tensor_tensor(more, by, turn, ALU.mult)
                        settle(t.tensor_tensor(turn, rate, turn, ALU.mult))
                        t.tensor_tensor(rate, rate, turn, ALU.add)
                        settle(t.tensor_tensor(by, by, more, ALU.add))
                    t.tensor_tensor(thr[:, slot, :], thr[:, slot, :], by, ALU.add).then_inc(moved[c + 1], 1)
                return stage

            def flag(ii, u):
                if u % TT == 0:
                    return
                k = searched(ii, u)
                wait_apart(pool, rated, k + 1, pool_passed)
                t.partition_all_reduce(unsure_all[:], unsure_sum[:], P, bass.bass_isa.ReduceOp.add)\
                    .then_inc(reduced, 1)
                wait_apart(pool, reduced, k + 1, pool_passed)
                t.tensor_copy(unsure_int[:], unsure_all[:]).then_inc(flagged, 1)

            def step(has):
                has(move(1, counted_act, 3), 2)
                has(first_guess, 3)
                has(move(2, counted_act, 3), 2)
                has(flag, 1)
                has(move(3, counted_act, 3), 2)
                has(move(0, counted_dve, 1), 3)

            turns(pool, step)

        @block.scalar
        def _(act):
            start_ahead(act, exped, pT_out, scaled)

            def exponentials(ii, u):
                slot, qt, n = u % SLOTS, u % TT, ii * UNITS + u
                L = (qt + 1) * P
                act.wait_ge(stated, n + 1)
                if qt >= 1:
                    nc.scalar.activation(scores_sb[:, slot, :, 0:L], ps_s[:, :, 0:L], ACT.Copy).then_inc(copied, 1)
                for j in range(R0):
                    sums = {"accum_out": rsum[:, slot, j:j + 1]} if qt == 0 else {}
                    last = nc.scalar.activation(exps[:, slot, j, 0:L], ps_s[:, j, 0:L], ACT.Exp,
                                                bias=nmax[:, slot, j:j + 1], **sums)
                last.then_inc(exped, 1)

            def count_scores(c):
                def stage(ii, u):
                    slot, qt = u % SLOTS, u % TT
                    if qt == 0:
                        return
                    L = (qt + 1) * P
                    act.wait_ge(moved[c], searched(ii, u) + 1)
                    for j in range(R0):
                        last = nc.scalar.activation(junk_act[:, j, 0:L], scores_sb[:, slot, j, 0:L], ACT.Sign,
                                                    bias=thr[:, slot, j:j + 1], scale=-1.0,
                                                    accum_out=count[:, slot, c, j:j + 1])
                    last.then_inc(counted_act, 1)
                return stage

            def probs_out(ii, u):
                for kb in range(u % TT + 1):
                    bank, c = chunk(ii, u, kb)
                    act.wait_ge(turned[bank], c + 1)
                    act.wait_ge(attended[bank], after(c))
                    nc.scalar.activation(pT[:, bank, :], ps_t[:, bank, :], ACT.Copy).then_inc(pT_out[bank], 1)

            def output(ii, u):
                s, slot, qt, i = u % 2, u % SLOTS, u % TT, ii * 2 + u // TT
                bank, c = chunk(ii, u, qt)
                act.wait_ge(attended[bank], after(c + 1))
                act.wait_ge(kept, ii * UNITS + u + 1)
                for j in range(R0):
                    last = nc.scalar.activation(o_all[:, i, qt, j * HD0:(j + 1) * HD0],
                                                ps_o[:, s, j * HD0:(j + 1) * HD0], ACT.Copy,
                                                scale=rinv[:, slot, j:j + 1])
                last.then_inc(scaled, 1)

            def step(has):
                has(count_scores(1), 2)
                has(probs_out, 0)
                has(count_scores(2), 2)
                has(exponentials, 3)
                has(count_scores(3), 2)
                has(output, 0)

            turns(act, step)




class Norm:

    def __init__(self, m):
        self.res = m.sbuf("res", [P, 2, D])
        self.xn = m.sbuf("xn", [P, 2, D])
        self.stats = m.sbuf("stats", [P, 2, 6])
        self.mv = m.sbuf("mv", [P, 2, 2])
        self.sd = m.sbuf("sd", [P, 2, 1])
        self.rstd = m.sbuf("rstd", [P, 2, 1])
        self.summed = m.sems("n_summed")
        self.stated = m.sems("n_stated")
        self.meaned = m.sems("n_meaned")
        self.rooted = m.sems("n_rooted")
        self.inverted = m.sems("n_inverted")
        self.normed = m.sems("n_normed")
        self.passed = m.sem("n_passed")
        self.pool_passed = m.sem("n_pool_passed")

    def on_dve(self, nc, dve, s, k2, out=None):
        out = self.xn[:, s, :] if out is None else out
        dve.wait_ge(self.summed[s], after(k2 + 1))
        nc.vector.bn_stats(self.stats[:, s, :], self.res[:, s, :]).then_inc(self.stated[s], 1)
        wait_apart(dve, self.stated[s], k2 + 1, self.passed)
        nc.vector.bn_aggr(self.mv[:, s, :], self.stats[:, s, :]).then_inc(self.meaned[s], 1)
        dve.wait_ge(self.rooted[s], k2 + 1)
        nc.vector.reciprocal(self.rstd[:, s, :], self.sd[:, s, :]).then_inc(self.inverted[s], 1)
        dve.wait_ge(self.inverted[s], k2 + 1)
        nc.vector.tensor_scalar(out, self.res[:, s, :], self.mv[:, s, 0:1], self.rstd[:, s, :],
                                ALU.subtract, ALU.mult).then_inc(self.normed[s], 1)

    def on_act(self, nc, act, s, k2, eps):
        act.wait_ge(self.meaned[s], k2 + 1)
        nc.scalar.activation(self.sd[:, s, :], self.mv[:, s, 1:2], ACT.Sqrt, bias=eps[:, 0:1])\
            .then_inc(self.rooted[s], 1)




def project_out0(nc, a, ident, eps, x_all, xT_all):
    with ExitStack() as ctx:
        m = Place(nc, ctx, "o0_")
        w = m.sbuf("w", [P, KC, D])
        rows = m.sbuf("rows", [P, TT, D])
        rowsT = m.sbuf("rowsT", [P, 2, D])
        x = m.sbuf("x", [P, 2, D])
        norm = Norm(m)
        ps_t = m.psum("ps_t", [P, 2, D])
        ps_y = m.psum("ps_y", [P, 2, D])
        ps_n = m.psum("ps_n", [P, 2, D])
        w_in = m.sem("w_in")
        x_in = m.sems("x_in")
        gathered = m.sem("gathered")
        batch_turned = m.sem("batch_turned")
        turned = m.sems("turned")
        rowsT_out = m.sems("rowsT_out")
        projected = m.sems("projected")
        copied = m.sems("copied")
        xn_turned = m.sems("xn_turned")
        xT_out = m.sems("xT_out")

        block = ctx.enter_context(nc.Block())
        o_view = x_all[:].rearrange("p b (g t c) -> p b t g c", g=G0, t=TT)
        x_view = x_all[:].rearrange("p b (t c) -> p b t c", t=TT)

        @block.sync
        def _(sp):
            sp.dma_start(w[:], a["wo0T"].rearrange("(k p) n -> p k n", p=P)).then_inc(w_in, 16)
            src = a["x"].rearrange("(b t p) n -> b t p n", b=NB, t=TT)
            with sp.Fori(0, NB) as b:
                for t in range(TT):
                    s, k2 = t % 2, b * 2 + t // 2
                    sp.wait_ge(norm.summed[s], after(k2))
                    sp.dma_start(x[:, s, :], src[b, t]).then_inc(x_in[s], 16)

        @block.gpsimd
        def _(pool):
            start_ahead(pool, copied)
            with pool.Fori(0, NB) as b:
                wait_apart(pool, batch_turned, after(b), norm.pool_passed)
                for t in range(TT):
                    nc.gpsimd.tensor_copy(rows[:, t, :].rearrange("p (g c) -> p g c", g=G0),
                                          o_view[:, b, t, :, :]).then_inc(gathered, 1)
                pool.wait_ge(gathered, b * TT + TT)
                for t in range(TT):
                    s, k2 = t % 2, b * 2 + t // 2
                    wait_apart(pool, norm.normed[s], after(k2 + 1), norm.pool_passed)
                    nc.gpsimd.tensor_copy(x_view[:, b, t, :], norm.xn[:, s, :]).then_inc(copied[s], 1)

        @block.tensor
        def _(pe):
            start_ahead(pe, batch_turned, turned, projected, xn_turned)
            pe.wait_ge(w_in, 16)
            with pe.Fori(0, NB) as b:
                for t in range(TT + 1):
                    if t < TT:
                        s, k2 = t % 2, b * 2 + t // 2
                        pe.wait_ge(gathered, b * TT + t + 1)
                        pe.wait_ge(rowsT_out[s], after(k2))
                        for k in range(KC):
                            last = nc.tensor.transpose(ps_t[:, s, k * P:(k + 1) * P], rows[:, t, k * P:(k + 1) * P],
                                                       ident[:])
                        last.then_inc(turned[s], 1)
                        pe.wait_ge(rowsT_out[s], after(k2 + 1))
                        pe.wait_ge(norm.summed[s], after(k2))
                        for k in range(KC):
                            last = nc.tensor.matmul(ps_y[:, s, :], rowsT[:, s, k * P:(k + 1) * P], w[:, k, :],
                                                    start=(k == 0), stop=(k == KC - 1))
                        last.then_inc(projected[s], 1)
                    if t == TT - 1:
                        pe.wait_ge(turned[1], after(b * 2 + 2))
                        pe.sem_inc(batch_turned, 1)
                    if t >= 1:
                        transpose_rows(nc, pe, ident, norm, (t - 1) % 2, b * 2 + (t - 1) // 2, ps_n, xn_turned, xT_out)

        @block.scalar
        def _(act):
            start_ahead(act, rowsT_out, xT_out)
            with act.Fori(0, NB) as b:
                for t in range(TT + 1):
                    if t < TT:
                        s, k2 = t % 2, b * 2 + t // 2
                        act.wait_ge(turned[s], after(k2 + 1))
                        act.wait_ge(projected[s], after(k2))
                        nc.scalar.activation(rowsT[:, s, :], ps_t[:, s, :], ACT.Copy).then_inc(rowsT_out[s], 1)
                    if t >= 1:
                        s, k2 = (t - 1) % 2, b * 2 + (t - 1) // 2
                        norm.on_act(nc, act, s, k2, eps)
                        act.wait_ge(xn_turned[s], after(k2 + 1))
                        nc.scalar.activation(xT_all[:, :, b, (t - 1) * P:t * P],
                                             ps_n[:, s, :].rearrange("p (k c) -> p k c", k=KC), ACT.Copy)\
                            .then_inc(xT_out[s], 1)

        @block.vector
        def _(dve):
            start_ahead(dve, norm.summed, norm.normed)
            with dve.Fori(0, NB) as b:
                for t in range(TT):
                    s, k2 = t % 2, b * 2 + t // 2
                    dve.wait_ge(projected[s], after(k2 + 1))
                    dve.wait_ge(x_in[s], 16 * (k2 + 1))
                    nc.vector.tensor_tensor(norm.res[:, s, :], ps_y[:, s, :], x[:, s, :], ALU.add)\
                        .then_inc(norm.summed[s], 1)
                    dve.wait_ge(copied[s], after(k2))
                    dve.wait_ge(xn_turned[s], after(k2))
                    norm.on_dve(nc, dve, s, k2)


def transpose_rows(nc, pe, ident, norm, s, k2, ps, turned, out):
    pe.wait_ge(norm.normed[s], after(k2 + 1))
    pe.wait_ge(out[s], after(k2))
    for k in range(KC):
        last = nc.tensor.transpose(ps[:, s, k * P:(k + 1) * P], norm.xn[:, s, k * P:(k + 1) * P], ident[:])
    last.then_inc(turned[s], 1)




def feed_forward0(nc, a, ident, eps, x_all, xT_all, w_gu, w_dn):
    USES = [(FT + 1 - f) // 2 for f in range(2)]
    with ExitStack() as ctx:
        m = Place(nc, ctx, "f0_")
        hT = m.sbuf("hT", [P, FT, S])
        silu = m.sbuf("silu", [P, 2, S])
        norm = Norm(m)
        ps_g = m.psum("ps_g", [P, 2, S])
        ps_u = m.psum("ps_u", [P, 2, S])
        ps_y = m.psum("ps_y", [P, 2, D])
        ps_n = m.psum("ps_n", [P, 2, D])
        up_done = m.sems("up_done")
        silu_done = m.sems("silu_done")
        gated = m.sems("gated")
        projected = m.sems("projected")
        copied = m.sems("copied")
        xn_turned = m.sems("xn_turned")
        xT_out = m.sems("xT_out")

        block = ctx.enter_context(nc.Block())
        x_view = x_all[:].rearrange("p b (t c) -> p b t c", t=TT)

        @block.tensor
        def _(pe):
            start_ahead(pe, projected, xn_turned)
            with pe.Fori(0, NB) as b:
                for f in range(FT):
                    s, c, r = f % 2, b * USES[f % 2] + f // 2, rows_of(f)
                    pe.wait_ge(gated[s], after(c))
                    for ps, col in ((ps_g, f * P), (ps_u, INTER + f * P)):
                        for k in range(KC):
                            last = nc.tensor.matmul(ps[0:r, s, :], w_gu[:, k, col:col + r], xT_all[:, k, b, :],
                                                    start=(k == 0), stop=(k == KC - 1))
                    last.then_inc(up_done[s], 1)
                for s in range(2):
                    pe.wait_ge(gated[s], after((b + 1) * USES[s]))
                for t in range(TT + 1):
                    if t < TT:
                        s, k2 = t % 2, b * 2 + t // 2
                        pe.wait_ge(norm.summed[s], after(k2))
                        for f in range(FT):
                            last = nc.tensor.matmul(ps_y[:, s, :], hT[0:rows_of(f), f, t * P:(t + 1) * P],
                                                    w_dn[0:rows_of(f), f, :], start=(f == 0), stop=(f == FT - 1))
                        last.then_inc(projected[s], 1)
                    if t >= 1:
                        transpose_rows(nc, pe, ident, norm, (t - 1) % 2, b * 2 + (t - 1) // 2, ps_n, xn_turned, xT_out)

        @block.scalar
        def _(act):
            start_ahead(act, xT_out)
            with act.Fori(0, NB) as b:
                for f in range(FT):
                    s, c, r = f % 2, b * USES[f % 2] + f // 2, rows_of(f)
                    act.wait_ge(up_done[s], c + 1)
                    act.wait_ge(gated[s], after(c))
                    nc.scalar.activation(silu[0:r, s, :], ps_g[0:r, s, :], ACT.Silu).then_inc(silu_done[s], 1)
                for t in range(TT):
                    s, k2 = t % 2, b * 2 + t // 2
                    norm.on_act(nc, act, s, k2, eps)
                    act.wait_ge(xn_turned[s], after(k2 + 1))
                    nc.scalar.activation(xT_all[:, :, b, t * P:(t + 1) * P],
                                         ps_n[:, s, :].rearrange("p (k c) -> p k c", k=KC), ACT.Copy)\
                        .then_inc(xT_out[s], 1)

        @block.vector
        def _(dve):
            start_ahead(dve, gated, norm.summed, norm.normed)
            with dve.Fori(0, NB) as b:
                for f in range(FT):
                    s, c, r = f % 2, b * USES[f % 2] + f // 2, rows_of(f)
                    dve.wait_ge(silu_done[s], c + 1)
                    nc.vector.tensor_tensor(hT[0:r, f, :], ps_u[0:r, s, :], silu[0:r, s, :], ALU.mult)\
                        .then_inc(gated[s], 1)
                for t in range(TT):
                    s, k2 = t % 2, b * 2 + t // 2
                    dve.wait_ge(projected[s], after(k2 + 1))
                    nc.vector.tensor_tensor(norm.res[:, s, :], ps_y[:, s, :], x_view[:, b, t, :], ALU.add)\
                        .then_inc(norm.summed[s], 1)
                    dve.wait_ge(copied[s], after(k2))
                    dve.wait_ge(xn_turned[s], after(k2))
                    norm.on_dve(nc, dve, s, k2)

        @block.gpsimd
        def _(pool):
            start_ahead(pool, copied)
            with pool.Fori(0, NB) as b:
                for t in range(TT):
                    s, k2 = t % 2, b * 2 + t // 2
                    wait_apart(pool, norm.normed[s], after(k2 + 1), norm.pool_passed)
                    nc.gpsimd.tensor_copy(x_view[:, b, t, :], norm.xn[:, s, :]).then_inc(copied[s], 1)




def attend_layer1(nc, a, ident, ident16, x_all, xT_all):
    HP = R1 // 2
    PADS = S + WIN
    with ExitStack() as ctx:
        m = Place(nc, ctx, "a1_")
        w = m.sbuf("w", [P, 2, KC, W1])
        wo = m.sbuf("wo", [P, 2, R1, D])
        mask = m.sbuf("mask", [P, NW, P], BF16)
        qT = m.sbuf("qT", [P, HP, NW, 2 * WIN])
        kT = m.sbuf("kT", [P, PADS])
        vT = m.sbuf("vT", [P, PADS])
        vw = m.sbuf("vw", [P, NW, HD1])
        probs = m.sbuf("probs", [P, HP, NW, P])
        pT = m.sbuf("pT", [P, HP, NW, P])
        oT = m.sbuf("oT", [P, R1, S])
        mx = m.sbuf("mx", [P, HP, NW])
        rsum = m.sbuf("rsum", [P, HP, NW])
        rinv = m.sbuf("rinv", [P, HP, NW])
        ps = m.psum("ps", [P, 4, 512])
        ps_y = m.psum("ps_y", [P, TT, D])
        mask_in = m.sem("mask_in")
        w_in = m.sems("w_in")
        padded = m.sem("padded")
        kv_done = m.sem("kv_done")
        q_done = m.sem("q_done")
        kv_out = m.sem("kv_out")
        q_out = m.sem("q_out")
        scored = m.sem("scored")
        maxed = m.sem("maxed")
        shifted = m.sem("shifted")
        exped = m.sem("exped")
        rsummed = m.sem("rsummed")
        inverted = m.sem("inverted")
        normed = m.sem("normed")
        v_turned = m.sem("v_turned")
        vw_out = m.sem("vw_out")
        p_turned = m.sem("p_turned")
        pT_out = m.sem("pT_out")
        attended = m.sem("attended")
        oT_out = m.sem("oT_out")
        projected = m.sem("projected")
        added = m.sem("added")

        block = ctx.enter_context(nc.Block())
        scale = float(HD1) ** -0.5
        x_view = x_all[:].rearrange("p b (t c) -> p b t c", t=TT)
        banks = [ps[:, 0:2, :].rearrange("p b (w c) -> p (b w) c", c=P),
                 ps[:, 2:4, :].rearrange("p b (w c) -> p (b w) c", c=P)]

        def items(eng, body):
            with eng.Fori(0, G1 // 2) as gg:
                for s in range(2):
                    with eng.Fori(0, NB) as b:
                        body(gg, s, b, (gg * 2 + s) * NB + b)

        @block.sync
        def _(sp):
            sp.dma_start(probs[:, 0, :, :], a["window"]).then_inc(mask_in, 16)

            def load(g, s):
                sp.dma_start(w[:, s, :, :], a["w1T"][g]).then_inc(w_in[s], 16)
                sp.dma_start(wo[:, s, :, :], a["wo1T"][g]).then_inc(w_in[s], 16)

            load(0, 0)
            load(1, 1)
            with sp.Fori(1, G1 // 2) as gg:
                for s in range(2):
                    sp.wait_ge(projected, ((gg - 1) * 2 + s + 1) * NB * TT)
                    load(gg * 2 + s, s)

        @block.tensor
        def _(pe):
            pe.wait_ge(padded, 3)

            def body(gg, g, b, i):
                pe.wait_ge(w_in[g], 32 * (gg + 1))

                def project(bank, col, sem):
                    for k in range(KC):
                        last = nc.tensor.matmul(ps[:, bank, :], w[:, g, k, col:col + HD1], xT_all[:, k, b, :],
                                                start=(k == 0), stop=(k == KC - 1))
                    last.then_inc(sem, 1)

                def scores(hp):
                    for half in range(2):
                        for q in range(4):
                            wi = 4 * half + q
                            nc.tensor.matmul(banks[hp][:, wi, :], qT[:, hp, wi, :], kT[:, wi * WIN:wi * WIN + P],
                                             start=(q == 0), stop=False, skip_group_check=True)
                        last = nc.tensor.matmul(ps[:, 2 * hp + half, :], ident16[:],
                                                mask[:, 4 * half:4 * half + 4, :].rearrange("p w c -> p (w c)"),
                                                start=False, stop=True, skip_group_check=True)
                    last.then_inc(scored, 1)

                def turn_probs(hp):
                    pe.wait_ge(normed, 2 * i + hp + 1)
                    for wi in range(NW):
                        last = nc.tensor.transpose(banks[hp][:, wi, :], probs[:, hp, wi, :], ident[:])
                    last.then_inc(p_turned, 1)

                def attend(hp):
                    pe.wait_ge(pT_out, 2 * i + hp + 1)
                    for wi in range(NW):
                        last = nc.tensor.matmul(banks[hp][:, wi, :], vw[:, wi, :], pT[:, hp, wi, :],
                                                start=(wi % 4 == 0), stop=True, skip_group_check=True)
                    last.then_inc(attended, 1)

                def project_out(hp):
                    pe.wait_ge(oT_out, 2 * i + hp + 1)
                    for t in range(TT):
                        for j in range(2 * hp, 2 * hp + 2):
                            last = nc.tensor.matmul(ps_y[:, t, :], oT[:, j, t * P:(t + 1) * P], wo[:, g, j, :],
                                                    start=(j == 0), stop=(j == R1 - 1))
                        if hp == HP - 1:
                            last.then_inc(projected, 1)

                project(0, R1 * HD1, kv_done)
                project(1, (R1 + 1) * HD1, kv_done)
                project(2, 0, q_done)
                project(3, HD1, q_done)
                pe.wait_ge(kv_out, 2 * i + 2)
                pe.wait_ge(q_out, 4 * i + 2)
                scores(0)
                project(2, 2 * HD1, q_done)
                project(3, 3 * HD1, q_done)
                pe.wait_ge(shifted, 2 * i + 1)
                for wi in range(NW):
                    last = nc.tensor.transpose(banks[0][:, wi, :], vT[:, wi * WIN:wi * WIN + P], ident[:])
                last.then_inc(v_turned, 1)
                pe.wait_ge(q_out, 4 * i + 4)
                scores(1)
                pe.wait_ge(vw_out, i + 1)
                turn_probs(0)
                attend(0)
                pe.wait_ge(added, after(4 * i))
                project_out(0)
                turn_probs(1)
                attend(1)
                project_out(1)

            items(pe, body)

        @block.scalar
        def _(act):
            def body(gg, g, b, i):
                def query(j):
                    act.wait_ge(q_done, 4 * i + j + 1)
                    dst = qT[:, j // 2, :, (j % 2) * WIN:(j % 2 + 1) * WIN]
                    nc.scalar.activation(dst, ps[:, 2 + j % 2, :].rearrange("p (w c) -> p w c", c=WIN), ACT.Copy)\
                        .then_inc(q_out, 1)

                for n, dst in enumerate((kT, vT)):
                    act.wait_ge(kv_done, 2 * i + n + 1)
                    nc.scalar.activation(dst[:, WIN:PADS], ps[:, n, :], ACT.Copy).then_inc(kv_out, 1)
                for j in range(R1):
                    query(j)

                def exponential(hp):
                    act.wait_ge(shifted, 2 * i + hp + 1)
                    nc.scalar.activation(probs[:, hp, :, :], probs[:, hp, :, :], ACT.Exp, scale=scale)\
                        .then_inc(exped, 1)

                def turned(hp):
                    act.wait_ge(p_turned, 2 * i + hp + 1)
                    nc.scalar.activation(pT[:, hp, :, :], banks[hp], ACT.Copy).then_inc(pT_out, 1)

                exponential(0)
                exponential(1)
                turned(0)
                turned(1)

            act.wait_ge(padded, 3)
            items(act, body)

        @block.gpsimd
        def _(pool):
            nc.gpsimd.memset(kT[:, 0:WIN], 0.0).then_inc(padded, 1)
            nc.gpsimd.memset(vT[:, 0:WIN], 0.0).then_inc(padded, 1)
            pool.wait_ge(mask_in, 16)
            nc.gpsimd.tensor_copy(mask[:], probs[:, 0, :, :]).then_inc(padded, 1)

            def body(gg, g, b, i):
                for hp in range(HP):
                    pool.wait_ge(inverted, 2 * i + hp + 1)
                    nc.gpsimd.tensor_tensor(probs[:, hp, :, :], probs[:, hp, :, :],
                                            bcast(rinv[:, hp, :], 2, P), ALU.mult).then_inc(normed, 1)

            items(pool, body)

        @block.vector
        def _(dve):
            start_ahead(dve, added)

            def body(gg, g, b, i):
                def shift(hp):
                    dve.wait_ge(scored, 2 * i + hp + 1)
                    nc.vector.tensor_reduce(mx[:, hp, :], banks[hp], AX.X, ALU.max).then_inc(maxed, 1)
                    dve.wait_ge(maxed, 2 * i + hp + 1)
                    nc.vector.tensor_tensor(probs[:, hp, :, :], banks[hp], bcast(mx[:, hp, :], 2, P),
                                            ALU.subtract).then_inc(shifted, 1)

                def invert(hp):
                    dve.wait_ge(exped, 2 * i + hp + 1)
                    nc.vector.tensor_reduce(rsum[:, hp, :], probs[:, hp, :, :], AX.X, ALU.add).then_inc(rsummed, 1)
                    dve.wait_ge(rsummed, 2 * i + hp + 1)
                    nc.vector.reciprocal(rinv[:, hp, :], rsum[:, hp, :]).then_inc(inverted, 1)

                def output(hp):
                    dve.wait_ge(attended, 2 * i + hp + 1)
                    for h in range(2):
                        last = nc.vector.tensor_copy(
                            oT[:, 2 * hp + h, :].rearrange("p (w c) -> p w c", c=WIN),
                            banks[hp][:, :, h * WIN:(h + 1) * WIN])
                    last.then_inc(oT_out, 1)

                shift(0)
                invert(0)
                dve.wait_ge(v_turned, i + 1)
                nc.vector.tensor_copy(vw[:], banks[0]).then_inc(vw_out, 1)
                shift(1)
                invert(1)
                output(0)
                output(1)
                for t in range(TT):
                    dve.wait_ge(projected, 4 * i + t + 1)
                    nc.vector.tensor_tensor(x_view[:, b, t, :], ps_y[:, t, :], x_view[:, b, t, :], ALU.add)\
                        .then_inc(added, 1)

            items(dve, body)




def feed_forward1(nc, a, ident, eps, x_all, out):
    NZ = E1 + E1 * RK
    with ExitStack() as ctx:
        m = Place(nc, ctx, "f1_")
        w = m.sbuf("w", [P, KC, D])
        wz = m.sbuf("wz", [P, KC, NZ])
        wb = m.sbuf("wb", [E1 * RK, D])
        bias = m.sbuf("bias", [P, E1])
        xT = m.sbuf("xT", [P, 2, D])
        logit = m.sbuf("logit", [P, 2, E1])
        best = m.sbuf("best", [P, 2, 1])
        is_best = m.sbuf("is_best", [P, 2, E1])
        left = m.sbuf("left", [P, 2, E1 + 1])
        chosen = m.sbuf("chosen", [P, 2, E1])
        z = m.sbuf("z", [P, 2, E1, RK])
        zT = m.sbuf("zT", [E1 * RK, 2, P])
        out_rows = m.sbuf("out_rows", [P, 2, D])
        first = Norm(Place(nc, ctx, "f1a_"))
        second = Norm(Place(nc, ctx, "f1b_"))
        ps_n = m.psum("ps_n", [P, 2, D])
        ps_y = m.psum("ps_y", [P, 2, D])
        ps_z = m.psum("ps_z", [P, 2, 512])
        ps_zT = m.psum("ps_zT", [P, 2, 512])
        w_in = m.sem("w_in")
        xn_turned = m.sems("xn_turned")
        xT_out = m.sems("xT_out")
        z_done = m.sems("z_done")
        picked = m.sem("picked")
        z_out = m.sems("z_out")
        z_turned = m.sems("z_turned")
        zT_out = m.sems("zT_out")
        y_done = m.sems("y_done")
        stored = m.sems("stored")
        PICKS = 4 + 2 * (E1 - 1)

        block = ctx.enter_context(nc.Block())
        x_view = x_all[:].rearrange("p b (t c) -> p b t c", t=TT)
        out_view = out.rearrange("(b t p) n -> b t p n", b=NB, t=TT)

        @block.sync
        def _(sp):
            start_ahead(sp, stored)
            sp.dma_start(w[:], a["w_upT"].rearrange("(k p) n -> p k n", p=P)).then_inc(w_in, 16)
            sp.dma_start(wz[:], a["wzT"].rearrange("(k p) n -> p k n", p=P)).then_inc(w_in, 16)
            sp.dma_start(wb[:], a["lora_BT"]).then_inc(w_in, 16)
            sp.dma_start(bias[:], a["bias"].partition_broadcast(P)).then_inc(w_in, 16)
            with sp.Fori(0, NB) as b:
                for t in range(TT):
                    s, k2 = t % 2, b * 2 + t // 2
                    sp.wait_ge(second.normed[s], after(k2 + 1))
                    sp.dma_start(out_view[b, t], out_rows[:, s, :]).then_inc(stored[s], 16)
            for s in range(2):
                sp.wait_ge(stored[s], after(NB * 2, 16))

        @block.tensor
        def _(pe):
            start_ahead(pe, xn_turned, z_turned, y_done)
            pe.wait_ge(w_in, 64)

            def base(b, t):
                s, k2 = t % 2, b * 2 + t // 2
                transpose_rows(nc, pe, ident, first, s, k2, ps_n, xn_turned, xT_out)
                pe.wait_ge(xT_out[s], after(k2 + 1))
                pe.wait_ge(z_out[s], after(k2))
                for k in range(KC):
                    last = nc.tensor.matmul(ps_z[:, s, 0:NZ], xT[:, s, k * P:(k + 1) * P], wz[:, k, :],
                                            start=(k == 0), stop=(k == KC - 1))
                last.then_inc(z_done[s], 1)
                pe.wait_ge(second.summed[s], after(k2))
                for k in range(KC):
                    nc.tensor.matmul(ps_y[:, s, :], xT[:, s, k * P:(k + 1) * P], w[:, k, :],
                                     start=(k == 0), stop=False)

            def expert(b, t):
                s, k2 = t % 2, b * 2 + t // 2
                pe.wait_ge(z_out[s], after(k2 + 1))
                pe.wait_ge(zT_out[s], after(k2))
                nc.tensor.transpose(ps_zT[0:E1 * RK, s, 0:P], z[:, s, :, :].rearrange("p e r -> p (e r)"), ident[:])\
                    .then_inc(z_turned[s], 1)
                pe.wait_ge(zT_out[s], after(k2 + 1))
                nc.tensor.matmul(ps_y[:, s, :], zT[:, s, :], wb[:], start=False, stop=True).then_inc(y_done[s], 1)

            with pe.Fori(0, NB) as b:
                for t in range(TT + 1):
                    if t < TT:
                        base(b, t)
                    if t >= 1:
                        expert(b, t - 1)

        @block.scalar
        def _(act):
            start_ahead(act, xT_out, zT_out)

            def head(b, t):
                s, k2 = t % 2, b * 2 + t // 2
                first.on_act(nc, act, s, k2, eps)
                act.wait_ge(xn_turned[s], after(k2 + 1))
                act.wait_ge(y_done[s], after(k2))
                nc.scalar.activation(xT[:, s, :], ps_n[:, s, :], ACT.Copy).then_inc(xT_out[s], 1)

            def tail(b, t):
                s, k2 = t % 2, b * 2 + t // 2
                act.wait_ge(z_turned[s], after(k2 + 1))
                nc.scalar.activation(zT[:, s, :], ps_zT[0:E1 * RK, s, 0:P], ACT.Copy).then_inc(zT_out[s], 1)
                second.on_act(nc, act, s, k2, eps)

            with act.Fori(0, NB) as b:
                for t in range(TT + 1):
                    if t < TT:
                        head(b, t)
                    if t >= 1:
                        tail(b, t - 1)

        @block.vector
        def _(dve):
            start_ahead(dve, first.summed, first.normed, second.summed, second.normed, z_out)

            def head(b, t):
                s, k2 = t % 2, b * 2 + t // 2
                nc.vector.tensor_copy(first.res[:, s, :], x_view[:, b, t, :]).then_inc(first.summed[s], 1)
                dve.wait_ge(xn_turned[s], after(k2))
                dve.wait_ge(second.summed[s], after(k2))
                first.on_dve(nc, dve, s, k2)

            def choose(b, t):
                s, k2 = t % 2, b * 2 + t // 2
                done = [0]

                def step(ins):
                    done[0] += 1
                    ins.then_inc(picked, 1)
                    dve.wait_ge(picked, (b * TT + t) * PICKS + done[0])

                dve.wait_ge(z_done[s], k2 + 1)
                step(nc.vector.tensor_tensor(logit[:, s, :], ps_z[:, s, 0:E1], bias[:], ALU.add))
                step(nc.vector.tensor_reduce(best[:, s, :], logit[:, s, :], AX.X, ALU.max))
                step(nc.vector.tensor_scalar(is_best[:, s, :], logit[:, s, :], best[:, s, :], None, ALU.is_ge))
                step(nc.vector.tensor_copy(chosen[:, s, 0:1], is_best[:, s, 0:1]))
                for e in range(1, E1):
                    step(nc.vector.tensor_reduce(left[:, s, e:e + 1], chosen[:, s, 0:e], AX.X, ALU.add))
                    step(nc.vector.tensor_tensor(chosen[:, s, e:e + 1], is_best[:, s, e:e + 1], left[:, s, e:e + 1],
                                                 ALU.is_gt))
                dve.wait_ge(z_turned[s], after(k2))
                nc.vector.tensor_tensor(z[:, s, :, :], ps_z[:, s, E1:NZ].rearrange("p (e r) -> p e r", r=RK),
                                        bcast(chosen[:, s, :], 2, RK), ALU.mult).then_inc(z_out[s], 1)

            def tail(b, t):
                s, k2 = t % 2, b * 2 + t // 2
                dve.wait_ge(y_done[s], after(k2 + 1))
                nc.vector.tensor_tensor(second.res[:, s, :], ps_y[:, s, :], first.xn[:, s, :], ALU.add)\
                    .then_inc(second.summed[s], 1)
                dve.wait_ge(stored[s], after(k2, 16))
                second.on_dve(nc, dve, s, k2, out_rows[:, s, :])

            with dve.Fori(0, NB) as b:
                for t in range(TT + 1):
                    if t < TT:
                        head(b, t)
                        choose(b, t)
                    if t >= 1:
                        tail(b, t - 1)


def load_constants(nc, a, ident, ident16, eps):
    with ExitStack() as ctx:
        m = Place(nc, ctx, "c_")
        ident_in = m.sem("ident_in")
        eps_set = m.sem("eps_set")
        block = ctx.enter_context(nc.Block())

        @block.sync
        def _(sp):
            sp.dma_start(ident[:], a["ident"]).then_inc(ident_in, 16)

        @block.vector
        def _(dve):
            nc.vector.memset(eps[:], EPS).then_inc(eps_set, 1)
            dve.wait_ge(ident_in, 16)
            nc.vector.tensor_copy(ident16[:], ident[:]).then_inc(eps_set, 1)
            dve.wait_ge(eps_set, 2)


def program(nc, a, out, debug=None):
    qT_dram = nc.dram_tensor("qT_scratch", [NB * D, S], F32).ap()
    kT_dram = nc.dram_tensor("kT_scratch", [NB * KV0, S], F32).ap()
    with ExitStack() as ctx:
        m = Place(nc, ctx, "")
        ident = m.sbuf("ident_sb", [P, P])
        ident16 = m.sbuf("ident16_sb", [P, P], BF16)
        eps = m.sbuf("eps_sb", [P, 1])
        x_all = m.sbuf("x_all", [P, NB, TT * D])
        xT_all = m.sbuf("xT_all", [P, KC, NB, S])
        load_constants(nc, a, ident, ident16, eps)
        with ExitStack() as ffn:
            mf = Place(nc, ffn, "")
            w_gu = mf.sbuf("w_gu", [P, KC, 2 * INTER])
            w_dn = mf.sbuf("w_dn", [P, FT, D])
            dequantise(nc, a, w_gu, w_dn, x_all[:].rearrange("p b n -> p (b n)"))
            with ExitStack() as att:
                v_all = Place(nc, att, "").sbuf("v_all", [P, NB, G0, TT, HD0])
                project_layer0(nc, a, ident, v_all, qT_dram, kT_dram)
                v_pairs = v_all[:].rearrange("p b g t d -> p (b g) t d")
                o_pairs = x_all[:].rearrange("p b (g t c) -> p (b g) t c", g=G0, t=TT)
                work = xT_all[:]
                attend_layer0(nc, a, ident, ident16, v_pairs, qT_dram, kT_dram, o_pairs, work)
            project_out0(nc, a, ident, eps, x_all, xT_all)
            if debug is not None:
                dump(nc, x_all, debug, 0)
            feed_forward0(nc, a, ident, eps, x_all, xT_all, w_gu, w_dn)
        if debug is not None:
            dump(nc, x_all, debug, 1)
        attend_layer1(nc, a, ident, ident16, x_all, xT_all)
        if debug is not None:
            dump(nc, x_all, debug, 2)
        feed_forward1(nc, a, ident, eps, x_all, out)


def dump(nc, x_all, debug, n):
    with ExitStack() as ctx:
        m = Place(nc, ctx, f"d{n}_")
        dumped = m.sem("dumped")
        block = ctx.enter_context(nc.Block())

        @block.sync
        def _(sp):
            dst = debug.rearrange("n (b t p) c -> n b p t c", b=NB, p=P)
            for b in range(NB):
                sp.dma_start(dst[n, b], x_all[:, b, :].rearrange("p (t c) -> p t c", t=TT)).then_inc(dumped, 16)
            sp.wait_ge(dumped, 16 * NB)


def constants():
    import numpy as np

    inv_freq = (1.0 / np.float32(10000.0) ** (np.arange(0, HD0, 2, dtype=np.float32) / np.float32(HD0)))
    freqs = np.outer(np.arange(S, dtype=np.float32), inv_freq.astype(np.float32)).astype(np.float32)
    emb = np.concatenate([freqs, freqs], axis=-1)
    cos, sin = np.cos(emb).astype(np.float32), np.sin(emb).astype(np.float32)
    sin[:, :HD0 // 2] *= -1
    scale = np.float32(HD0 ** -0.5)
    rope = np.stack([cos * scale, sin * scale, cos, sin], axis=1)
    rope = rope.reshape(TT, P, 4, HD0).transpose(1, 0, 2, 3)
    q, c = np.arange(P)[:, None], np.arange(P)[None, :]
    causal = np.where(c > q, NEG, 0.0).astype(np.float32)
    seen = (c > q % WIN) & (c <= q % WIN + WIN)
    window = np.broadcast_to(np.where(seen, 0.0, NEG)[:, None, :], (P, NW, P)).copy()
    window[:, 0, :WIN] = NEG
    guess = np.zeros((P, TT, 2), np.float32)
    for row in range(P, S):
        low, high = -8.0, 8.0
        for _ in range(60):
            z = (low + high) / 2
            low, high = (z, high) if 0.5 * math.erfc(z / math.sqrt(2.0)) > TARGET / (row + 1) else (low, z)
        density = math.exp(-z * z / 2) / math.sqrt(2 * math.pi)
        guess[row % P, row // P] = z / 2, 0.5 / ((row + 1) * density)
    iota8 = np.broadcast_to(np.arange(TOP, dtype=np.float32), (P, R0, TOP)).copy()
    return {
        "guess": guess,
        "iota8": iota8,
        "rope": np.ascontiguousarray(rope),
        "causal": causal,
        "window": window.astype(np.float32),
        "ident": np.eye(P, dtype=np.float32),
        "shift": (4 * (np.arange(P, dtype=np.uint32) % PACK)).reshape(P, 1),
        "iota": np.arange(16, dtype=np.float32).reshape(16, 1),
    }


def layout(i):
    import numpy as np

    x = i["L0_attn_hidden_states"].reshape(NB * S, D)
    w1 = [i["L1_attn_wq"].reshape(G1, R1 * HD1, KC, P), i["L1_attn_wk"].reshape(G1, HD1, KC, P),
          i["L1_attn_wv"].reshape(G1, HD1, KC, P)]
    return {
        "x": x,
        "xT": x.T,
        "wqkvT": np.concatenate([i["L0_attn_Wq"], i["L0_attn_Wk"], i["L0_attn_Wv"]]).T,
        "wo0T": i["L0_attn_Wo"].T,
        "qw_gu": np.repeat(i["L0_ffn_qweight_gu"], PACK, axis=0),
        "qw_dn": np.repeat(i["L0_ffn_qweight_down"], PACK, axis=0),
        "qzeros_gu": i["L0_ffn_qzeros_gu"],
        "qzeros_dn": i["L0_ffn_qzeros_down"],
        "scales_gu": i["L0_ffn_scales_gu"],
        "scales_dn": i["L0_ffn_scales_down"],
        "g_idx_gu": i["L0_ffn_g_idx_gu"],
        "g_idx_dn": i["L0_ffn_g_idx_down"],
        "w1T": np.concatenate(w1, axis=1).transpose(0, 3, 2, 1),
        "wo1T": i["L1_attn_wo"].T.reshape(G1, R1, HD1, D).transpose(0, 2, 1, 3),
        "w_upT": i["L1_ffn_W_up"].T,
        "wzT": np.concatenate([i["L1_ffn_gate_w"], i["L1_ffn_lora_A"].reshape(E1 * RK, D)]).T,
        "lora_BT": i["L1_ffn_lora_B"].transpose(0, 2, 1).reshape(E1 * RK, D),
        "bias": i["L1_ffn_expert_bias"],
    }


def kernel(**inputs):
    import numpy as np
    import concourse.bacc as bacc
    from concourse.bass_utils import run_bass_kernel_spmd

    nc = bacc.Bacc("TRN2", target_bir_lowering=False, num_devices=1)
    arrays, aps = {}, {}
    host = layout({k: np.asarray(v) for k, v in inputs.items()})
    for name, v in {**host, **constants()}.items():
        v = np.ascontiguousarray(v)
        arrays[f"in_{name}"] = v
        aps[name] = nc.dram_tensor(f"in_{name}", v.shape, mybir.dt.from_np(v.dtype), kind="ExternalInput").ap()
    out = nc.dram_tensor("out", [NB * S, D], F32, kind="ExternalOutput").ap()
    debug = nc.dram_tensor("debug", [3, NB * S, D], F32, kind="ExternalOutput").ap() if DEBUG else None
    program(nc, aps, out, debug)
    r = run_bass_kernel_spmd(nc, [arrays], core_ids=[0])
    return r.results[0]["out"].reshape(NB, S, D)


DEBUG = False
```

```python
import math
from contextlib import ExitStack

import concourse.bass as bass
from concourse import mybir

ALU = mybir.AluOpType
ACT = mybir.ActivationFunctionType
AX = mybir.AxisListType
F32 = mybir.dt.float32
F32R = mybir.dt.float32r
BF16 = mybir.dt.bfloat16
U32 = mybir.dt.uint32
I32 = mybir.dt.int32
U8 = mybir.dt.uint8

P = 128
D = 512
KC = D // P
NB = 4
S = 512
TT = S // P
EPS = 1e-5

H0 = 32
G0 = 8
HD0 = D // H0
R0 = H0 // G0
KV0 = G0 * HD0
KEEP = 128
TOP = 8
NEG = -3.0e38

INTER = 1376
FT = (INTER + P - 1) // P
GU_GROUPS = 4
DN_GROUPS = 10
TARGET = 124.0
WITHIN = 3.5
PACK = 8

H1 = 32
G1 = 8
R1 = H1 // G1
HD1 = 128
WIN = 64
NW = S // WIN
W1 = (R1 + 2) * HD1

E1 = 4
RK = 8


START = 8


def rows_of(f):
    return min(P, INTER - f * P)


def after(k, unit=1):
    return unit * k + START


class Place:

    def __init__(self, nc, ctx, prefix):
        self.nc, self.ctx, self.prefix = nc, ctx, prefix
        self.owned = []
        ctx.callback(self.release)

    def release(self):
        if self.owned:
            self.nc.clear_and_free_semaphores(self.owned)
            self.nc.all_engine_barrier()

    def sbuf(self, name, shape, dtype=F32):
        return self.ctx.enter_context(self.nc.sbuf_tensor(self.prefix + name, shape, dtype))

    def psum(self, name, shape, dtype=F32):
        return self.ctx.enter_context(self.nc.psum_tensor(self.prefix + name, shape, dtype))

    def sem(self, name):
        s = self.nc.alloc_semaphore(self.prefix + name)
        self.owned.append(s)
        return s

    def sems(self, name, n=2):
        return [self.sem(f"{name}{i}") for i in range(n)]


def bcast(ap, axis, n):
    v = ap.unsqueeze(axis)
    shape = list(v.shape)
    shape[axis] = n
    return v.broadcast_to(shape)


def wait_apart(eng, sem, value, passed):
    eng.wait_ge(sem, value)
    eng.sem_inc(passed, 1)


def start_ahead(eng, *groups):
    for g in groups:
        for s in (g if isinstance(g, list) else [g]):
            eng.sem_inc(s, START)


def tiles(eng, step, ahead):

    def run(b, t, last):
        def has(stage, by):
            if t + by >= TT and not last:
                stage(b + 1, t + by - TT)
            elif 0 <= t + by < TT:
                stage(b, t + by)
        step(has)

    for t in range(-ahead, 0):
        run(0, t, False)
    with eng.Fori(0, NB - 1) as b:
        for t in range(TT):
            run(b, t, False)
    for t in range(TT):
        run(NB - 1, t, True)




def dequantise(nc, a, w_gu, w_dn, space):
    CH = 512
    BANKS = 4
    with ExitStack() as ctx:
        m = Place(nc, ctx, "dq_")
        words = space.bitcast(U32)[:, 0:4 * INTER].rearrange("p (s n) -> p s n", s=2)
        shift = m.sbuf("shift", [P, 1], U32)
        iota = m.sbuf("iota", [16, 1])
        gidx_i = space.bitcast(I32)[0:16, 4 * INTER:4 * INTER + D + INTER]
        gidx = m.sbuf("gidx", [16, D + INTER])
        wrap = m.sbuf("wrap", [16, D + INTER])
        onehot = m.sbuf("onehot", [16, D + INTER], F32R)
        scratch = w_dn[:].rearrange("p f n -> p (f n)")
        scale_gu = scratch[0:GU_GROUPS, 0:2 * INTER]
        scale_dn = m.sbuf("scale_dn", [DN_GROUPS, D])
        zw_gu = m.sbuf("zw_gu", [GU_GROUPS, 2 * INTER // PACK], U32)
        zw_dn = m.sbuf("zw_dn", [DN_GROUPS, D // PACK], U32)
        zi_gu = scratch.bitcast(U32)[0:GU_GROUPS, 2 * INTER:4 * INTER]
        zi_dn = m.sbuf("zi_dn", [DN_GROUPS, D], U32)
        zero_gu = m.sbuf("zero_gu", [GU_GROUPS, 2 * INTER], F32R)
        zero_dn = m.sbuf("zero_dn", [DN_GROUPS, D], F32R)
        high_gu = m.sbuf("high_gu", [GU_GROUPS, 2 * INTER], F32R)
        high_dn = m.sbuf("high_dn", [DN_GROUPS, D], F32R)
        low_gu = m.sbuf("low_gu", [GU_GROUPS, 2 * INTER], F32R)
        low_dn = m.sbuf("low_dn", [DN_GROUPS, D], F32R)
        centred = m.sbuf("centred", [P, 2, CH])
        ps_scale = m.psum("ps_scale", [P, BANKS, CH])
        ps_zero = m.psum("ps_zero", [P, BANKS, CH])
        small_in = m.sem("small_in")
        words_in = m.sems("words_in")
        unpacked = m.sem("unpacked")
        prepared = m.sem("prepared")
        rounded = m.sem("rounded")
        spread = m.sem("spread")
        centre_done = m.sem("centre_done")
        piece_done = m.sem("piece_done")

        chunks = [("gu", k, P) for k in range(KC)] + [("dn", f, rows_of(f)) for f in range(FT)]
        pieces = []
        for c, (kind, k, rows) in enumerate(chunks):
            width = 2 * INTER if kind == "gu" else D
            pieces += [(c, j, min(CH, width - j)) for j in range(0, width, CH)]

        block = ctx.enter_context(nc.Block())

        @block.sync
        def _(sp):
            sp.dma_start(gidx_i[0:GU_GROUPS, 0:D], a["g_idx_gu"].partition_broadcast(GU_GROUPS)).then_inc(small_in, 16)
            sp.dma_start(gidx_i[0:DN_GROUPS, D:], a["g_idx_dn"].partition_broadcast(DN_GROUPS)).then_inc(small_in, 16)
            for dst, src in ((shift, "shift"), (iota, "iota"), (scale_gu, "scales_gu"), (scale_dn, "scales_dn"),
                             (zw_gu, "qzeros_gu"), (zw_dn, "qzeros_dn")):
                sp.dma_start(dst[:, :], a[src]).then_inc(small_in, 16)
            for c, (kind, k, rows) in enumerate(chunks):
                if c >= 2:
                    sp.wait_ge(piece_done, max(n + 1 for n, p in enumerate(pieces) if p[0] == c - 2))
                width = 2 * INTER if kind == "gu" else D
                src = a["qw_gu"] if kind == "gu" else a["qw_dn"]
                sp.dma_start(words[0:rows, c % 2, 0:width], src[k * P:k * P + rows, :]).then_inc(words_in[c % 2], 16)

        @block.scalar
        def _(act):
            act.wait_ge(small_in, 16 * 8)
            nc.scalar.activation(high_gu[:], scale_gu, ACT.Copy).then_inc(rounded, 1)
            nc.scalar.activation(high_dn[:], scale_dn[:], ACT.Copy).then_inc(rounded, 1)

        @block.vector
        def _(dve):
            steps = [0]

            def step(ins):
                steps[0] += 1
                ins.then_inc(prepared, 1)

            def settle():
                dve.wait_ge(prepared, steps[0])

            dve.wait_ge(small_in, 16 * 8)
            for rows, cols, n in ((GU_GROUPS, slice(0, D), GU_GROUPS), (DN_GROUPS, slice(D, D + INTER), DN_GROUPS)):
                g, h, w = gidx[0:rows, cols], onehot[0:rows, cols], wrap[0:rows, cols]
                step(nc.vector.tensor_copy(g, gidx_i[0:rows, cols]))
                settle()
                step(nc.vector.tensor_scalar(w, g, 0.0, float(n), ALU.is_lt, ALU.mult))
                settle()
                step(nc.vector.tensor_tensor(g, g, w, ALU.add))
                settle()
                step(nc.vector.tensor_scalar(g, g, 0.0, float(n - 1), ALU.max, ALU.min))
                settle()
                step(nc.vector.tensor_scalar(h, g, iota[0:rows, 0:1], None, ALU.is_equal))
            for zw, zi, zero in ((zw_gu, zi_gu, zero_gu), (zw_dn, zi_dn, zero_dn)):
                v = zi[:, :].rearrange("p (c s) -> p c s", s=PACK)
                for s in range(PACK):
                    step(nc.vector.tensor_scalar(v[:, :, s], zw[:], 4 * s, 15,
                                                 ALU.logical_shift_right, ALU.bitwise_and))
                settle()
                step(nc.vector.tensor_scalar(zero[:], zi[:, :], 1.0, None, ALU.add))
            dve.wait_ge(rounded, 2)
            for low, scale, high in ((low_gu, scale_gu, high_gu), (low_dn, scale_dn, high_dn)):
                step(nc.vector.tensor_tensor(low[:], scale[:, :], high[:].bitcast(F32), ALU.subtract))

            n = 0
            for c, (kind, k, rows) in enumerate(chunks):
                width = 2 * INTER if kind == "gu" else D
                dve.wait_ge(words_in[c % 2], 16 * (c // 2 + 1))
                u = words[0:rows, c % 2, 0:width]
                nc.vector.tensor_scalar(u, u, shift[0:rows, 0:1], 15, ALU.logical_shift_right,
                                        ALU.bitwise_and).then_inc(unpacked, 1)
                dve.wait_ge(unpacked, c + 1)
                while n < len(pieces) and pieces[n][0] == c:
                    _, j, w = pieces[n]
                    dst = w_gu[0:rows, k, j:j + w] if kind == "gu" else w_dn[0:rows, k, j:j + w]
                    dve.wait_ge(spread, n + 1)
                    nc.vector.tensor_tensor(centred[0:rows, n % 2, 0:w], words[0:rows, c % 2, j:j + w],
                                            ps_zero[0:rows, n % BANKS, 0:w], ALU.subtract).then_inc(centre_done, 1)
                    dve.wait_ge(centre_done, n + 1)
                    nc.vector.tensor_tensor(dst, centred[0:rows, n % 2, 0:w], ps_scale[0:rows, n % BANKS, 0:w],
                                            ALU.mult).then_inc(piece_done, 1)
                    n += 1

        @block.tensor
        def _(pe):
            pe.wait_ge(prepared, 2 * 5 + 2 * (PACK + 1) + 2)
            for n, (c, j, w) in enumerate(pieces):
                kind, k, rows = chunks[c]
                if n >= BANKS:
                    pe.wait_ge(piece_done, n - BANKS + 1)
                if kind == "gu":
                    hot, parts, ze = onehot[0:GU_GROUPS, k * P:k * P + rows], (high_gu, low_gu), zero_gu
                else:
                    hot, parts, ze = onehot[0:DN_GROUPS, D + k * P:D + k * P + rows], (high_dn, low_dn), zero_dn
                for x, part in enumerate(parts):
                    nc.tensor.matmul(ps_scale[0:rows, n % BANKS, 0:w], hot, part[:, j:j + w], start=(x == 0), stop=(x == 1))
                nc.tensor.matmul(ps_zero[0:rows, n % BANKS, 0:w], hot, ze[:, j:j + w], start=True,
                                 stop=True).then_inc(spread, 1)




def project_layer0(nc, a, ident, v_all, qT_dram, kT_dram):
    W = D + 2 * KV0
    QB, KB = H0 // 2, G0
    GROUP = 8
    GROUPS = (QB + KB) // GROUP
    with ExitStack() as ctx:
        m = Place(nc, ctx, "p0_")
        w = m.sbuf("w", [P, KC, W])
        rope = m.sbuf("rope", [P, TT, 4, HD0])
        xT = m.sbuf("xT", [P, 2, KC, P])
        cosed = m.sbuf("cosed", [P, 2, D + KV0])
        sined = m.sbuf("sined", [P, 2, D + KV0])
        roped = m.sbuf("roped", [P, 2, D + KV0])
        stack = m.sbuf("stack", [P, 2, (QB + KB) * P])
        turned = m.sbuf("turned", [P, GROUPS, GROUP, P])
        ps_q = m.psum("ps_q", [P, 2, D])
        ps_kv = m.psum("ps_kv", [P, 2, 512])
        ps_t = m.psum("ps_t", [P, 2, GROUP * P])
        weights_in = m.sem("weights_in")
        x_in = m.sems("x_in")
        projected = m.sems("projected")
        rotated = m.sems("rotated")
        summed = m.sems("summed")
        high_done = m.sems("high_done")
        low_done = m.sems("low_done")
        stack_used = m.sems("stack_used")
        transposed = m.sems("transposed")
        evacuated = m.sems("evacuated")
        stored = m.sems("stored", GROUPS)

        block = ctx.enter_context(nc.Block())

        def group(b, t, g):
            n = t * GROUPS + g
            return n % 2, b * (TT * GROUPS // 2) + n // 2

        def stack_views(s, parts):
            q = stack[:, s, 0:QB * P].rearrange("p (h i x d) -> p h i x d", i=2, x=2, d=HD0)
            k = stack[:, s, QB * P:].rearrange("p (g i x e d) -> p g i x e d", i=2, x=2, e=2, d=HD0)
            return q[:, :, :, parts, :], [k[:, :, i, parts, :, :] for i in range(2)]

        def roped_views(s):
            q = roped[:, s, 0:D].rearrange("p (h d) -> p h d", d=HD0)
            k = roped[:, s, D:].rearrange("p (g d) -> p g d", d=HD0)
            return bcast(q, 2, 2), bcast(k, 2, 2)

        @block.sync
        def _(sp):
            for k in range(KC):
                sp.dma_start(w[:, k, :], a["wqkvT"][k * P:(k + 1) * P, :]).then_inc(weights_in, 16)
            sp.dma_start(rope[:], a["rope"]).then_inc(weights_in, 16)
            start_ahead(sp, stored)
            src = a["xT"].rearrange("(k p) (b t c) -> p k b t c", p=P, b=NB, t=TT)

            def load(b, t):
                sp.wait_ge(projected[t % 2], after(b * 2 + t // 2))
                sp.dma_start(xT[:, t % 2, :, :], src[:, :, b, t, :]).then_inc(x_in[t % 2], 16)

            def store(b, t):
                for g in range(GROUPS):
                    bank, c = group(b, t, g)
                    sp.wait_ge(evacuated[bank], after(c + 1))
                    dram, x = (qT_dram, g * GROUP) if g < QB // GROUP else (kT_dram, 0)
                    dst = dram.rearrange("(b k p) (t c) -> b t p k c", b=NB, p=P, t=TT)
                    sp.dma_start(dst[b, t][:, x:x + GROUP, :], turned[:, g, :, :]).then_inc(stored[g], 16)

            def step(has):
                has(store, 0)
                has(load, 4)

            tiles(sp, step, 4)
            for g in range(GROUPS):
                sp.wait_ge(stored[g], after(NB * TT, 16))

        @block.tensor
        def _(pe):
            start_ahead(pe, projected, stack_used)
            pe.wait_ge(weights_in, 16 * (KC + 1))

            def project(b, t):
                s, k2 = t % 2, b * 2 + t // 2
                pe.wait_ge(x_in[s], 16 * (k2 + 1))
                pe.wait_ge(rotated[s], after(k2))
                for k in range(KC):
                    nc.tensor.matmul(ps_q[:, s, :], xT[:, s, k, :], w[:, k, 0:D], start=(k == 0), stop=(k == KC - 1))
                for k in range(KC):
                    last = nc.tensor.matmul(ps_kv[:, s, 0:2 * KV0], xT[:, s, k, :], w[:, k, D:W],
                                            start=(k == 0), stop=(k == KC - 1))
                last.then_inc(projected[s], 1)

            def transpose(b, t):
                s, k2 = t % 2, b * 2 + t // 2
                pe.wait_ge(low_done[s], after(k2 + 1))
                for g in range(GROUPS):
                    bank, c = group(b, t, g)
                    pe.wait_ge(evacuated[bank], after(c))
                    for x in range(GROUP):
                        col = (g * GROUP + x) * P
                        last = nc.tensor.transpose(ps_t[:, bank, x * P:(x + 1) * P], stack[:, s, col:col + P], ident[:])
                    last.then_inc(transposed[bank], 1)
                pe.wait_ge(transposed[bank], c + 1)
                pe.sem_inc(stack_used[s], 1)

            def step(has):
                has(transpose, 0)
                has(project, 2)

            tiles(pe, step, 2)

        @block.vector
        def _(dve):
            start_ahead(dve, rotated, low_done)
            dve.wait_ge(weights_in, 16 * (KC + 1))
            half = HD0 // 2

            def rotate(b, t):
                s, k2 = t % 2, b * 2 + t // 2
                dve.wait_ge(projected[s], after(k2 + 1))
                dve.wait_ge(summed[s], after(k2))
                for src, lo, heads, cos in ((ps_q[:, s, :], 0, H0, 0), (ps_kv[:, s, 0:KV0], D, G0, 2)):
                    width = heads * HD0
                    x = src.rearrange("p (h d) -> p h d", d=HD0)
                    c_out = cosed[:, s, lo:lo + width].rearrange("p (h d) -> p h d", d=HD0)
                    s_out = sined[:, s, lo:lo + width].rearrange("p (h d) -> p h d", d=HD0)
                    nc.vector.tensor_tensor(c_out, x, bcast(rope[:, t, cos, :], 1, heads), ALU.mult)
                    nc.vector.tensor_tensor(s_out[:, :, 0:half], x[:, :, half:],
                                            bcast(rope[:, t, cos + 1, 0:half], 1, heads), ALU.mult)
                    nc.vector.tensor_tensor(s_out[:, :, half:], x[:, :, 0:half],
                                            bcast(rope[:, t, cos + 1, half:], 1, heads), ALU.mult)
                last = nc.vector.tensor_copy(v_all[:, b, :, t, :], ps_kv[:, s, KV0:2 * KV0]
                                             .rearrange("p (g d) -> p g d", d=HD0))
                last.then_inc(rotated[s], 1)

            def low_parts(b, t):
                s, k2 = t % 2, b * 2 + t // 2
                dve.wait_ge(high_done[s], after(k2 + 1))
                (qr, kr), (qh, kh), (ql, kl) = roped_views(s), stack_views(s, 0), stack_views(s, 1)
                nc.vector.tensor_tensor(ql.bitcast(F32R), qr, qh, ALU.subtract)
                for i in range(2):
                    last = nc.vector.tensor_tensor(kl[i].bitcast(F32R), kr, kh[i], ALU.subtract)
                last.then_inc(low_done[s], 1)

            def step(has):
                has(low_parts, 1)
                has(rotate, 2)

            tiles(dve, step, 2)

        @block.gpsimd
        def _(pool):
            start_ahead(pool, summed)
            with pool.Fori(0, NB) as b:
                for t in range(TT):
                    s, k2 = t % 2, b * 2 + t // 2
                    pool.wait_ge(rotated[s], after(k2 + 1))
                    pool.wait_ge(low_done[s], after(k2))
                    nc.gpsimd.tensor_tensor(roped[:, s, :], cosed[:, s, :], sined[:, s, :], ALU.add)\
                        .then_inc(summed[s], 1)

        @block.scalar
        def _(act):
            start_ahead(act, high_done, evacuated)

            def high_parts(b, t):
                s, k2 = t % 2, b * 2 + t // 2
                act.wait_ge(summed[s], after(k2 + 1))
                act.wait_ge(stack_used[s], after(k2))
                (qr, kr), (qh, kh) = roped_views(s), stack_views(s, 0)
                nc.scalar.activation(qh.bitcast(F32R), qr, ACT.Copy)
                for i in range(2):
                    last = nc.scalar.activation(kh[i].bitcast(F32R), kr, ACT.Copy)
                last.then_inc(high_done[s], 1)

            def evacuate(b, t):
                for g in range(GROUPS):
                    bank, c = group(b, t, g)
                    act.wait_ge(transposed[bank], c + 1)
                    act.wait_ge(stored[g], after(b * TT + t, 16))
                    nc.scalar.activation(turned[:, g, :, :], ps_t[:, bank, :].rearrange("p (k c) -> p k c", c=P),
                                         ACT.Copy).then_inc(evacuated[bank], 1)

            def step(has):
                has(evacuate, 0)
                has(high_parts, 1)

            tiles(act, step, 2)




def attend_layer0(nc, a, ident, ident16, v_all, qT_dram, kT_dram, o_all):
    PAIRS = NB * G0
    UNITS = 2 * TT
    TURNS = PAIRS // 2
    CHUNKS = TT * (TT + 1) // 2
    ROUNDS = KEEP // TOP
    SEARCHED = 2 * (TT - 1)
    SLOTS = UNITS
    AHEAD = 6
    SELECT_STEPS = 7
    with ExitStack() as ctx:
        m = Place(nc, ctx, "a0_")
        qT = m.sbuf("qT", [P, 2, R0 // 2, S], F32R)
        kT = m.sbuf("kT", [P, 2, S], F32R)
        mask32 = m.sbuf("mask32", [P, P])
        mask = m.sbuf("mask", [P, P], BF16)
        exps = [m.sbuf(f"exps{u}", [P, R0, (u % TT + 1) * P]) for u in range(UNITS)]
        scores_sb = [m.sbuf(f"scores{u}", [P, R0, (u % TT + 1) * P]) if u % TT else None for u in range(UNITS)]
        junk = m.sbuf("junk", [P, TT, R0, S], U8)
        junk_act = m.sbuf("junk_act", [P, 3, R0, S], BF16)
        guess = m.sbuf("guess", [P, TT, 2])
        half = m.sbuf("half", [P, R0])
        iota = m.sbuf("iota", [P, R0, TOP])
        nmax = m.sbuf("nmax", [P, SLOTS, R0])
        stats = m.sbuf("stats", [P, SLOTS, R0, 6])
        thr = m.sbuf("thr", [P, SLOTS, R0])
        slope = m.sbuf("slope", [P, SLOTS, R0])
        count = m.sbuf("count", [P, SLOTS, 5, R0])
        error = m.sbuf("error", [P, SLOTS, 2, R0])
        tmp = m.sbuf("tmp", [P, SLOTS, 5, 4, R0])
        missing = m.sbuf("missing", [P, R0])
        top = m.sbuf("top", [P, R0, TOP + 1])
        hot = m.sbuf("hot", [P, R0, TOP])
        picked = m.sbuf("picked", [P, R0, 2, TOP])
        bound = m.sbuf("bound", [P, R0, 2])
        unsure = m.sbuf("unsure", [P, R0 + 1])
        unsure_all = m.sbuf("unsure_all", [P, R0 + 1])
        unsure_int = m.sbuf("unsure_int", [P, R0 + 1], I32)
        rsum = m.sbuf("rsum", [P, SLOTS, R0])
        rinv = m.sbuf("rinv", [P, SLOTS, R0])
        pT = m.sbuf("pT", [P, 2, R0 * P])
        ps_s = m.psum("ps_s", [P, R0, S])
        ps_t = m.psum("ps_t", [P, 2, R0 * P])
        ps_o = m.psum("ps_o", [P, 2, 512])
        consts_in = m.sem("consts_in")
        consts_ready = m.sem("consts_ready")
        heads_in = m.sems("heads_in")
        scored = m.sem("scored")
        stated = m.sem("stated")
        copied = m.sem("copied")
        exped = m.sem("exped")
        moved = m.sems("moved", 5)
        counted = m.sems("counted", 4)
        step_done = m.sem("step_done")
        rated = m.sem("rated")
        chained = m.sem("chained")
        reduced = m.sem("reduced")
        flagged = m.sem("flagged")
        passed = m.sem("passed")
        pool_passed = m.sem("pool_passed")
        kept = m.sem("kept")
        turned = m.sems("turned")
        pT_out = m.sems("pT_out")
        attended = m.sems("attended")
        scaled = m.sem("scaled")

        block = ctx.enter_context(nc.Block())

        def chunk(ii, u, kb):
            local = (u // TT) * CHUNKS + (u % TT) * (u % TT + 1) // 2 + kb
            return local % 2, ii * CHUNKS + local // 2

        def searched(ii, u):
            return ii * SEARCHED + (u // TT) * (TT - 1) + u % TT - 1

        def turns(eng, step):

            def run(ii, u, last):
                def has(stage, ahead):
                    v = u + ahead
                    if v < 0 or (last and v >= UNITS):
                        return
                    if v >= UNITS:
                        stage(ii + 1, v - UNITS)
                    else:
                        stage(ii, v)
                step(has)

            for u in range(-AHEAD, 0):
                run(0, u, False)
            with eng.Fori(0, TURNS - 1) as ii:
                for u in range(UNITS):
                    run(ii, u, False)
            for u in range(UNITS):
                run(TURNS - 1, u, True)

        @block.sync
        def _(sp):
            for dst, src in ((mask32, "causal"), (guess, "guess"), (iota, "iota8")):
                sp.dma_start(dst[:], a[src]).then_inc(consts_in, 16)

            def load(i, s):
                for c in range(R0 // 2):
                    sp.dma_start(qT[:, s, c, :].bitcast(F32), qT_dram[bass.ds((i * 2 + c) * P, P), :]).then_inc(heads_in[s], 16)
                sp.dma_start(kT[:, s, :].bitcast(F32), kT_dram[bass.ds(i * P, P), :]).then_inc(heads_in[s], 16)

            load(0, 0)
            load(1, 1)
            with sp.Fori(1, TURNS) as ii:
                for s in range(2):
                    sp.wait_ge(scored, (ii - 1) * UNITS + (s + 1) * TT)
                    load(ii * 2 + s, s)

        @block.tensor
        def _(pe):
            start_ahead(pe, *attended)
            pe.wait_ge(consts_ready, 4)

            def scores(ii, u):
                s, qt = u // TT, u % TT
                n = ii * UNITS + u
                L = (qt + 1) * P
                if qt == 0:
                    pe.wait_ge(heads_in[s], 16 * (R0 // 2 + 1) * (ii + 1))
                pe.wait_ge(exped, after(n))
                for j in range(R0):
                    rows = slice(j % 2 * (P // 2), (j % 2 + 1) * (P // 2))
                    nc.tensor.matmul(ps_s[:, j, 0:L], qT[rows, s, j // 2, qt * P:(qt + 1) * P],
                                     kT[rows, s, 0:L], start=True, stop=False)
                for j in range(R0):
                    last = nc.tensor.matmul(ps_s[:, j, L - P:L], ident16[:], mask[:], start=False, stop=True)
                last.then_inc(scored, 1)

            def turn(kb):
                def stage(ii, u):
                    if kb > u % TT:
                        return
                    bank, c = chunk(ii, u, kb)
                    probs = exps[u] if u % TT == 0 else scores_sb[u]
                    if kb == 0:
                        pe.wait_ge(kept, ii * UNITS + u + 1)
                    pe.wait_ge(pT_out[bank], after(c))
                    for j in range(R0):
                        last = nc.tensor.transpose(ps_t[:, bank, j * P:(j + 1) * P],
                                                   probs[:, j, kb * P:(kb + 1) * P], ident[:])
                    last.then_inc(turned[bank], 1)
                return stage

            def attend(kb):
                def stage(ii, u):
                    s, qt, i = u % 2, u % TT, ii * 2 + u // TT
                    if kb > qt:
                        return
                    bank, c = chunk(ii, u, kb)
                    if kb == 0:
                        pe.wait_ge(scaled, after(ii * UNITS + u - 1))
                    pe.wait_ge(pT_out[bank], after(c + 1))
                    for j in range(R0):
                        last = nc.tensor.matmul(ps_o[:, s, j * HD0:(j + 1) * HD0], pT[:, bank, j * P:(j + 1) * P],
                                                v_all[:, i, kb, :], start=(kb == 0 and j == 0),
                                                stop=(kb == qt), skip_group_check=True)
                    last.then_inc(attended[bank], 1)
                return stage

            def step(has):
                has(scores, 6)
                has(turn(0), 0)
                has(turn(1), 0)
                has(attend(0), 0)
                has(turn(2), 0)
                has(attend(1), 0)
                has(turn(3), 0)
                has(attend(2), 0)
                has(attend(3), 0)

            turns(pe, step)

        @block.vector
        def _(dve):
            def statistics(ii, u):
                slot, qt, n = u % SLOTS, u % TT, ii * UNITS + u
                dve.wait_ge(scored, n + 1)
                dve.wait_ge(scaled, after(n - SLOTS + 1))
                last = nc.vector.tensor_reduce(nmax[:, slot, :], ps_s[:, :, 0:(qt + 1) * P], AX.X, ALU.max, negate=True)
                for j in range(R0 if qt >= 1 else 0):
                    last = nc.vector.bn_stats(stats[:, slot, j, :], ps_s[:, j, 0:qt * P])
                last.then_inc(stated, 1)

            def count_scores(ii, u, c):
                slot, L = u % SLOTS, (u % TT + 1) * P
                for j in range(R0):
                    last = nc.vector.tensor_scalar(junk[:, u % TT if c == 0 else 0, j, 0:L], scores_sb[slot][:, j, 0:L], thr[:, slot, j:j + 1], None,
                                                   ALU.is_ge, ALU.add, accum_out=count[:, slot, c, j:j + 1])
                return last

            def first_count(ii, u):
                if u % TT == 0:
                    return
                k = searched(ii, u)
                dve.wait_ge(copied, k + 1)
                dve.wait_ge(moved[0], k + 1)
                count_scores(ii, u, 0).then_inc(counted[0], 1)

            def select(ii, u):
                slot, qt, n = u % SLOTS, u % TT, ii * UNITS + u
                L = (qt + 1) * P
                done = [0]

                def signal(last):
                    done[0] += 1
                    last.then_inc(step_done, 1)

                def settle(last):
                    signal(last)
                    dve.wait_ge(step_done, done[0])

                if qt == 0:
                    dve.wait_ge(exped, after(n + 1))
                    nc.vector.reciprocal(rinv[:, slot, :], rsum[:, slot, :]).then_inc(kept, 1)
                    return
                k = searched(ii, u)
                dve.sem_clear(step_done)
                wait_apart(dve, exped, after(n + 1), passed)
                dve.wait_ge(moved[4], k + 1)
                signal(count_scores(ii, u, 4))
                for j in range(R0):
                    row = scores_sb[slot][:, j, 0:L]
                    last = nc.vector.scalar_tensor_tensor(out=row, in0=row, scalar=thr[:, slot, j:j + 1],
                                                          in1=exps[slot][:, j, 0:L], op0=ALU.is_lt, op1=ALU.mult)
                settle(last)
                nc.vector.tensor_scalar(missing[:], count[:, slot, 4, :], -1.0, float(KEEP), ALU.mult, ALU.add)\
                    .then_inc(step_done, 1)
                done[0] += 1
                for j in range(R0):
                    nc.vector.max(top[:, j, 1:TOP + 1], scores_sb[slot][:, j, 0:L])
                dve.wait_ge(step_done, done[0])
                last = nc.vector.tensor_tensor(hot[:], iota[:], bcast(missing[:], 2, TOP), ALU.is_equal)
                settle(last)
                for side in range(2):
                    last = nc.vector.tensor_tensor(picked[:, :, side, :], hot[:], top[:, :, side:side + TOP], ALU.mult)
                settle(last)
                settle(nc.vector.tensor_reduce(bound[:], picked[:], AX.X, ALU.add))
                nc.vector.scalar_tensor_tensor(out=unsure[:, 0:R0], in0=bound[:, :, 0], scalar=1.0, in1=bound[:, :, 1],
                                               op0=ALU.mult, op1=ALU.is_le,
                                               accum_out=unsure[:, R0:R0 + 1]).then_inc(rated, 1)
                for j in range(R0):
                    row = exps[slot][:, j, 0:L]
                    last = nc.vector.scalar_tensor_tensor(out=scores_sb[slot][:, j, 0:L], in0=row,
                                                          scalar=bound[:, j, 1:2], in1=row, op0=ALU.is_gt,
                                                          op1=ALU.mult, accum_out=rsum[:, slot, j:j + 1])
                signal(last)
                assert done[0] == SELECT_STEPS

            def select_again(slot, L, j):
                rest, largest = scores_sb[slot][:, j, 0:L], top[:, j, 1:TOP + 1]
                done = [0]

                def settle(last):
                    done[0] += 1
                    last.then_inc(step_done, 1)
                    dve.wait_ge(step_done, done[0])

                dve.sem_clear(step_done)
                for r in range(ROUNDS):
                    src = exps[slot][:, j, 0:L] if r == 0 else rest
                    settle(nc.vector.max(largest, src))
                    settle(nc.vector.match_replace(rest, largest, src, 0.0))
                settle(nc.vector.scalar_tensor_tensor(
                    out=rest, in0=exps[slot][:, j, 0:L], scalar=1.0, in1=rest,
                    op0=ALU.mult, op1=ALU.subtract, accum_out=rsum[:, slot, j:j + 1]))

            def finish(ii, u):
                slot, qt = u % SLOTS, u % TT
                if qt == 0:
                    return
                dve.wait_ge(step_done, SELECT_STEPS)
                wait_apart(dve, flagged, searched(ii, u) + 1, passed)
                rows = dve.value_load(unsure_int[0:1, R0:R0 + 1])
                with dve.If(rows > 0):
                    for j in range(R0):
                        rows_of_head = dve.value_load(unsure_int[0:1, j:j + 1])
                        with dve.If(rows_of_head > 0):
                            select_again(slot, (qt + 1) * P, j)
                nc.vector.reciprocal(rinv[:, slot, :], rsum[:, slot, :]).then_inc(kept, 1)

            def step(has):
                has(finish, 0)
                has(select, 1)
                has(statistics, 6)
                has(first_count, 5)

            dve.wait_ge(consts_ready, 4)
            turns(dve, step)

        @block.gpsimd
        def _(pool):
            t = nc.gpsimd
            pool.wait_ge(consts_in, 48)
            t.tensor_copy(mask[:], mask32[:]).then_inc(consts_ready, 1)
            t.memset(half[:], 0.5).then_inc(consts_ready, 1)
            t.memset(top[:], 0.0).then_inc(consts_ready, 1)
            t.memset(tmp[:], 0.0).then_inc(consts_ready, 1)

            def chain():
                pool.sem_clear(chained)
                done = [0]

                def settle(last):
                    done[0] += 1
                    last.then_inc(chained, 1)
                    pool.wait_ge(chained, done[0])

                return settle

            def first_guess(ii, u):
                slot, qt = u % SLOTS, u % TT
                if qt == 0:
                    return
                wait_apart(pool, stated, ii * UNITS + u + 1, pool_passed)
                st = stats[:, slot, :, :]
                settle = chain()
                var, dev, mean, sd = (tmp[:, slot, 0, x, :] for x in range(4))
                t.tensor_tensor(dev, st[:, :, 1], st[:, :, 4], ALU.subtract)
                t.tensor_tensor(var, st[:, :, 2], st[:, :, 5], ALU.add)
                settle(t.tensor_tensor(mean, st[:, :, 1], st[:, :, 4], ALU.add))
                t.tensor_tensor(dev, dev, dev, ALU.mult)
                t.tensor_scalar(mean, mean, 0.5, 0.0, ALU.mult, ALU.add)
                settle(t.tensor_scalar(var, var, 4.0 / (qt * P), 0.0, ALU.mult, ALU.add))
                settle(t.tensor_tensor(var, var, dev, ALU.add))
                settle(t.tensor_tensor(sd, var, half[:], ALU.pow))
                t.tensor_scalar(slope[:, slot, :], sd, guess[:, qt, 1:2], None, ALU.mult)
                settle(t.tensor_scalar(sd, sd, guess[:, qt, 0:1], None, ALU.mult))
                t.tensor_tensor(thr[:, slot, :], sd, mean, ALU.add).then_inc(moved[0], 1)

            def move(c):
                def stage(ii, u):
                    slot, qt = u % SLOTS, u % TT
                    if qt == 0:
                        return
                    k = searched(ii, u)
                    L = (qt + 1) * P
                    wait_apart(pool, counted[c], k + 1, pool_passed)
                    new, old = error[:, slot, c % 2, :], error[:, slot, (c + 1) % 2, :]
                    settle = chain()
                    by, turn, more, outside = (tmp[:, slot, c + 1, x, :] for x in range(4))
                    rate = slope[:, slot, :]
                    if c == 0:
                        settle(t.tensor_scalar(new, count[:, slot, c, :], 1.0, -TARGET, ALU.mult, ALU.add))
                        settle(t.tensor_tensor(by, new, rate, ALU.mult))
                    else:
                        settle(t.tensor_scalar(new, count[:, slot, c, :], -0.5, L / 2 - TARGET, ALU.mult, ALU.add))
                        t.tensor_tensor(by, new, rate, ALU.mult)
                        t.tensor_tensor(outside, new, new, ALU.mult)
                        settle(t.tensor_tensor(turn, new, old, ALU.mult))
                        t.tensor_scalar(outside, outside, WITHIN * WITHIN, 1.0, ALU.is_gt, ALU.mult)
                        settle(t.tensor_scalar(turn, turn, 0.0, -0.5, ALU.is_lt, ALU.mult))
                        settle(t.tensor_tensor(by, by, outside, ALU.mult))
                        t.tensor_tensor(more, by, turn, ALU.mult)
                        settle(t.tensor_tensor(turn, rate, turn, ALU.mult))
                        t.tensor_tensor(rate, rate, turn, ALU.add)
                        settle(t.tensor_tensor(by, by, more, ALU.add))
                    t.tensor_tensor(thr[:, slot, :], thr[:, slot, :], by, ALU.add).then_inc(moved[c + 1], 1)
                return stage

            def flag(ii, u):
                if u % TT == 0:
                    return
                k = searched(ii, u)
                wait_apart(pool, rated, k + 1, pool_passed)
                t.partition_all_reduce(unsure_all[:], unsure[:], P, bass.bass_isa.ReduceOp.add)\
                    .then_inc(reduced, 1)
                wait_apart(pool, reduced, k + 1, pool_passed)
                t.tensor_copy(unsure_int[:], unsure_all[:]).then_inc(flagged, 1)

            def step(has):
                has(move(3), 2)
                has(flag, 1)
                has(move(2), 3)
                has(move(1), 4)
                has(first_guess, 6)
                has(move(0), 5)

            turns(pool, step)

        @block.scalar
        def _(act):
            start_ahead(act, exped, pT_out, scaled)

            def exponentials(ii, u):
                slot, qt, n = u % SLOTS, u % TT, ii * UNITS + u
                L = (qt + 1) * P
                act.wait_ge(stated, n + 1)
                if qt >= 1:
                    nc.scalar.activation(scores_sb[slot][:, :, 0:L], ps_s[:, :, 0:L], ACT.Copy).then_inc(copied, 1)
                for j in range(R0):
                    sums = {"accum_out": rsum[:, slot, j:j + 1]} if qt == 0 else {}
                    last = nc.scalar.activation(exps[slot][:, j, 0:L], ps_s[:, j, 0:L], ACT.Exp,
                                                bias=nmax[:, slot, j:j + 1], **sums)
                last.then_inc(exped, 1)

            def count_scores(c):
                def stage(ii, u):
                    slot, qt = u % SLOTS, u % TT
                    if qt == 0:
                        return
                    L = (qt + 1) * P
                    act.wait_ge(moved[c], searched(ii, u) + 1)
                    for j in range(R0):
                        last = nc.scalar.activation(junk_act[:, c - 1, j, 0:L], scores_sb[slot][:, j, 0:L], ACT.Sign,
                                                    bias=thr[:, slot, j:j + 1], scale=-1.0,
                                                    accum_out=count[:, slot, c, j:j + 1])
                    last.then_inc(counted[c], 1)
                return stage

            def probs_out(kb):
                def stage(ii, u):
                    if kb > u % TT:
                        return
                    bank, c = chunk(ii, u, kb)
                    act.wait_ge(turned[bank], c + 1)
                    act.wait_ge(attended[bank], after(c))
                    nc.scalar.activation(pT[:, bank, :], ps_t[:, bank, :], ACT.Copy).then_inc(pT_out[bank], 1)
                return stage

            def output(ii, u):
                s, slot, qt, i = u % 2, u % SLOTS, u % TT, ii * 2 + u // TT
                bank, c = chunk(ii, u, qt)
                act.wait_ge(attended[bank], after(c + 1))
                act.wait_ge(kept, ii * UNITS + u + 1)
                for j in range(R0):
                    last = nc.scalar.activation(o_all[:, i, qt, j * HD0:(j + 1) * HD0],
                                                ps_o[:, s, j * HD0:(j + 1) * HD0], ACT.Copy,
                                                scale=rinv[:, slot, j:j + 1])
                last.then_inc(scaled, 1)

            def step(has):
                has(count_scores(3), 2)
                has(probs_out(0), 0)
                has(count_scores(2), 3)
                has(probs_out(1), 0)
                has(count_scores(1), 4)
                has(probs_out(2), 0)
                has(probs_out(3), 0)
                has(exponentials, 6)
                has(output, 0)

            turns(act, step)




class Norm:

    def __init__(self, m):
        self.res = m.sbuf("res", [P, 2, D])
        self.xn = m.sbuf("xn", [P, 2, D])
        self.stats = m.sbuf("stats", [P, 2, 6])
        self.mv = m.sbuf("mv", [P, 2, 2])
        self.sd = m.sbuf("sd", [P, 2, 1])
        self.rstd = m.sbuf("rstd", [P, 2, 1])
        self.summed = m.sems("n_summed")
        self.stated = m.sems("n_stated")
        self.meaned = m.sems("n_meaned")
        self.rooted = m.sems("n_rooted")
        self.inverted = m.sems("n_inverted")
        self.normed = m.sems("n_normed")
        self.passed = m.sem("n_passed")
        self.pool_passed = m.sem("n_pool_passed")

    def on_dve(self, nc, dve, s, k2, out=None):
        out = self.xn[:, s, :] if out is None else out
        dve.wait_ge(self.summed[s], after(k2 + 1))
        nc.vector.bn_stats(self.stats[:, s, :], self.res[:, s, :]).then_inc(self.stated[s], 1)
        wait_apart(dve, self.stated[s], k2 + 1, self.passed)
        nc.vector.bn_aggr(self.mv[:, s, :], self.stats[:, s, :]).then_inc(self.meaned[s], 1)
        dve.wait_ge(self.rooted[s], k2 + 1)
        nc.vector.reciprocal(self.rstd[:, s, :], self.sd[:, s, :]).then_inc(self.inverted[s], 1)
        dve.wait_ge(self.inverted[s], k2 + 1)
        nc.vector.tensor_scalar(out, self.res[:, s, :], self.mv[:, s, 0:1], self.rstd[:, s, :],
                                ALU.subtract, ALU.mult).then_inc(self.normed[s], 1)

    def on_act(self, nc, act, s, k2, eps):
        act.wait_ge(self.meaned[s], k2 + 1)
        nc.scalar.activation(self.sd[:, s, :], self.mv[:, s, 1:2], ACT.Sqrt, bias=eps[:, 0:1])\
            .then_inc(self.rooted[s], 1)




def project_out0(nc, a, ident, eps, x_all, xT_all):
    with ExitStack() as ctx:
        m = Place(nc, ctx, "o0_")
        w = m.sbuf("w", [P, KC, D])
        rows = m.sbuf("rows", [P, TT, D])
        rowsT = m.sbuf("rowsT", [P, 2, D])
        x = m.sbuf("x", [P, 2, D])
        norm = Norm(m)
        ps_t = m.psum("ps_t", [P, 2, D])
        ps_y = m.psum("ps_y", [P, 2, D])
        ps_n = m.psum("ps_n", [P, 2, D])
        w_in = m.sem("w_in")
        x_in = m.sems("x_in")
        gathered = m.sem("gathered")
        turned = m.sems("turned")
        rowsT_out = m.sems("rowsT_out")
        projected = m.sems("projected")
        copied = m.sems("copied")
        xn_turned = m.sems("xn_turned")
        xT_out = m.sems("xT_out")

        block = ctx.enter_context(nc.Block())
        o_view = x_all[:].rearrange("p b (g t c) -> p b t g c", g=G0, t=TT)
        x_view = x_all[:].rearrange("p b (t c) -> p b t c", t=TT)

        @block.sync
        def _(sp):
            sp.dma_start(w[:], a["wo0T"].rearrange("(k p) n -> p k n", p=P)).then_inc(w_in, 16)
            src = a["x"].rearrange("(b t p) n -> b t p n", b=NB, t=TT)
            with sp.Fori(0, NB) as b:
                for t in range(TT):
                    s, k2 = t % 2, b * 2 + t // 2
                    sp.wait_ge(norm.summed[s], after(k2))
                    sp.dma_start(x[:, s, :], src[b, t]).then_inc(x_in[s], 16)

        @block.gpsimd
        def _(pool):
            start_ahead(pool, copied)
            with pool.Fori(0, NB) as b:
                wait_apart(pool, gathered, b * TT + TT, norm.pool_passed)
                for t in range(TT):
                    s, k2 = t % 2, b * 2 + t // 2
                    wait_apart(pool, norm.normed[s], after(k2 + 1), norm.pool_passed)
                    nc.gpsimd.tensor_copy(x_view[:, b, t, :], norm.xn[:, s, :]).then_inc(copied[s], 1)

        @block.tensor
        def _(pe):
            start_ahead(pe, turned, projected, xn_turned)
            pe.wait_ge(w_in, 16)

            def turn(b, t):
                s, k2 = t % 2, b * 2 + t // 2
                pe.wait_ge(gathered, b * TT + t + 1)
                pe.wait_ge(rowsT_out[s], after(k2))
                for k in range(KC):
                    last = nc.tensor.transpose(ps_t[:, s, k * P:(k + 1) * P], rows[:, t, k * P:(k + 1) * P], ident[:])
                last.then_inc(turned[s], 1)

            def project(b, t):
                s, k2 = t % 2, b * 2 + t // 2
                pe.wait_ge(rowsT_out[s], after(k2 + 1))
                pe.wait_ge(norm.summed[s], after(k2))
                for k in range(KC):
                    last = nc.tensor.matmul(ps_y[:, s, :], rowsT[:, s, k * P:(k + 1) * P], w[:, k, :],
                                            start=(k == 0), stop=(k == KC - 1))
                last.then_inc(projected[s], 1)

            def turn_xn(b, t):
                transpose_rows(nc, pe, ident, norm, t % 2, b * 2 + t // 2, ps_n, xn_turned, xT_out)

            def step(has):
                has(turn, 3)
                has(turn_xn, 0)
                has(project, 2)

            tiles(pe, step, 3)

        @block.scalar
        def _(act):
            start_ahead(act, rowsT_out, xT_out)

            def gather(b, t):
                act.wait_ge(turned[t % 2], after(b * 2 + t // 2 - 1))
                nc.scalar.activation(rows[:, t, :].rearrange("p (g c) -> p g c", g=G0), o_view[:, b, t, :, :],
                                     ACT.Copy).then_inc(gathered, 1)

            def rows_out(b, t):
                s, k2 = t % 2, b * 2 + t // 2
                act.wait_ge(turned[s], after(k2 + 1))
                act.wait_ge(projected[s], after(k2))
                nc.scalar.activation(rowsT[:, s, :], ps_t[:, s, :], ACT.Copy).then_inc(rowsT_out[s], 1)

            def root(b, t):
                norm.on_act(nc, act, t % 2, b * 2 + t // 2, eps)

            def xn_out(b, t):
                s, k2 = t % 2, b * 2 + t // 2
                act.wait_ge(xn_turned[s], after(k2 + 1))
                nc.scalar.activation(xT_all[:, :, b, t * P:(t + 1) * P],
                                     ps_n[:, s, :].rearrange("p (k c) -> p k c", k=KC), ACT.Copy)\
                    .then_inc(xT_out[s], 1)

            def step(has):
                has(gather, TT)
                has(rows_out, 3)
                has(xn_out, 0)
                has(root, 2)

            tiles(act, step, TT)

        @block.vector
        def _(dve):
            start_ahead(dve, norm.summed, norm.normed)
            with dve.Fori(0, NB) as b:
                for t in range(TT):
                    s, k2 = t % 2, b * 2 + t // 2
                    dve.wait_ge(projected[s], after(k2 + 1))
                    dve.wait_ge(x_in[s], 16 * (k2 + 1))
                    nc.vector.tensor_tensor(norm.res[:, s, :], ps_y[:, s, :], x[:, s, :], ALU.add)\
                        .then_inc(norm.summed[s], 1)
                    dve.wait_ge(copied[s], after(k2))
                    dve.wait_ge(xn_turned[s], after(k2))
                    norm.on_dve(nc, dve, s, k2)


def transpose_rows(nc, pe, ident, norm, s, k2, ps, turned, out):
    pe.wait_ge(norm.normed[s], after(k2 + 1))
    pe.wait_ge(out[s], after(k2))
    for k in range(KC):
        last = nc.tensor.transpose(ps[:, s, k * P:(k + 1) * P], norm.xn[:, s, k * P:(k + 1) * P], ident[:])
    last.then_inc(turned[s], 1)




def feed_forward0(nc, eps, x_all, xT_all, w_gu, w_dn):
    USES = [(FT + 1 - f) // 2 for f in range(2)]
    with ExitStack() as ctx:
        m = Place(nc, ctx, "f0_")
        hT = m.sbuf("hT", [P, FT, S])
        silu = m.sbuf("silu", [P, 2, S])
        norm = Norm(m)
        ps_g = m.psum("ps_g", [P, 2, S])
        ps_u = m.psum("ps_u", [P, 2, S])
        ps_y = m.psum("ps_y", [P, 2, D])
        up_done = m.sems("up_done")
        silu_done = m.sems("silu_done")
        gated = m.sems("gated")
        projected = m.sems("projected")
        copied = m.sems("copied")

        block = ctx.enter_context(nc.Block())
        x_view = x_all[:].rearrange("p b (t c) -> p b t c", t=TT)

        @block.tensor
        def _(pe):
            start_ahead(pe, projected)
            with pe.Fori(0, NB) as b:
                for f in range(FT):
                    s, c, r = f % 2, b * USES[f % 2] + f // 2, rows_of(f)
                    pe.wait_ge(gated[s], after(c))
                    for ps, col in ((ps_g, f * P), (ps_u, INTER + f * P)):
                        for k in range(KC):
                            last = nc.tensor.matmul(ps[0:r, s, :], w_gu[:, k, col:col + r], xT_all[:, k, b, :],
                                                    start=(k == 0), stop=(k == KC - 1))
                    last.then_inc(up_done[s], 1)
                for s in range(2):
                    pe.wait_ge(gated[s], after((b + 1) * USES[s]))
                for t in range(TT):
                    s, k2 = t % 2, b * 2 + t // 2
                    pe.wait_ge(norm.summed[s], after(k2))
                    for f in range(FT):
                        last = nc.tensor.matmul(ps_y[:, s, :], hT[0:rows_of(f), f, t * P:(t + 1) * P],
                                                w_dn[0:rows_of(f), f, :], start=(f == 0), stop=(f == FT - 1))
                    last.then_inc(projected[s], 1)

        @block.scalar
        def _(act):
            with act.Fori(0, NB) as b:
                for f in range(FT):
                    s, c, r = f % 2, b * USES[f % 2] + f // 2, rows_of(f)
                    act.wait_ge(up_done[s], c + 1)
                    act.wait_ge(gated[s], after(c))
                    nc.scalar.activation(silu[0:r, s, :], ps_g[0:r, s, :], ACT.Silu).then_inc(silu_done[s], 1)
                for t in range(TT):
                    s, k2 = t % 2, b * 2 + t // 2
                    norm.on_act(nc, act, s, k2, eps)

        @block.vector
        def _(dve):
            start_ahead(dve, gated, norm.summed, norm.normed)
            with dve.Fori(0, NB) as b:
                for f in range(FT):
                    s, c, r = f % 2, b * USES[f % 2] + f // 2, rows_of(f)
                    dve.wait_ge(silu_done[s], c + 1)
                    nc.vector.tensor_tensor(hT[0:r, f, :], ps_u[0:r, s, :], silu[0:r, s, :], ALU.mult)\
                        .then_inc(gated[s], 1)
                for t in range(TT):
                    s, k2 = t % 2, b * 2 + t // 2
                    dve.wait_ge(projected[s], after(k2 + 1))
                    nc.vector.tensor_tensor(norm.res[:, s, :], ps_y[:, s, :], x_view[:, b, t, :], ALU.add)\
                        .then_inc(norm.summed[s], 1)
                    dve.wait_ge(copied[s], after(k2))
                    norm.on_dve(nc, dve, s, k2)

        @block.gpsimd
        def _(pool):
            start_ahead(pool, copied)
            with pool.Fori(0, NB) as b:
                for t in range(TT):
                    s, k2 = t % 2, b * 2 + t // 2
                    wait_apart(pool, norm.normed[s], after(k2 + 1), norm.pool_passed)
                    nc.gpsimd.tensor_copy(x_view[:, b, t, :], norm.xn[:, s, :]).then_inc(copied[s], 1)




def attend_layer1(nc, a, ident, ident16, x_all):
    HP = R1 // 2
    PADS = S + WIN
    with ExitStack() as ctx:
        m = Place(nc, ctx, "a1_")
        w_high = m.sbuf("w_high", [P, KC, W1], F32R)
        w_low = m.sbuf("w_low", [P, KC, W1], F32R)
        wo_high = m.sbuf("wo_high", [P, R1, D], F32R)
        wo_low = m.sbuf("wo_low", [P, R1, D], F32R)
        loaded = m.sbuf("loaded", [P, KC * W1])
        xT_high = m.sbuf("xT_high", [P, KC, NB, S], F32R)
        xT_low = m.sbuf("xT_low", [P, KC, NB, S], F32R)
        mask = m.sbuf("mask", [P, NW, P], BF16)
        qT = m.sbuf("qT", [P, HP, NW, 2 * WIN])
        kT = m.sbuf("kT", [P, PADS])
        vT = m.sbuf("vT", [P, PADS])
        vw = m.sbuf("vw", [P, NW, HD1])
        probs = m.sbuf("probs", [P, HP, NW, P])
        pT = m.sbuf("pT", [P, HP, NW, P])
        oT_high = m.sbuf("oT_high", [P, R1, S], F32R)
        oT_low = m.sbuf("oT_low", [P, R1, S], F32R)
        mx = m.sbuf("mx", [P, HP, NW])
        rsum = m.sbuf("rsum", [P, HP, NW])
        rinv = m.sbuf("rinv", [P, HP, NW])
        ps = m.psum("ps", [P, 4, 512])
        ps_p = m.psum("ps_p", [P, 2, 512])
        ps_y = m.psum("ps_y", [P, 2, D])
        mask_in = m.sem("mask_in")
        x_turned = m.sem("x_turned")
        x_high = m.sem("x_high")
        x_split = m.sem("x_split")
        w_in = m.sem("w_in")
        wo_in = m.sem("wo_in")
        w_rounded = m.sem("w_rounded")
        w_split = m.sem("w_split")
        wo_rounded = m.sem("wo_rounded")
        wo_split = m.sem("wo_split")
        padded = m.sem("padded")
        kv_done = m.sem("kv_done")
        q_done = m.sem("q_done")
        kv_out = m.sem("kv_out")
        q_out = m.sem("q_out")
        scored = m.sem("scored")
        maxed = m.sem("maxed")
        shifted = m.sem("shifted")
        exped = m.sem("exped")
        rsummed = m.sem("rsummed")
        inverted = m.sem("inverted")
        normed = m.sem("normed")
        v_turned = m.sem("v_turned")
        vw_out = m.sem("vw_out")
        p_turned = m.sem("p_turned")
        pT_out = m.sem("pT_out")
        attended = m.sem("attended")
        oT_rounded = m.sem("oT_rounded")
        oT_out = m.sem("oT_out")
        projected = m.sem("projected")
        added = m.sem("added")

        block = ctx.enter_context(nc.Block())
        scale = float(HD1) ** -0.5
        x_view = x_all[:].rearrange("p b (t c) -> p b t c", t=TT)
        banks = [ps[:, 0:2, :].rearrange("p b (w c) -> p (b w) c", c=P),
                 ps[:, 2:4, :].rearrange("p b (w c) -> p (b w) c", c=P)]

        w_loaded = loaded[:].rearrange("p (k c) -> p k c", k=KC)
        wo_loaded = loaded[:, 0:R1 * D].rearrange("p (j c) -> p j c", j=R1)

        def oT_windows(oT, j):
            return oT[:, j, :].rearrange("p (w c) -> p w c", c=WIN)

        def items(eng, body):

            def group(g, last):
                body(g, 0, g * NB, True, False, 1)
                with eng.Fori(1, NB - 1) as b:
                    body(g, b, g * NB + b, False, False, b + 1)
                body(g, NB - 1, g * NB + NB - 1, False, not last, None if last else 0)

            with eng.Fori(0, G1 - 1) as g:
                group(g, False)
            group(G1 - 1, True)

        @block.sync
        def _(sp):
            sp.dma_start(probs[:, 0, :, :], a["window"]).then_inc(mask_in, 16)
            sp.dma_start(w_loaded, a["w1T"][0]).then_inc(w_in, 16)
            sp.wait_ge(w_split, 1)
            sp.dma_start(wo_loaded, a["wo1T"][0]).then_inc(wo_in, 16)
            with sp.Fori(1, G1) as g:
                sp.wait_ge(wo_split, g)
                sp.dma_start(w_loaded, a["w1T"][g]).then_inc(w_in, 16)
                sp.wait_ge(w_split, g + 1)
                sp.dma_start(wo_loaded, a["wo1T"][g]).then_inc(wo_in, 16)

        @block.tensor
        def _(pe):
            start_ahead(pe, q_done, projected)
            for b in range(NB):
                for t in range(TT):
                    pe.wait_ge(x_split, after((b - 1) * TT + t + 1))
                    for k in range(KC):
                        last = nc.tensor.transpose(ps[:, t, k * P:(k + 1) * P], x_view[:, b, t, k * P:(k + 1) * P],
                                                   ident[:])
                    last.then_inc(x_turned, 1)
            pe.wait_ge(padded, 3)

            def project(n, b):
                cols = slice(((n + R1) if n < 2 else (n - 2)) * HD1, ((n + R1) if n < 2 else (n - 2)) * HD1 + HD1)
                for k in range(KC):
                    nc.tensor.matmul(ps_p[:, n % 2, :], w_low[:, k, cols], xT_high[:, k, b, :], start=(k == 0), stop=False)
                    nc.tensor.matmul(ps_p[:, n % 2, :], w_high[:, k, cols], xT_low[:, k, b, :],
                                     start=False, stop=False)
                    last = nc.tensor.matmul(ps_p[:, n % 2, :], w_high[:, k, cols], xT_high[:, k, b, :],
                                            start=False, stop=(k == KC - 1))
                last.then_inc(kv_done if n < 2 else q_done, 1)

            def project_query(j, b, i):
                if j < 2:
                    pe.wait_ge(kv_out, 2 * i + j + 1)
                else:
                    pe.wait_ge(q_out, 4 * i + j - 1)
                project(j + 2, b)

            def body(g, b, i, first, last_of_group, b_next):
                def scores(hp):
                    for half in range(2):
                        for q in range(4):
                            wi = 4 * half + q
                            nc.tensor.matmul(banks[hp][:, wi, :], qT[:, hp, wi, :], kT[:, wi * WIN:wi * WIN + P],
                                             start=(q == 0), stop=False, skip_group_check=True)
                        last = nc.tensor.matmul(ps[:, 2 * hp + half, :], ident16[:],
                                                mask[:, 4 * half:4 * half + 4, :].rearrange("p w c -> p (w c)"),
                                                start=False, stop=True, skip_group_check=True)
                    last.then_inc(scored, 1)

                def turn_probs(hp):
                    pe.wait_ge(normed, 2 * i + hp + 1)
                    for wi in range(NW):
                        last = nc.tensor.transpose(banks[hp][:, wi, :], probs[:, hp, wi, :], ident[:])
                    last.then_inc(p_turned, 1)

                def attend(hp):
                    pe.wait_ge(pT_out, 2 * i + hp + 1)
                    for wi in range(NW):
                        last = nc.tensor.matmul(banks[hp][:, wi, :], vw[:, wi, :], pT[:, hp, wi, :],
                                                start=(wi % 4 == 0), stop=True, skip_group_check=True)
                    last.then_inc(attended, 1)

                def project_next(n):
                    if b_next is None:
                        return
                    if n == 0 and last_of_group:
                        pe.wait_ge(w_split, g + 2)
                    if n < 2:
                        project(n, b_next)
                    else:
                        project_query(n - 2, b_next, i + 1)

                pe.wait_ge(kv_out, 2 * i + 2)
                pe.wait_ge(q_out, 4 * i + 4)
                scores(0)
                scores(1)
                project_next(0)
                pe.wait_ge(shifted, 2 * i + 1)
                for wi in range(NW):
                    last = nc.tensor.transpose(banks[0][:, wi, :], vT[:, wi * WIN:wi * WIN + P], ident[:])
                last.then_inc(v_turned, 1)
                project_next(1)
                pe.wait_ge(vw_out, i + 1)
                turn_probs(0)
                project_next(2)
                turn_probs(1)
                project_next(3)
                attend(0)
                attend(1)
                project_next(4)
                project_next(5)
                if first:
                    pe.wait_ge(wo_split, g + 1)
                pe.wait_ge(oT_out, 2 * i + 2)
                for t in range(TT):
                    pe.wait_ge(added, after(4 * i + t - 1))
                    rows = slice(t * P, (t + 1) * P)
                    for j in range(R1):
                        nc.tensor.matmul(ps_y[:, t % 2, :], oT_low[:, j, rows], wo_high[:, j, :],
                                         start=(j == 0), stop=False)
                        nc.tensor.matmul(ps_y[:, t % 2, :], oT_high[:, j, rows], wo_low[:, j, :],
                                         start=False, stop=False)
                        last = nc.tensor.matmul(ps_y[:, t % 2, :], oT_high[:, j, rows], wo_high[:, j, :],
                                                start=False, stop=(j == R1 - 1))
                    last.then_inc(projected, 1)

            pe.wait_ge(w_split, 1)
            pe.wait_ge(x_split, after(NB * TT))
            project(0, 0)
            project(1, 0)
            for j in range(R1):
                project_query(j, 0, 0)
            items(pe, body)

        @block.scalar
        def _(act):
            def key_value(n, i):
                act.wait_ge(kv_done, 2 * i + n + 1)
                dst = (kT, vT)[n]
                nc.scalar.activation(dst[:, WIN:PADS], ps_p[:, n, :], ACT.Copy).then_inc(kv_out, 1)

            def query(j, i):
                act.wait_ge(q_done, after(4 * i + j + 1))
                dst = qT[:, j // 2, :, (j % 2) * WIN:(j % 2 + 1) * WIN]
                nc.scalar.activation(dst, ps_p[:, j % 2, :].rearrange("p (w c) -> p w c", c=WIN), ACT.Copy)\
                    .then_inc(q_out, 1)

            def round_weights(g):
                act.wait_ge(w_in, 16 * (g + 1))
                act.wait_ge(q_done, after(g * (NB * R1)))
                nc.scalar.activation(w_high[:], w_loaded, ACT.Copy).then_inc(w_rounded, 1)

            def body(g, b, i, first, last_of_group, b_next):
                def exponential(hp):
                    act.wait_ge(shifted, 2 * i + hp + 1)
                    nc.scalar.activation(probs[:, hp, :, :], probs[:, hp, :, :], ACT.Exp, scale=scale)\
                        .then_inc(exped, 1)

                def turned(hp):
                    act.wait_ge(p_turned, 2 * i + hp + 1)
                    nc.scalar.activation(pT[:, hp, :, :], banks[hp], ACT.Copy).then_inc(pT_out, 1)

                def round_output(hp):
                    act.wait_ge(attended, 2 * i + hp + 1)
                    for h in range(2):
                        last = nc.scalar.activation(oT_windows(oT_high, 2 * hp + h),
                                                    banks[hp][:, :, h * WIN:(h + 1) * WIN], ACT.Copy)
                    last.then_inc(oT_rounded, 1)

                def next_out(out, n):
                    if b_next is not None:
                        out(n, i + 1)

                if last_of_group:
                    round_weights(g + 1)
                exponential(0)
                exponential(1)
                next_out(key_value, 0)
                next_out(key_value, 1)
                turned(0)
                next_out(query, 0)
                if first:
                    act.wait_ge(wo_in, 16 * (g + 1))
                    act.wait_ge(projected, after(g * (NB * TT)))
                    nc.scalar.activation(wo_high[:], wo_loaded, ACT.Copy).then_inc(wo_rounded, 1)
                turned(1)
                next_out(query, 1)
                round_output(0)
                round_output(1)
                next_out(query, 2)
                next_out(query, 3)

            act.wait_ge(padded, 3)
            with act.Fori(0, NB) as b:
                for t in range(TT):
                    act.wait_ge(x_turned, b * TT + t + 1)
                    nc.scalar.activation(xT_high[:, :, b, t * P:(t + 1) * P],
                                         ps[:, t, :].rearrange("p (k c) -> p k c", k=KC), ACT.Copy).then_inc(x_high, 1)
            round_weights(0)
            for n in range(2):
                key_value(n, 0)
            for j in range(R1):
                query(j, 0)
            items(act, body)

        @block.gpsimd
        def _(pool):
            nc.gpsimd.memset(kT[:, 0:WIN], 0.0).then_inc(padded, 1)
            nc.gpsimd.memset(vT[:, 0:WIN], 0.0).then_inc(padded, 1)
            pool.wait_ge(mask_in, 16)
            nc.gpsimd.tensor_copy(mask[:], probs[:, 0, :, :]).then_inc(padded, 1)

            def body(g, b, i, first, last_of_group, b_next):
                for hp in range(HP):
                    pool.wait_ge(inverted, 2 * i + hp + 1)
                    nc.gpsimd.tensor_tensor(probs[:, hp, :, :], probs[:, hp, :, :],
                                            bcast(rinv[:, hp, :], 2, P), ALU.mult).then_inc(normed, 1)

            items(pool, body)

        @block.vector
        def _(dve):
            start_ahead(dve, added, x_split)

            def low_weights(g):
                dve.wait_ge(w_rounded, g + 1)
                nc.vector.tensor_tensor(w_low[:], w_loaded, w_high[:].bitcast(F32), ALU.subtract)\
                    .then_inc(w_split, 1)

            def body(g, b, i, first, last_of_group, b_next):
                def shift(hp):
                    dve.wait_ge(scored, 2 * i + hp + 1)
                    nc.vector.tensor_reduce(mx[:, hp, :], banks[hp], AX.X, ALU.max).then_inc(maxed, 1)
                    dve.wait_ge(maxed, 2 * i + hp + 1)
                    nc.vector.tensor_tensor(probs[:, hp, :, :], banks[hp], bcast(mx[:, hp, :], 2, P),
                                            ALU.subtract).then_inc(shifted, 1)

                def invert(hp):
                    dve.wait_ge(exped, 2 * i + hp + 1)
                    nc.vector.tensor_reduce(rsum[:, hp, :], probs[:, hp, :, :], AX.X, ALU.add).then_inc(rsummed, 1)
                    dve.wait_ge(rsummed, 2 * i + hp + 1)
                    nc.vector.reciprocal(rinv[:, hp, :], rsum[:, hp, :]).then_inc(inverted, 1)

                def output(hp):
                    dve.wait_ge(oT_rounded, 2 * i + hp + 1)
                    for h in range(2):
                        last = nc.vector.tensor_tensor(oT_windows(oT_low, 2 * hp + h),
                                                       banks[hp][:, :, h * WIN:(h + 1) * WIN],
                                                       oT_windows(oT_high, 2 * hp + h).bitcast(F32), ALU.subtract)
                    last.then_inc(oT_out, 1)

                if last_of_group:
                    low_weights(g + 1)
                shift(0)
                shift(1)
                invert(0)
                dve.wait_ge(v_turned, i + 1)
                nc.vector.tensor_copy(vw[:], banks[0]).then_inc(vw_out, 1)
                invert(1)
                if first:
                    dve.wait_ge(wo_rounded, g + 1)
                    nc.vector.tensor_tensor(wo_low[:], wo_loaded, wo_high[:].bitcast(F32), ALU.subtract)\
                        .then_inc(wo_split, 1)
                output(0)
                output(1)
                for t in range(TT):
                    dve.wait_ge(projected, after(4 * i + t + 1))
                    nc.vector.tensor_tensor(x_view[:, b, t, :], ps_y[:, t % 2, :], x_view[:, b, t, :], ALU.add)\
                        .then_inc(added, 1)

            with dve.Fori(0, NB) as b:
                for t in range(TT):
                    dve.wait_ge(x_high, b * TT + t + 1)
                    nc.vector.tensor_tensor(xT_low[:, :, b, t * P:(t + 1) * P],
                                            ps[:, t, :].rearrange("p (k c) -> p k c", k=KC),
                                            xT_high[:, :, b, t * P:(t + 1) * P].bitcast(F32), ALU.subtract)\
                        .then_inc(x_split, 1)
            low_weights(0)
            items(dve, body)




def feed_forward1(nc, a, ident, eps, x_all, out):
    NZ = E1 + E1 * RK
    with ExitStack() as ctx:
        m = Place(nc, ctx, "f1_")
        w = m.sbuf("w", [P, KC, D])
        wz = m.sbuf("wz", [P, KC, NZ])
        wb = m.sbuf("wb", [E1 * RK, D])
        bias = m.sbuf("bias", [P, E1])
        xT = m.sbuf("xT", [P, 2, D])
        logit = m.sbuf("logit", [P, 2, E1])
        best = m.sbuf("best", [P, 2, 1])
        is_best = m.sbuf("is_best", [P, 2, E1])
        left = m.sbuf("left", [P, 2, E1 + 1])
        chosen = m.sbuf("chosen", [P, 2, E1])
        z = m.sbuf("z", [P, 2, E1, RK])
        zT = m.sbuf("zT", [E1 * RK, 2, P])
        out_rows = m.sbuf("out_rows", [P, 2, D])
        first = Norm(Place(nc, ctx, "f1a_"))
        second = Norm(Place(nc, ctx, "f1b_"))
        ps_n = m.psum("ps_n", [P, 2, D])
        ps_y = m.psum("ps_y", [P, 2, D])
        ps_z = m.psum("ps_z", [P, 2, 512])
        ps_zT = m.psum("ps_zT", [P, 2, 512])
        w_in = m.sem("w_in")
        xn_turned = m.sems("xn_turned")
        xT_out = m.sems("xT_out")
        z_done = m.sems("z_done")
        picked = m.sem("picked")
        z_out = m.sems("z_out")
        z_turned = m.sems("z_turned")
        zT_out = m.sems("zT_out")
        y_done = m.sems("y_done")
        stored = m.sems("stored")
        PICKS = 4 + 2 * (E1 - 1)

        block = ctx.enter_context(nc.Block())
        x_view = x_all[:].rearrange("p b (t c) -> p b t c", t=TT)
        out_view = out.rearrange("(b t p) n -> b t p n", b=NB, t=TT)

        @block.sync
        def _(sp):
            start_ahead(sp, stored)
            sp.dma_start(w[:], a["w_upT"].rearrange("(k p) n -> p k n", p=P)).then_inc(w_in, 16)
            sp.dma_start(wz[:], a["wzT"].rearrange("(k p) n -> p k n", p=P)).then_inc(w_in, 16)
            sp.dma_start(wb[:], a["lora_BT"]).then_inc(w_in, 16)
            sp.dma_start(bias[:], a["bias"].partition_broadcast(P)).then_inc(w_in, 16)
            with sp.Fori(0, NB) as b:
                for t in range(TT):
                    s, k2 = t % 2, b * 2 + t // 2
                    sp.wait_ge(second.normed[s], after(k2 + 1))
                    sp.dma_start(out_view[b, t], out_rows[:, s, :]).then_inc(stored[s], 16)
            for s in range(2):
                sp.wait_ge(stored[s], after(NB * 2, 16))

        @block.tensor
        def _(pe):
            start_ahead(pe, xn_turned, z_turned, y_done)
            pe.wait_ge(w_in, 64)

            def turn(b, t):
                transpose_rows(nc, pe, ident, first, t % 2, b * 2 + t // 2, ps_n, xn_turned, xT_out)

            def base(b, t):
                s, k2 = t % 2, b * 2 + t // 2
                pe.wait_ge(xT_out[s], after(k2 + 1))
                pe.wait_ge(z_out[s], after(k2))
                for k in range(KC):
                    last = nc.tensor.matmul(ps_z[:, s, 0:NZ], xT[:, s, k * P:(k + 1) * P], wz[:, k, :],
                                            start=(k == 0), stop=(k == KC - 1))
                last.then_inc(z_done[s], 1)
                pe.wait_ge(second.summed[s], after(k2))
                for k in range(KC):
                    nc.tensor.matmul(ps_y[:, s, :], xT[:, s, k * P:(k + 1) * P], w[:, k, :],
                                     start=(k == 0), stop=False)

            def expert(b, t):
                s, k2 = t % 2, b * 2 + t // 2
                pe.wait_ge(z_out[s], after(k2 + 1))
                pe.wait_ge(zT_out[s], after(k2))
                nc.tensor.transpose(ps_zT[0:E1 * RK, s, 0:P], z[:, s, :, :].rearrange("p e r -> p (e r)"), ident[:])\
                    .then_inc(z_turned[s], 1)
                pe.wait_ge(zT_out[s], after(k2 + 1))
                nc.tensor.matmul(ps_y[:, s, :], zT[:, s, :], wb[:], start=False, stop=True).then_inc(y_done[s], 1)

            def step(has):
                has(turn, 2)
                has(expert, 1)
                has(base, 2)

            tiles(pe, step, 2)

        @block.scalar
        def _(act):
            start_ahead(act, xT_out, zT_out)

            def root_first(b, t):
                first.on_act(nc, act, t % 2, b * 2 + t // 2, eps)

            def root_second(b, t):
                second.on_act(nc, act, t % 2, b * 2 + t // 2, eps)

            def rows_out(b, t):
                s, k2 = t % 2, b * 2 + t // 2
                act.wait_ge(xn_turned[s], after(k2 + 1))
                act.wait_ge(y_done[s], after(k2))
                nc.scalar.activation(xT[:, s, :], ps_n[:, s, :], ACT.Copy).then_inc(xT_out[s], 1)

            def coordinates_out(b, t):
                s, k2 = t % 2, b * 2 + t // 2
                act.wait_ge(z_turned[s], after(k2 + 1))
                nc.scalar.activation(zT[:, s, :], ps_zT[0:E1 * RK, s, 0:P], ACT.Copy).then_inc(zT_out[s], 1)

            def step(has):
                has(root_second, 0)
                has(root_first, 2)
                has(rows_out, 2)
                has(coordinates_out, 1)

            tiles(act, step, 2)

        @block.vector
        def _(dve):
            start_ahead(dve, first.summed, first.normed, second.summed, second.normed, z_out)

            def head(b, t):
                s, k2 = t % 2, b * 2 + t // 2
                nc.vector.tensor_copy(first.res[:, s, :], x_view[:, b, t, :]).then_inc(first.summed[s], 1)
                dve.wait_ge(xn_turned[s], after(k2))
                dve.wait_ge(second.summed[s], after(k2))
                first.on_dve(nc, dve, s, k2)

            def choose(b, t):
                s, k2 = t % 2, b * 2 + t // 2
                done = [0]

                def step(ins):
                    done[0] += 1
                    ins.then_inc(picked, 1)
                    dve.wait_ge(picked, (b * TT + t) * PICKS + done[0])

                dve.wait_ge(z_done[s], k2 + 1)
                step(nc.vector.tensor_tensor(logit[:, s, :], ps_z[:, s, 0:E1], bias[:], ALU.add))
                step(nc.vector.tensor_reduce(best[:, s, :], logit[:, s, :], AX.X, ALU.max))
                step(nc.vector.tensor_scalar(is_best[:, s, :], logit[:, s, :], best[:, s, :], None, ALU.is_ge))
                step(nc.vector.tensor_copy(chosen[:, s, 0:1], is_best[:, s, 0:1]))
                for e in range(1, E1):
                    step(nc.vector.tensor_reduce(left[:, s, e:e + 1], chosen[:, s, 0:e], AX.X, ALU.add))
                    step(nc.vector.tensor_tensor(chosen[:, s, e:e + 1], is_best[:, s, e:e + 1], left[:, s, e:e + 1],
                                                 ALU.is_gt))
                dve.wait_ge(z_turned[s], after(k2))
                nc.vector.tensor_tensor(z[:, s, :, :], ps_z[:, s, E1:NZ].rearrange("p (e r) -> p e r", r=RK),
                                        bcast(chosen[:, s, :], 2, RK), ALU.mult).then_inc(z_out[s], 1)

            def tail(b, t):
                s, k2 = t % 2, b * 2 + t // 2
                dve.wait_ge(y_done[s], after(k2 + 1))
                nc.vector.tensor_tensor(second.res[:, s, :], ps_y[:, s, :], first.xn[:, s, :], ALU.add)\
                    .then_inc(second.summed[s], 1)
                dve.wait_ge(stored[s], after(k2, 16))
                second.on_dve(nc, dve, s, k2, out_rows[:, s, :])

            def step(has):
                has(tail, 0)
                has(head, 2)
                has(choose, 1)

            tiles(dve, step, 2)


def load_constants(nc, a, ident, ident16, eps):
    with ExitStack() as ctx:
        m = Place(nc, ctx, "c_")
        ident_in = m.sem("ident_in")
        eps_set = m.sem("eps_set")
        block = ctx.enter_context(nc.Block())

        @block.sync
        def _(sp):
            sp.dma_start(ident[:], a["ident"]).then_inc(ident_in, 16)

        @block.vector
        def _(dve):
            nc.vector.memset(eps[:], EPS).then_inc(eps_set, 1)
            dve.wait_ge(ident_in, 16)
            nc.vector.tensor_copy(ident16[:], ident[:]).then_inc(eps_set, 1)
            dve.wait_ge(eps_set, 2)


def program(nc, a, out, debug=None):
    qT_dram = nc.dram_tensor("qT_scratch", [NB * H0 // 2 * P, S], F32).ap()
    kT_dram = nc.dram_tensor("kT_scratch", [NB * G0 * P, S], F32).ap()
    with ExitStack() as ctx:
        m = Place(nc, ctx, "")
        ident = m.sbuf("ident_sb", [P, P])
        ident16 = m.sbuf("ident16_sb", [P, P], BF16)
        eps = m.sbuf("eps_sb", [P, 1])
        x_all = m.sbuf("x_all", [P, NB, TT * D])
        load_constants(nc, a, ident, ident16, eps)
        with ExitStack() as att:
            v_all = Place(nc, att, "").sbuf("v_all", [P, NB, G0, TT, HD0])
            project_layer0(nc, a, ident, v_all, qT_dram, kT_dram)
            v_pairs = v_all[:].rearrange("p b g t d -> p (b g) t d")
            o_pairs = x_all[:].rearrange("p b (g t c) -> p (b g) t c", g=G0, t=TT)
            attend_layer0(nc, a, ident, ident16, v_pairs, qT_dram, kT_dram, o_pairs)
        with ExitStack() as ffn:
            mf = Place(nc, ffn, "")
            xT_all = mf.sbuf("xT_all", [P, KC, NB, S])
            w_gu = mf.sbuf("w_gu", [P, KC, 2 * INTER])
            w_dn = mf.sbuf("w_dn", [P, FT, D])
            dequantise(nc, a, w_gu, w_dn, xT_all[:].rearrange("p k b n -> p (k b n)"))
            project_out0(nc, a, ident, eps, x_all, xT_all)
            if debug is not None:
                dump(nc, x_all, debug, 0)
            feed_forward0(nc, eps, x_all, xT_all, w_gu, w_dn)
        if debug is not None:
            dump(nc, x_all, debug, 1)
        attend_layer1(nc, a, ident, ident16, x_all)
        if debug is not None:
            dump(nc, x_all, debug, 2)
        feed_forward1(nc, a, ident, eps, x_all, out)


def dump(nc, x_all, debug, n):
    with ExitStack() as ctx:
        m = Place(nc, ctx, f"d{n}_")
        dumped = m.sem("dumped")
        block = ctx.enter_context(nc.Block())

        @block.sync
        def _(sp):
            dst = debug.rearrange("n (b t p) c -> n b p t c", b=NB, p=P)
            for b in range(NB):
                sp.dma_start(dst[n, b], x_all[:, b, :].rearrange("p (t c) -> p t c", t=TT)).then_inc(dumped, 16)
            sp.wait_ge(dumped, 16 * NB)


def constants():
    import numpy as np

    inv_freq = (1.0 / np.float32(10000.0) ** (np.arange(0, HD0, 2, dtype=np.float32) / np.float32(HD0)))
    freqs = np.outer(np.arange(S, dtype=np.float32), inv_freq.astype(np.float32)).astype(np.float32)
    emb = np.concatenate([freqs, freqs], axis=-1)
    cos, sin = np.cos(emb).astype(np.float32), np.sin(emb).astype(np.float32)
    sin[:, :HD0 // 2] *= -1
    scale = np.float32(HD0 ** -0.5)
    rope = np.stack([cos * scale, sin * scale, cos, sin], axis=1)
    rope = rope.reshape(TT, P, 4, HD0).transpose(1, 0, 2, 3)
    q, c = np.arange(P)[:, None], np.arange(P)[None, :]
    causal = np.where(c > q, NEG, 0.0).astype(np.float32)
    seen = (c > q % WIN) & (c <= q % WIN + WIN)
    window = np.broadcast_to(np.where(seen, 0.0, NEG)[:, None, :], (P, NW, P)).copy()
    window[:, 0, :WIN] = NEG
    guess = np.zeros((P, TT, 2), np.float32)
    for row in range(P, S):
        low, high = -8.0, 8.0
        for _ in range(60):
            z = (low + high) / 2
            low, high = (z, high) if 0.5 * math.erfc(z / math.sqrt(2.0)) > TARGET / (row + 1) else (low, z)
        density = math.exp(-z * z / 2) / math.sqrt(2 * math.pi)
        guess[row % P, row // P] = z / 2, 0.5 / ((row + 1) * density)
    iota8 = np.broadcast_to(np.arange(TOP, dtype=np.float32), (P, R0, TOP)).copy()
    return {
        "guess": guess,
        "iota8": iota8,
        "rope": np.ascontiguousarray(rope),
        "causal": causal,
        "window": window.astype(np.float32),
        "ident": np.eye(P, dtype=np.float32),
        "shift": (4 * (np.arange(P, dtype=np.uint32) % PACK)).reshape(P, 1),
        "iota": np.arange(16, dtype=np.float32).reshape(16, 1),
    }


def layout(i):
    import numpy as np

    x = i["L0_attn_hidden_states"].reshape(NB * S, D)
    w1 = [i["L1_attn_wq"].reshape(G1, R1 * HD1, KC, P), i["L1_attn_wk"].reshape(G1, HD1, KC, P),
          i["L1_attn_wv"].reshape(G1, HD1, KC, P)]
    return {
        "x": x,
        "xT": x.T,
        "wqkvT": np.concatenate([i["L0_attn_Wq"], i["L0_attn_Wk"], i["L0_attn_Wv"]]).T,
        "wo0T": i["L0_attn_Wo"].T,
        "qw_gu": np.repeat(i["L0_ffn_qweight_gu"], PACK, axis=0),
        "qw_dn": np.repeat(i["L0_ffn_qweight_down"], PACK, axis=0),
        "qzeros_gu": i["L0_ffn_qzeros_gu"],
        "qzeros_dn": i["L0_ffn_qzeros_down"],
        "scales_gu": i["L0_ffn_scales_gu"],
        "scales_dn": i["L0_ffn_scales_down"],
        "g_idx_gu": i["L0_ffn_g_idx_gu"],
        "g_idx_dn": i["L0_ffn_g_idx_down"],
        "w1T": np.concatenate(w1, axis=1).transpose(0, 3, 2, 1),
        "wo1T": i["L1_attn_wo"].T.reshape(G1, R1, HD1, D).transpose(0, 2, 1, 3),
        "w_upT": i["L1_ffn_W_up"].T,
        "wzT": np.concatenate([i["L1_ffn_gate_w"], i["L1_ffn_lora_A"].reshape(E1 * RK, D)]).T,
        "lora_BT": i["L1_ffn_lora_B"].transpose(0, 2, 1).reshape(E1 * RK, D),
        "bias": i["L1_ffn_expert_bias"],
    }


def kernel(**inputs):
    import numpy as np
    import concourse.bacc as bacc
    from concourse.bass_utils import run_bass_kernel_spmd

    nc = bacc.Bacc("TRN2", target_bir_lowering=False, num_devices=1)
    arrays, aps = {}, {}
    host = layout({k: np.asarray(v) for k, v in inputs.items()})
    for name, v in {**host, **constants()}.items():
        v = np.ascontiguousarray(v)
        arrays[f"in_{name}"] = v
        aps[name] = nc.dram_tensor(f"in_{name}", v.shape, mybir.dt.from_np(v.dtype), kind="ExternalInput").ap()
    out = nc.dram_tensor("out", [NB * S, D], F32, kind="ExternalOutput").ap()
    debug = nc.dram_tensor("debug", [3, NB * S, D], F32, kind="ExternalOutput").ap() if DEBUG else None
    program(nc, aps, out, debug)
    r = run_bass_kernel_spmd(nc, [arrays], core_ids=[0])
    return r.results[0]["out"].reshape(NB, S, D)


DEBUG = False
```
